# Optimizing a Trainium2 kernel written in Bass

```python
import numpy as np
import jax
import jax.numpy as jnp

def _softmax(x, axis=-1):
    return jax.nn.softmax(x, axis=axis)

def _gelu(x):
    return jax.nn.gelu(x, approximate=True)

def _silu(x):
    return jax.nn.silu(x)

def _sigmoid(x):
    return jax.nn.sigmoid(x)

def _layernorm(x, axis=-1, eps=1e-05):
    m = jnp.mean(x, axis=axis, keepdims=True)
    v = jnp.var(x, axis=axis, keepdims=True)
    return (x - m) / jnp.sqrt(v + eps)

def _scatter_add(tgt, idx, src, axis=0):
    return tgt.at[idx].add(src)

def _segment_sum(src, seg, n):
    return jax.ops.segment_sum(src, seg, n)
kernel_name = 'mk_adj_ffn_d1_adj_r2_03d0fb'

def setup_inputs(seed: int=0):
    np.random.seed(seed)
    _w = jnp.asarray

    def _rec_inputs():
        import jax
        import jax.numpy as jnp
        _gk = jax.random.key(seed)
        x = -0.000929 + 1 * jax.random.normal(jax.random.fold_in(_gk, 1), (4096, 256), jnp.float32)
        _w = (1.0 + jnp.arange(4096, dtype=jnp.float32)) ** (-0.5)
        _w = _w / _w.mean()
        _pij = jnp.clip(0.00390625 * _w[:, None] * _w[None, :], 0.0, 1.0)
        _a = jax.random.uniform(jax.random.fold_in(_gk, 2), (4096, 4096)) < _pij
        adj = _a.astype(jnp.int32)
        return (x, adj)
    x, adj = _rec_inputs()

    def _L0_gnn_setup():
        import jax, jax.numpy as jnp
        import numpy as np
        B, IN_F, OUT_F, H = (1024, 256, 256, 8)
        D = OUT_F // H
        key = jax.random.key(seed)
        ks = jax.random.split(key, 4)
        x = jax.random.normal(ks[0], (B, IN_F), dtype=jnp.float32)
        W_w = jax.random.normal(ks[1], (OUT_F, IN_F), dtype=jnp.float32) * (1.0 / np.sqrt(IN_F))
        W_b = jnp.zeros((OUT_F,), dtype=jnp.float32)
        a = jax.random.normal(ks[2], (2 * D, 1), dtype=jnp.float32) * 0.1
        adj = jax.random.randint(ks[3], (B, B), 0, 2, dtype=jnp.int32)
        return {'x': x, 'adj': adj, 'W_w': W_w, 'W_b': W_b, 'a': a}
    _L0_gnn_all = _L0_gnn_setup()
    _L0_gnn_in = {k: v for k, v in _L0_gnn_all.items() if k in ('W_w', 'W_b', 'a')}
    del _L0_gnn_all

    def _L0_ffn_setup():
        import jax, jax.numpy as jnp
        import numpy as np
        S, B, D, F, E, K = (512, 2, 256, 1024, 8, 2)
        key = jax.random.key(seed)
        ks = jax.random.split(key, 12)
        s = lambda *sh: 1.0 / np.sqrt(sh[0])
        inp = {'x': jax.random.normal(ks[0], (S, B, D), dtype=jnp.float32), 'Wg': jax.random.normal(ks[1], (D, E), dtype=jnp.float32) * s(D), 'bg': jnp.zeros((E,), dtype=jnp.float32), 'W1': jax.random.normal(ks[2], (E, D, F), dtype=jnp.float32) * s(D), 'b1': jnp.zeros((E, F), dtype=jnp.float32), 'W2': jax.random.normal(ks[3], (E, F, D), dtype=jnp.float32) * s(F), 'b2': jnp.zeros((E, D), dtype=jnp.float32), 'Ws1': jax.random.normal(ks[4], (D, F), dtype=jnp.float32) * s(D), 'bs1': jnp.zeros((F,), dtype=jnp.float32), 'Ws2': jax.random.normal(ks[5], (F, D), dtype=jnp.float32) * s(F), 'bs2': jnp.zeros((D,), dtype=jnp.float32)}
        return inp
    _L0_ffn_all = _L0_ffn_setup()
    _L0_ffn_in = {k: v for k, v in _L0_ffn_all.items() if k in ('Wg', 'bg', 'W1', 'b1', 'W2', 'b2', 'Ws1', 'bs1', 'Ws2', 'bs2')}
    del _L0_ffn_all
    return {'x': x, 'adj': adj, 'L0_gnn_W_w': _L0_gnn_in['W_w'], 'L0_gnn_W_b': _L0_gnn_in['W_b'], 'L0_gnn_a': _L0_gnn_in['a'], 'L0_ffn_Wg': _L0_ffn_in['Wg'], 'L0_ffn_bg': _L0_ffn_in['bg'], 'L0_ffn_W1': _L0_ffn_in['W1'], 'L0_ffn_b1': _L0_ffn_in['b1'], 'L0_ffn_W2': _L0_ffn_in['W2'], 'L0_ffn_b2': _L0_ffn_in['b2'], 'L0_ffn_Ws1': _L0_ffn_in['Ws1'], 'L0_ffn_bs1': _L0_ffn_in['bs1'], 'L0_ffn_Ws2': _L0_ffn_in['Ws2'], 'L0_ffn_bs2': _L0_ffn_in['bs2']}

def reference(x, adj, L0_gnn_W_w, L0_gnn_W_b, L0_gnn_a, L0_ffn_Wg, L0_ffn_bg, L0_ffn_W1, L0_ffn_b1, L0_ffn_W2, L0_ffn_b2, L0_ffn_Ws1, L0_ffn_bs1, L0_ffn_Ws2, L0_ffn_bs2):
    import jax
    import jax.numpy as jnp

    def _L0_gnn_ref(x, adj, W_w, W_b, a):
        import jax, jax.numpy as jnp
        import numpy as np
        B, IN_F, OUT_F, H = (1024, 256, 256, 8)
        D = OUT_F // H
        Bn = x.shape[0]
        h = (x @ W_w.T + W_b).reshape(Bn, H, D)
        a_src, a_dst = (a[:D, 0], a[D:, 0])
        s_src = jnp.einsum('bhd,d->bh', h, a_src)
        s_dst = jnp.einsum('bhd,d->bh', h, a_dst)
        e = jax.nn.leaky_relu(s_src[:, None, :] + s_dst[None, :, :], negative_slope=0.2)
        e = jnp.where(adj[:, :, None] == 0, jnp.float32(-1000000000.0), e)
        attn = jax.nn.softmax(e, axis=1)
        h_prime = jnp.einsum('ijh,jhd->ihd', attn, h).reshape(Bn, H * D)
        return jax.nn.elu(h_prime)

    def _L0_ffn_ref(x, Wg, bg, W1, b1, W2, b2, Ws1, bs1, Ws2, bs2):
        import jax, jax.numpy as jnp
        import numpy as np
        S, B, D, F, E, K = (512, 2, 256, 1024, 8, 2)
        gate_logits = jnp.einsum('sbd,de->sbe', x, Wg) + bg
        weights, selected = jax.lax.top_k(gate_logits, K)
        weights = jax.nn.softmax(weights.astype(jnp.float32), axis=-1)
        onehot = jax.nn.one_hot(selected, E, dtype=weights.dtype)
        comb = jnp.einsum('sbk,sbke->sbe', weights, onehot)
        h = jax.nn.relu(jnp.einsum('sbd,edf->sbef', x, W1) + b1)
        y = jnp.einsum('sbef,efd->sbed', h, W2) + b2
        out = jnp.einsum('sbe,sbed->sbd', comb, y)
        hs = jax.nn.relu(jnp.einsum('sbd,df->sbf', x, Ws1) + bs1)
        shared = jnp.einsum('sbf,fd->sbd', hs, Ws2) + bs2
        out = out + 1.0 / K * shared
        return out
    x = x + _L0_gnn_ref(_layernorm(x, axis=-1), adj, L0_gnn_W_w, L0_gnn_W_b, L0_gnn_a)
    x = x + _L0_ffn_ref(_layernorm(x, axis=-1)[None], L0_ffn_Wg, L0_ffn_bg, L0_ffn_W1, L0_ffn_b1, L0_ffn_W2, L0_ffn_b2, L0_ffn_Ws1, L0_ffn_bs1, L0_ffn_Ws2, L0_ffn_bs2)[0]
    return x

_drawn_inputs = setup_inputs


def setup_inputs(seed=0):
    import zlib

    import numpy as np

    out = dict(_drawn_inputs(seed))
    spreads = {'L0_gnn_W_b': (0.0, 0.1),
     'L0_ffn_bg': (0.0, 0.1),
     'L0_ffn_b1': (0.0, 0.1),
     'L0_ffn_b2': (0.0, 0.1),
     'L0_ffn_bs1': (0.0, 0.308),
     'L0_ffn_bs2': (0.0, 0.1)}
    factors = {}
    for name, (base, spread) in spreads.items():
        noise = np.random.default_rng([zlib.crc32(name.encode()), seed]).standard_normal(out[name].shape)
        drawn = base * np.exp(spread * noise) if base else spread * noise
        out[name] = jnp.asarray(drawn.astype(out[name].dtype))
    for name, factor in factors.items():
        out[name] = (out[name] * factor).astype(out[name].dtype)
    return out
```

```python
from contextlib import ExitStack
import math

import concourse.bass as bass
from concourse import mybir

F32 = mybir.dt.float32
F16 = mybir.dt.float16
F8 = mybir.dt.float8e4
I32 = mybir.dt.int32
U32 = mybir.dt.uint32
ALU = mybir.AluOpType
ACT = mybir.ActivationFunctionType
AX = mybir.AxisListType.X
RMAX = bass.bass_isa.ReduceOp.max

P = 128
N = 4096
D = 256
H = 8
HD = D // H
DC = D // P
NT = N // P
BI = 1024
NB = N // BI
IT = BI // P
VC = HD + 1
VW = 4 * VC
GJ = 4
NG = NT // GJ
ACT_T = [2, 2, 2, 3, 2, 2, 2, 3]
DVE_T = [GJ - n for n in ACT_T]
RING = 4
STAGE = 2
VSCALE = 256.0
STEP = 2.0 ** 40
BANK = 512
E = 8
K = 2
F = 1024
FC = F // P
EW = 8 * F
UNITS = 4 * (E + 1)
SLOT = 256
SUB = SLOT // P
SH_SLOTS = N // SLOT
MOE_SLOTS = (K * N - E) // SLOT + E
SLOTS = SH_SLOTS + MOE_SLOTS
N_ROWS = SLOTS * SLOT
XS = 16.0
WS = 256.0


def rsqrt_refined(nc, done, y, t, v):
    done(nc.vector.reciprocal(y, y))
    done(nc.vector.tensor_tensor(t, y, y, ALU.mult))
    done(nc.vector.tensor_tensor(t, t, v, ALU.mult))
    done(nc.vector.tensor_scalar(t, t, -0.5, 1.5, ALU.mult, ALU.add))
    done(nc.vector.tensor_tensor(y, y, t, ALU.mult))


def gat(nc, ctx, x_sb, x, adj_t, w_t, w_n, b_w, a, w_all, s_dram, v_dram, d_dram, w16_dram, xs_dram):
    def sb(name, shape, dt=F32):
        return ctx.enter_context(nc.sbuf_tensor(name, shape, dt))

    def ps(name, shape):
        return ctx.enter_context(nc.psum_tensor(name, shape, F32))

    def sem(name):
        return ctx.enter_context(nc.semaphore(name))

    wext = sb("wext", [P, DC, D + 2 * H])
    wn_sb = sb("wn_sb", [P, DC, D])
    acol = sb("acol", [P, 2])
    ablk = sb("ablk", [P, DC, 2 * H])
    bcol = sb("bcol", [P, DC])
    bext = sb("bext", [1, D + 2 * H])
    ba_src = sb("ba_src", [H, 1])
    ones = sb("ones", [P, P])
    ident = sb("ident", [P, P])
    stats = sb("stats", [P, NT, 6])
    mv = sb("mv", [P, NT, 2])
    rstd = sb("rstd", [P, NT])
    var = sb("var", [P, NT])
    tmp = sb("tmp", [P, NT])
    xn = sb("xn", [P, 2, D])
    st_sb = sb("st_sb", [H, 2, 4 * P])
    hext = sb("hext", [P, NT, D + 2 * H])
    hmean = sb("hmean", [P, D])
    dmx = sb("dmx", [P, H])
    dmxa = sb("dmxa", [P, H])
    dcol = sb("dcol", [P, H, 2, NT])
    fw = sb("fw", [P, 2, NT, H])
    zi = sb("zi", [P, NT, H])
    ab = sb("ab", [P, 2, NT, H])
    lnc = sb("lnc", [P, 1])
    stage = sb("stage", [P, STAGE, 2, BI], I32)
    masks = sb("masks", [P, NT + RING * GJ, BI], F8)
    mask = masks[:, 0:NT, :]
    m_ring = masks[:, NT:NT + RING * GJ, :]
    flat = masks[:, :, :].rearrange("p a b -> p (a b)")
    VB = NT * 2 * VC * 4
    v32 = [flat[:, k * VB:(k + 1) * VB].bitcast(F32).rearrange("p (t s c) -> p t s c", s=2, c=VC) for k in range(2)]
    vbuild = [flat[:, (k + 2) * VB:(k + 3) * VB].bitcast(F16) for k in range(2)]
    vb_halves = [v.rearrange("p (t s l c) -> p t s l c", s=2, l=2, c=VC) for v in vbuild]
    stage_f = stage[:, 0:2, :, :].bitcast(F32).rearrange("p k a i -> p k (a i)").rearrange("p k (t d) -> p k t d", d=D)
    v_cur = sb("v_cur", [P, 2, NT, VW], F16)
    d_cur = sb("d_cur", [P, 2, 2, NT])
    s_cur = sb("s_cur", [P, 2, BI])
    xnt = s_cur[:, :, :].rearrange("p k (c n) -> p k c n", c=DC)
    comb = sb("comb", [P, 2, IT, 2, 2, VC])
    hp = hext[:, :, 0:D]
    pw = sb("pw", [P, 2, IT, VC])
    den = sb("den", [P, NT, H])
    flag = sb("flag", [P, IT])
    wf = sb("wf", [P, F])
    w16 = sb("w16", [P, 2, F], F16)
    zeros = w16[:, 0, 0:2 * D]
    fl = sb("fl", [P, IT, HD])

    acc = [[ps(f"acc{q}{k}", [P, BANK]) for k in range(3)] for q in range(2)]
    aux = [ps(f"aux{k}", [P, BANK]) for k in range(2)]

    names = """w_in a_in ident_ok stats_ok var_ok std_ok rstd_ok xn_ok xt_ps xt_ok h_ps h_ok sT_ps sT_ok st_out wa_ps wa_ok
        dmx_ok dmxa_ok fw_in fw_ok v32_ok vhi_ok vb_ok vb_out d_ok d_out hm_ps hm_ok dch pch ach setup_done
        conv_ok dve_t act_t m_ready pe_done comb_ok comb_free settled z_ok z_out wf_in wch w16_out hp_ok""".split()
    S = {n: sem(n) for n in names}
    x_in = [sem(f"x_in{k}") for k in range(4)]
    v_in = [sem(f"v_in{q}") for q in range(2)]
    adj_in = [sem(f"adj_in{k}") for k in range(STAGE)]

    adj_v = adj_t.rearrange("b (n k) p i -> b n p k i", k=2)

    def acc_tile(q, it, a0, a1):
        o = (it % 3) * VW
        return acc[q][it // 3][:, o + a0:o + a1]

    def settle(eng):
        eng.sem_inc(S["settled"], 1)

    def load_head(eng, q, b, h):
        eng.dma_start(v_cur[:, q, :, :].rearrange("p t c -> p (t c)"), v_dram[h]).then_inc(v_in[q], 16)
        eng.dma_start(d_cur[:, q, :, :].rearrange("p a t -> p (a t)"), d_dram[h]).then_inc(v_in[q], 16)
        eng.dma_start(s_cur[:, q, :], s_dram[h:h + 1, bass.ds(b * BI, BI)].broadcast_to([P, BI])).then_inc(v_in[q], 16)

    block = ctx.enter_context(nc.Block())

    @block.sync
    def _(sp):
        sp.dma_start(wext[:, :, 0:D], w_t.rearrange("(c p) n -> p c n", p=P)).then_inc(S["w_in"], 16)
        sp.dma_start(wn_sb[:, :, :], w_n.rearrange("(c p) n -> p c n", p=P)).then_inc(S["w_in"], 16)
        sp.dma_start(bcol[:, :], b_w.rearrange("(c p) -> p c", p=P)).then_inc(S["w_in"], 16)
        sp.dma_start(bext[:, 0:D], b_w.rearrange("(a n) -> a n", a=1)).then_inc(S["w_in"], 16)
        for q in range(4):
            sp.dma_start(acol[32 * q:32 * q + 32, :], a.rearrange("(s c) o -> c (s o)", s=2)).then_inc(S["a_in"], 16)
        for k in range(4):
            sp.dma_start(x_sb[:, k * 8:k * 8 + 8, :], x[k * 1024:(k + 1) * 1024, :].rearrange("(t p) d -> p t d", p=P)).then_inc(x_in[k], 16)
        for n in range(STAGE):
            sp.dma_start(stage[:, n, :, :], adj_v[0, n]).then_inc(adj_in[n], 16)
        for k in range(NT // 4):
            sp.wait_ge(S["sT_ok"], k + 1)
            sp.dma_start(s_dram[:, k * 4 * P:(k + 1) * 4 * P], st_sb[:, k % 2, :]).then_inc(S["st_out"], 16)
            sp.wait_ge(S["st_out"], 16 * (k + 1))
        sp.wait_ge(S["d_ok"], 1)
        sp.dma_start(d_dram.rearrange("h p c -> p h c"), dcol[:, :, :, :].rearrange("p h a t -> p h (a t)")).then_inc(S["d_out"], 16)
        sp.wait_ge(S["d_out"], 16)
        for h in range(H):
            sp.wait_ge(S["vb_ok"], h + 1)
            sp.dma_start(v_dram[h], vbuild[h % 2]).then_inc(S["vb_out"], 16)
            sp.wait_ge(S["vb_out"], 16 * (h + 1))
            if h < 2:
                load_head(sp, h, 0, h)

        def block_loads(b, last):
            for n in range(NG * 2 - (STAGE if last else 0)):
                sp.wait_ge(S["conv_ok"], b * (NG * 2) + n + 1)
                nn = n + STAGE
                src = adj_v[bass.ds(b + nn // 16, 1), nn % 16].rearrange("a p k i -> (a p) k i")
                sp.dma_start(stage[:, n % STAGE, :, :], src).then_inc(adj_in[n % STAGE], 16)
            for h in range(H - (2 if last else 0)):
                sp.wait_ge(S["pe_done"], (b * H + h) * NG + NG)
                load_head(sp, h % 2, b + (h + 2) // H, (h + 2) % H)

        with sp.Fori(0, NB - 1) as b:
            block_loads(b, False)
        block_loads(NB - 1, True)
        sp.wait_ge(S["w16_out"], 16 * UNITS)

    @block.gpsimd
    def _(pool):
        nc.gpsimd.memset(ident[:, :], 0.0).then_inc(S["pch"], 1)
        nc.gpsimd.memset(lnc[:, :], math.log(VSCALE)).then_inc(S["pch"], 1)
        nc.gpsimd.memset(ones[:, :], 1.0).then_inc(S["pch"], 1)
        pool.wait_ge(S["pch"], 3)
        nc.gpsimd.affine_select(out=ident[:, :], in_=ident[:, :], compare_op=ALU.not_equal, fill=1.0, base=0,
                                pattern=[[-1, P]], channel_multiplier=1).then_inc(S["ident_ok"], 1)
        nc.gpsimd.memset(zeros, 0.0).then_inc(S["z_ok"], 1)
        pool.wait_ge(S["z_ok"], 1)
        rows = (N_ROWS - N) // P
        pool.dma_start(xs_dram[N:N_ROWS, :].rearrange("(p r) c -> p r c", p=P),
                       zeros.rearrange("p (o c) -> p o c", o=1).broadcast_to([P, rows, 2 * D])).then_inc(S["z_out"], 16)
        pool.wait_ge(S["dmx_ok"], 1)
        nc.gpsimd.partition_all_reduce(dmxa[:, :], dmx[:, :], P, RMAX).then_inc(S["dmxa_ok"], 1)

        LINKS = 9

        def finish_head(b, h, q):
            g = b * H + h
            link = [0]

            def done(ins):
                link[0] += 1
                ins.then_inc(S["pch"], 1)
                pool.wait_ge(S["pch"], 3 + g * LINKS + link[0])

            pool.wait_ge(S["comb_ok"], g + 1)
            al = ab[:, 0, bass.ds(b * IT, IT), h:h + 1].broadcast_to([P, IT, VC])
            be = ab[:, 1, bass.ds(b * IT, IT), h:h + 1].broadcast_to([P, IT, VC])
            for s in range(2):
                done(nc.gpsimd.tensor_tensor(pw[:, s], comb[:, q, :, s, 0, :], comb[:, q, :, s, 1, :], ALU.add))
            done(nc.gpsimd.tensor_tensor(pw[:, 0], pw[:, 0], al, ALU.mult))
            done(nc.gpsimd.tensor_tensor(pw[:, 1], pw[:, 1], be, ALU.mult))
            done(nc.gpsimd.tensor_tensor(pw[:, 0], pw[:, 0], pw[:, 1], ALU.add))
            settle(pool)
            done(nc.gpsimd.tensor_scalar(flag[:, :], pw[:, 0, :, HD], 0.0, None, ALU.is_equal))
            done(nc.gpsimd.tensor_tensor(den[:, bass.ds(b * IT, IT), h], pw[:, 0, :, HD], flag[:, :], ALU.add))
            done(nc.gpsimd.tensor_tensor(fl[:, :, :], flag[:, :].rearrange("p (t o) -> p t o", o=1).broadcast_to([P, IT, HD]),
                                         hmean[:, h * HD:(h + 1) * HD].rearrange("p (o c) -> p o c", o=1).broadcast_to([P, IT, HD]), ALU.mult))
            done(nc.gpsimd.tensor_tensor(hp[:, bass.ds(b * IT, IT), h * HD:(h + 1) * HD], pw[:, 0, :, 0:HD], fl[:, :, :], ALU.add))
            pool.sem_inc(S["comb_free"], 1)

        pool.wait_ge(S["hm_ok"], 1)
        pool.wait_ge(S["setup_done"], 1)
        pool.wait_ge(S["z_out"], 16)

        def split_unit(u):
            if not isinstance(u, int) or u:
                pool.wait_ge(S["wch"], u * 3)
            pool.dma_start(wf[:, :], w_all[bass.ds(u, 1)].rearrange("o p c -> (o p) c")).then_inc(S["wf_in"], 16)
            pool.wait_ge(S["wf_in"], u * 16 + 16)
            settle(pool)
            nc.gpsimd.tensor_scalar(wf[:, :], wf[:, :], WS, None, ALU.mult).then_inc(S["wch"], 1)
            pool.wait_ge(S["wch"], u * 3 + 1)
            if not isinstance(u, int) or u:
                pool.wait_ge(S["w16_out"], u * 16)
            settle(pool)
            nc.gpsimd.tensor_copy(w16[:, 0, :], wf[:, :]).then_inc(S["wch"], 1)
            pool.wait_ge(S["wch"], u * 3 + 2)
            nc.gpsimd.tensor_tensor(w16[:, 1, :], wf[:, :], w16[:, 0, :], ALU.subtract).then_inc(S["wch"], 1)
            pool.wait_ge(S["wch"], u * 3 + 3)
            pool.dma_start(w16_dram[bass.ds(u, 1)].rearrange("o p l c -> (o p) (l c)"), w16[:, :, :].rearrange("p l c -> p (l c)")).then_inc(S["w16_out"], 16)

        pool.sem_inc(S["comb_free"], 1)
        split_unit(0)
        with pool.Fori(0, NB) as b:
            for h in range(H):
                finish_head(b, h, h % 2)
                split_unit(b * H + h + 1)
        for u in range(NB * H + 1, UNITS):
            split_unit(u)

    @block.tensor
    def _(pe):
        pe.wait_ge(S["w_in"], 64)
        pe.wait_ge(S["wa_ok"], 1)
        pe.wait_ge(S["ident_ok"], 1)
        wa = aux[0]
        for c in range(DC):
            for k in range(DC):
                nc.tensor.matmul(wa[:, c * 16:c * 16 + 16], wn_sb[:, k, c * P:(c + 1) * P], ablk[:, k, :], start=(c == 0 and k == 0), stop=(k == DC - 1), skip_group_check=True)
        for k in range(DC):
            nc.tensor.matmul(wa[0:1, 32:48], bcol[:, k:k + 1], ablk[:, k, :], start=False, stop=(k == DC - 1), skip_group_check=True)
        for k in range(DC):
            last = nc.tensor.matmul(wa[0:H, 48:49], ablk[:, k, 0:H], bcol[:, k:k + 1], start=False, stop=(k == DC - 1), skip_group_check=True)
        last.then_inc(S["wa_ps"], 1)
        pe.wait_ge(S["wa_ok"], 2)
        for t in range(NT):
            pe.wait_ge(S["xn_ok"], t + 1)
            if t >= 2:
                pe.wait_ge(S["xt_ok"], t - 1)
            for c in range(DC):
                last = nc.tensor.transpose(acc[0][t % 2][:, c * P:(c + 1) * P], xn[:, t % 2, c * P:(c + 1) * P], ident[:, :])
            last.then_inc(S["xt_ps"], 1)
            pe.wait_ge(S["xt_ok"], t + 1)
            if t >= 2:
                pe.wait_ge(S["h_ok"], t - 1)
            o = (t % 4) * P
            for c in range(DC):
                nc.tensor.matmul(acc[1][t % 2][:, 0:D + 2 * H], xnt[:, (t // 4) % 2, c, o:o + P], wext[:, c, :], start=(c == 0), stop=False)
            nc.tensor.matmul(acc[1][t % 2][:, 0:D + 2 * H], ones[0:1, :], bext[:, :], start=False, stop=True).then_inc(S["h_ps"], 1)
            if t % 4 == 3:
                k = t // 4
                if k >= 2:
                    pe.wait_ge(S["sT_ok"], k - 1)
                for c in range(DC):
                    last = nc.tensor.matmul(aux[k % 2][0:H, :], wext[:, c, D:D + H], xnt[:, k % 2, c, :], start=(c == 0), stop=(c == DC - 1))
                last.then_inc(S["sT_ps"], 1)
        pe.wait_ge(S["h_ok"], NT)
        for t in range(NT):
            last = nc.tensor.matmul(acc[0][2][:, 0:D], ones[:, :], hext[:, t, 0:D], start=(t == 0), stop=(t == NT - 1))
        last.then_inc(S["hm_ps"], 1)
        pe.wait_ge(S["hm_ok"], 1)

        def head(b, r, q):
            g = b * H + 2 * r + q
            pe.wait_ge(v_in[q], (b * (H // 2) + r) * 48 + 48)
            for n in range(NG):
                pe.wait_ge(S["m_ready"], g * NG + n + 1)
                if n == 0 and not (isinstance(g, int) and g < 2):
                    pe.wait_ge(S["comb_ok"], g - 1)
                settle(pe)
                for jj in range(GJ):
                    j = n * GJ + jj
                    slot = j % (RING * GJ)
                    for it in range(IT):
                        nc.tensor.matmul(acc_tile(q, it, 0, VW), m_ring[:, slot, it * P:(it + 1) * P], v_cur[:, q, j, :],
                                         start=(j == 0 and it % 3 == 0), stop=False, skip_group_check=True)
                        last = nc.tensor.matmul(acc_tile(q, it, 2 * VC, VW), mask[:, j, it * P:(it + 1) * P], v_cur[:, q, j, 2 * VC:VW],
                                                start=False, stop=(j == NT - 1), skip_group_check=True)
                last.then_inc(S["pe_done"], 1)

        head(0, 0, 0)
        head(0, 0, 1)
        with pe.Fori(1, NB * H // 2) as r:
            head(0, r, 0)
            head(0, r, 1)

    @block.scalar
    def _(act):
        for t in range(NT):
            if t % 8 == 0:
                act.wait_ge(S["var_ok"], t // 8 + 1)
                nc.scalar.activation(rstd[:, t:t + 8], var[:, t:t + 8], ACT.Sqrt).then_inc(S["std_ok"], 1)
            act.wait_ge(S["xt_ps"], t + 1)
            if t >= 8 and t % 4 == 0:
                act.wait_ge(S["sT_ps"], t // 4 - 1)
            nc.scalar.activation(xnt[:, (t // 4) % 2, :, (t % 4) * P:(t % 4 + 1) * P],
                                 acc[0][t % 2][:, 0:D].rearrange("p (c n) -> p c n", c=DC), ACT.Copy).then_inc(S["xt_ok"], 1)
            act.wait_ge(S["h_ps"], t + 1)
            nc.scalar.activation(hext[:, t, :], acc[1][t % 2][:, 0:D + 2 * H], ACT.Copy).then_inc(S["h_ok"], 1)
            if t % 4 == 3:
                k = t // 4
                act.wait_ge(S["sT_ps"], k + 1)
                if k >= 2:
                    act.wait_ge(S["st_out"], 16 * (k - 1))
                nc.scalar.activation(st_sb[:, k % 2, :], aux[k % 2][0:H, :], ACT.Identity, bias=ba_src[:, :]).then_inc(S["sT_ok"], 1)
        act.wait_ge(S["fw_in"], 1)
        nc.scalar.activation(fw[:, 0], fw[:, 0], ACT.Exp, bias=lnc[:, :]).then_inc(S["fw_ok"], 1)
        nc.scalar.activation(fw[:, 1], fw[:, 1], ACT.Exp, bias=lnc[:, :]).then_inc(S["fw_ok"], 1)
        nc.scalar.activation(ab[:, :, :, :], ab[:, :, :, :], ACT.Exp).then_inc(S["fw_ok"], 1)
        act.wait_ge(S["hm_ps"], 1)
        nc.scalar.activation(hmean[:, :], acc[0][2][:, 0:D], ACT.Copy, scale=1.0 / N).then_inc(S["hm_ok"], 1)
        for h in range(H):
            act.wait_ge(S["v32_ok"], h + 1)
            if h >= 2:
                act.wait_ge(S["vb_out"], 16 * (h - 1))
            nc.scalar.activation(vb_halves[h % 2][:, :, :, 0, :], v32[h % 2], ACT.Copy).then_inc(S["vhi_ok"], 1)

        act.wait_ge(S["vb_out"], 16 * H)

        def head(b, r, q):
            g = b * H + 2 * r + q
            act.wait_ge(v_in[q], (b * (H // 2) + r) * 48 + 48)
            for n in range(NG):
                if isinstance(g, int) and g == 0:
                    if n >= RING:
                        act.wait_ge(S["pe_done"], n - RING + 1)
                else:
                    act.wait_ge(S["pe_done"], g * NG + n - RING + 1)
                settle(act)
                for jj in range(ACT_T[n]):
                    j = n * GJ + jj
                    nc.scalar.activation(m_ring[:, j % (RING * GJ), :], s_cur[:, q, :], ACT.Sigmoid,
                                         bias=d_cur[:, q, 1, j:j + 1], scale=STEP, saturate=False).then_inc(S["act_t"], 1)

        head(0, 0, 0)
        head(0, 0, 1)
        with act.Fori(1, NB * H // 2) as r:
            head(0, r, 0)
            head(0, r, 1)

        for k in range(4):
            act.wait_ge(S["xn_ok"], NT + k + 1)
            nc.scalar.activation(stage_f[:, k % 2], stage_f[:, k % 2], ACT.Exp).then_inc(S["ach"], 1)

    @block.vector
    def _(dve):
        nd = [0]

        def done(ins):
            nd[0] += 1
            ins.then_inc(S["dch"], 1)
            dve.wait_ge(S["dch"], nd[0])

        done(nc.vector.memset(ablk[:, :, :], 0.0))
        dve.wait_ge(S["a_in"], 64)
        for q in range(4):
            for c in range(DC):
                for s in range(2):
                    k = s * H + c * 4 + q
                    last = nc.vector.tensor_copy(ablk[32 * q:32 * q + 32, c, k:k + 1], acol[32 * q:32 * q + 32, s:s + 1])
        done(last)
        dve.sem_inc(S["wa_ok"], 1)
        dve.wait_ge(S["wa_ps"], 1)
        nc.vector.tensor_copy(wext[:, :, D:D + 16], aux[0][:, 0:32].rearrange("p (c k) -> p c k", c=DC))
        nc.vector.tensor_copy(bext[:, D:D + 16], aux[0][0:1, 32:48])
        nc.vector.tensor_copy(ba_src[:, :], aux[0][0:H, 48:49]).then_inc(S["wa_ok"], 1)
        for k in range(4):
            dve.wait_ge(x_in[k], 16)
            for t in range(k * 8, k * 8 + 8):
                nc.vector.bn_stats(stats[:, t, :], x_sb[:, t, :]).then_inc(S["stats_ok"], 1)
            dve.wait_ge(S["stats_ok"], k * 8 + 8)
            for t in range(k * 8, k * 8 + 8):
                last = nc.vector.bn_aggr(mv[:, t, :], stats[:, t, :])
            done(last)
            sl = slice(k * 8, k * 8 + 8)
            nc.vector.tensor_scalar(var[:, sl], mv[:, sl, 1], 1e-5, None, ALU.add).then_inc(S["var_ok"], 1)
            dve.wait_ge(S["std_ok"], k + 1)
            rsqrt_refined(nc, done, rstd[:, sl], tmp[:, sl], var[:, sl])
            for t in range(k * 8, k * 8 + 8):
                if t >= 2:
                    dve.wait_ge(S["xt_ps"], t - 1)
                nc.vector.tensor_scalar(xn[:, t % 2, :], x_sb[:, t, :], mv[:, t, 0:1], rstd[:, t:t + 1], ALU.subtract, ALU.mult).then_inc(S["xn_ok"], 1)
        dve.wait_ge(S["h_ok"], NT)
        dst = hext[:, :, D + H:D + 2 * H]
        nc.vector.tensor_reduce(dmx[:, :], dst.rearrange("p t h -> p h t"), AX, ALU.max).then_inc(S["dmx_ok"], 1)
        nc.vector.tensor_scalar(dcol[:, :, 0, :], dst.rearrange("p t h -> p h t"), -1.0, None, ALU.mult)
        nc.vector.tensor_scalar(dcol[:, :, 1, :], dst.rearrange("p t h -> p h t"), STEP, None, ALU.mult).then_inc(S["d_ok"], 1)
        dve.wait_ge(S["dmxa_ok"], 1)
        dmb = dmxa[:, :].rearrange("p (o h) -> p o h", o=1).broadcast_to([P, NT, H])
        done(nc.vector.tensor_tensor(fw[:, 0], dst, dmb, ALU.subtract))
        done(nc.vector.tensor_scalar(fw[:, 1], fw[:, 0], 0.2, None, ALU.mult))
        done(nc.vector.tensor_tensor(zi[:, :, :], hext[:, :, D:D + H], dmb, ALU.add))
        done(nc.vector.tensor_scalar(ab[:, 0], zi[:, :, :], 0.8, 0.0, ALU.mult, ALU.min))
        done(nc.vector.tensor_scalar(ab[:, 1], zi[:, :, :], -0.8, 0.0, ALU.mult, ALU.min))
        dve.sem_inc(S["fw_in"], 1)
        dve.wait_ge(S["fw_ok"], 3)
        done(nc.vector.tensor_scalar(fw[:, 1], fw[:, 1], -1.0, None, ALU.mult))
        def v_low(h):
            dve.wait_ge(S["vhi_ok"], h + 1)
            nc.vector.tensor_tensor(vb_halves[h % 2][:, :, :, 1, :], v32[h % 2], vb_halves[h % 2][:, :, :, 0, :], ALU.subtract).then_inc(S["vb_ok"], 1)

        for h in range(H):
            if h >= 2:
                dve.wait_ge(S["vb_ok"], h - 1)
            for s in range(2):
                f = fw[:, s, :, h:h + 1]
                nc.vector.tensor_tensor(v32[h % 2][:, :, s, 0:HD], hext[:, :, h * HD:(h + 1) * HD], f.broadcast_to([P, NT, HD]), ALU.mult)
                last = nc.vector.tensor_copy(v32[h % 2][:, :, s, HD:VC], f)
            last.then_inc(S["v32_ok"], 1)
            if h:
                v_low(h - 1)
        v_low(H - 1)
        dve.wait_ge(S["vb_out"], 16 * H)
        dve.sem_inc(S["setup_done"], 1)

        ms = m_ring[:, :, :].bitcast(U32)
        mk = mask[:, :, :].bitcast(U32)

        def evacuate(g, q):
            dve.wait_ge(S["pe_done"], g * NG + NG)
            if not (isinstance(g, int) and g == 0):
                dve.wait_ge(S["comb_free"], g)
            for k in range(3):
                t0, t1 = 3 * k, min(3 * k + 3, IT)
                last = nc.vector.tensor_copy(comb[:, q, t0:t1, :, :, :].rearrange("p t s l c -> p (t s l c)"), acc[q][k][:, 0:(t1 - t0) * VW])
            last.then_inc(S["comb_ok"], 1)

        def head(b, r, q, first, before):
            g = b * H + 2 * r + q
            dve.wait_ge(v_in[q], (b * (H // 2) + r) * 48 + 48)
            for n in range(NG):
                if isinstance(g, int) and g == 0:
                    if n >= RING:
                        dve.wait_ge(S["pe_done"], n - RING + 1)
                else:
                    dve.wait_ge(S["pe_done"], g * NG + n - RING + 1)
                settle(dve)
                if first:
                    if not isinstance(g, int):
                        dve.wait_ge(S["pe_done"], g * NG - NG + n + 1)
                    for k in range(2 * n, 2 * n + 2):
                        dve.wait_ge(adj_in[k % STAGE], b * (16 // STAGE * 16) + (k // STAGE) * 16 + 16)
                        settle(dve)
                        nc.vector.tensor_scalar(mask[:, 2 * k:2 * k + 2, :], stage[:, k % STAGE, :, :], 0, -1.0, ALU.not_equal, ALU.mult, saturate=False).then_inc(S["conv_ok"], 1)
                for jj in range(ACT_T[n], GJ):
                    j = n * GJ + jj
                    nc.vector.tensor_scalar(m_ring[:, j % (RING * GJ), :], s_cur[:, q, :], d_cur[:, q, 0, j:j + 1], None, ALU.is_gt, saturate=False).then_inc(S["dve_t"], 1)
                dve.wait_ge(S["dve_t"], g * sum(DVE_T) + sum(DVE_T[:n + 1]))
                dve.wait_ge(S["act_t"], g * sum(ACT_T) + sum(ACT_T[:n + 1]))
                if first:
                    dve.wait_ge(S["conv_ok"], b * 16 + 2 * n + 2)
                j0 = (n * GJ) % (RING * GJ)
                nc.vector.tensor_tensor(ms[:, j0:j0 + GJ, :], ms[:, j0:j0 + GJ, :], mk[:, n * GJ:(n + 1) * GJ, :], ALU.bitwise_and).then_inc(S["m_ready"], 1)
                if n == 1 and before:
                    before()

        def blk(b):
            head(b, 0, 0, True, None)
            head(b, 0, 1, False, lambda: evacuate(b * H, 0))
            with dve.Fori(1, H // 2) as r:
                head(b, r, 0, False, lambda: evacuate(b * H + 2 * r - 1, 1))
                head(b, r, 1, False, lambda: evacuate(b * H + 2 * r, 0))
            evacuate(b * H + H - 1, 1)

        blk(0)
        with dve.Fori(1, NB) as b:
            blk(b)

        dve.wait_ge(S["comb_free"], NB * H + 1)
        done(nc.vector.reciprocal(den[:, :, :], den[:, :, :]))
        for k in range(4):
            sl = slice(8 * k, 8 * k + 8)
            for h in range(H):
                last = nc.vector.tensor_tensor(hp[:, sl, h * HD:(h + 1) * HD], hp[:, sl, h * HD:(h + 1) * HD], den[:, sl, h:h + 1].broadcast_to([P, 8, HD]), ALU.mult)
        done(last)
        c0 = nd[0]
        for k in range(4):
            sl = slice(8 * k, 8 * k + 8)
            if k >= 2:
                dve.wait_ge(S["hp_ok"], 8 * (k - 1))
            nc.vector.tensor_scalar(stage_f[:, k % 2], hp[:, sl, :], 0.0, None, ALU.min).then_inc(S["xn_ok"], 1)
            nc.vector.scalar_tensor_tensor(out=x_sb[:, sl, :], in0=hp[:, sl, :], scalar=0.0, in1=x_sb[:, sl, :], op0=ALU.max, op1=ALU.add).then_inc(S["dch"], 1)
            c0 += 1
            dve.wait_ge(S["ach"], k + 1)
            dve.wait_ge(S["dch"], c0)
            nc.vector.scalar_tensor_tensor(out=x_sb[:, sl, :], in0=stage_f[:, k % 2], scalar=-1.0, in1=x_sb[:, sl, :], op0=ALU.add, op1=ALU.add).then_inc(S["hp_ok"], 8)


def ffn(nc, ctx, x_sb, w_route, b_route, b1_all, b2_all, w16_dram, xs_dram, ys_dram, out_dram):
    def sb(name, shape, dt=F32):
        return ctx.enter_context(nc.sbuf_tensor(name, shape, dt))

    def ps(name, shape, dt=F32):
        return ctx.enter_context(nc.psum_tensor(name, shape, dt))

    def sem(name):
        return ctx.enter_context(nc.semaphore(name))

    w_sb = sb("w_sb", [P, E + 1, EW], F16)
    w_flat = w_sb[:, :, :].rearrange("p e c -> p (e c)")
    b1_sb = sb("b1_sb", [P, (E + 1) * FC])
    b2_sb = sb("b2_sb", [P, E + 1, D])
    hf = sb("hf", [P, FC // 2, SLOT])
    hh = sb("hh", [P, 2, FC, SLOT], F16)
    xs = sb("xs", [P, SUB, 2, D], F16)
    xt = sb("xt", [P, 2, DC, SLOT], F16)
    y_sb = sb("y_sb", [P, SUB, D])
    pos_i = sb("pos_i", [P, 2, NT], I32)
    wts = sb("wts", [P, 2, NT])
    emap = sb("emap", [P, MOE_SLOTS], I32)

    xhl = w_sb[:, 6:8, :].rearrange("p e c -> p (e c)").rearrange("p (t l d) -> p t l d", l=2, d=D)
    used = [0]

    def temp(n, dt=F32):
        a = used[0]
        used[0] += 2 * n
        assert used[0] <= EW
        return w_sb[:, 5, a:a + 2 * n].bitcast(dt)

    def te(v):
        return v.rearrange("p (t e) -> p t e", e=E)

    logit, one0, one1, both, scan0, scan1 = [te(temp(NT * E)) for _ in range(6)]
    scr = temp(MOE_SLOTS * E)
    top, mark, gap = temp(NT), temp(NT), temp(NT)
    stats, mv = temp(NT * 6), temp(NT * 2)
    stats, mv = stats.rearrange("p (t k) -> p t k", k=6), mv.rearrange("p (t k) -> p t k", k=2)
    rstd, var, tmp = temp(NT), temp(NT), temp(NT)
    iota_i = temp(MOE_SLOTS, I32)
    iota_f, k256, desc, cnt, ends, ends2 = temp(MOE_SLOTS), temp(16), temp(E), temp(E), temp(E), temp(E)
    bg_sb, wgf = temp(E), temp(DC * E)
    posf = temp(NT)
    xnf = [y_sb[:, k, :] for k in range(2)]
    wg = temp(DC * E)[:, :].bitcast(F16).rearrange("p (l c e) -> p l c e", l=2, e=E)
    ident16 = sb("ident16", [P, P], F16)
    tri = hf[:, 0, 0:P]
    ones = hf[:, 1, 0:P]

    ps_t = [ps(f"ps_t{k}", [P, 1024], F16) for k in range(2)]
    ps_h = [ps(f"ps_h{k}", [P, BANK]) for k in range(4)]
    ps_y = ps("ps_y", [P, BANK])
    ps_g = ps("ps_g", [P, BANK])

    names = """cst_in w_in w_late z_cst cst vch2 f_stats f_var f_std xn_ok2 xhi_ok xlo_ok tr_ps tr_ok g_ps g_ok gap_ok ex_ok
        both_ok rank_ps pos_ok xs_out sc_done xs_in t_done xt_ok2 h_ps2 relu_ok hi_ok conv y_ps y_ok y_out
        fin_ok settled2""".split()
    S = {n: sem(n) for n in names}
    fin_out = [sem(f"fin_out{k}") for k in range(4)]
    g_in = [sem(f"g_in{k}") for k in range(4)]
    s_in = [sem(f"s_in{k}") for k in range(4)]

    def settle(eng):
        eng.sem_inc(S["settled2"], 1)

    def w_at(e, o, n):
        return w_flat[:, bass.ds(e * EW + o, n)] if not isinstance(e, int) else w_sb[:, e, o:o + n]

    def w1_at(e, c, l, f):
        return w_at(e, c * 2048 + l * 1024 + f * P, P)

    def w2_at(e, f, l):
        return w_at(e, (2 + f // 4) * 2048 + l * 1024 + (f % 4) * D, D)

    gbuf = w_sb[:, 0, :].bitcast(F32).rearrange("p (k s d) -> p k s d", k=4, d=D)

    block = ctx.enter_context(nc.Block())

    @block.sync
    def _(sp):
        sp.dma_start(wgf, w_route.rearrange("(c p) e -> p c e", p=P)).then_inc(S["cst_in"], 16)
        sp.dma_start(bg_sb, b_route.rearrange("(a e) -> a e", a=1).broadcast_to([P, E])).then_inc(S["cst_in"], 16)
        sp.dma_start(b1_sb[:, :], b1_all.rearrange("(g p) -> p g", p=P)).then_inc(S["cst_in"], 16)
        sp.dma_start(b2_sb[:, :, :], b2_all.rearrange("(a e) d -> a e d", a=1).broadcast_to([P, E + 1, D])).then_inc(S["cst_in"], 16)
        for e in [E] + list(range(5)):
            sp.dma_start(w_sb[:, e, :].rearrange("p (u c) -> p u c", u=4), w16_dram[4 * e:4 * e + 4].rearrange("u p l c -> p u (l c)")).then_inc(S["w_in"], 16)
        for k in range(4):
            sp.wait_ge(S["xlo_ok"], 8 * k + 8)
            sp.dma_start(xs_dram[k * 1024:(k + 1) * 1024, :].rearrange("(t p) c -> p t c", p=P), xhl[:, 8 * k:8 * k + 8, :, :].rearrange("p t l d -> p t (l d)")).then_inc(S["xs_out"], 16)
        sp.wait_ge(S["xs_out"], 64)

        def load_slot(s):
            src = xs_dram[bass.ds(s * SLOT, SLOT), :].rearrange("(u p) c -> p u c", p=P)
            sp.dma_start(xs[:, :, :, :].rearrange("p u l d -> p u (l d)"), src).then_inc(S["xs_in"], 16)

        def store_slot(s):
            sp.wait_ge(S["y_ok"], s + 1)
            sp.dma_start(ys_dram[bass.ds(s * SLOT, SLOT), :].rearrange("(u p) d -> p u d", p=P), y_sb[:, :, :]).then_inc(S["y_out"], 16)

        load_slot(0)
        with sp.Fori(0, SH_SLOTS - 1) as s:
            sp.wait_ge(S["t_done"], s + 1)
            load_slot(s + 1)
            store_slot(s)
        sp.wait_ge(S["sc_done"], 16 * 2 * NT)
        for e in range(5, E):
            sp.dma_start(w_sb[:, e, :].rearrange("p (u c) -> p u c", u=4), w16_dram[4 * e:4 * e + 4].rearrange("u p l c -> p u (l c)")).then_inc(S["w_late"], 16)
        with sp.Fori(SH_SLOTS - 1, SLOTS - 1) as s:
            sp.wait_ge(S["t_done"], s + 1)
            load_slot(s + 1)
            store_slot(s)
        store_slot(SLOTS - 1)
        sp.wait_ge(S["y_out"], 16 * SLOTS)
        for t in range(NT):
            if t >= 4:
                sp.wait_ge(fin_out[t % 4], 16 * (t // 4))
            sp.dma_start(gbuf[:, t % 4, 2, :], ys_dram[t * P:(t + 1) * P, :]).then_inc(s_in[t % 4], 16)
            if t >= 2:
                sp.wait_ge(S["fin_ok"], t - 1)
                sp.dma_start(out_dram[(t - 2) * P:(t - 1) * P, :], gbuf[:, (t - 2) % 4, 3, :]).then_inc(fin_out[(t - 2) % 4], 16)
        for t in range(NT - 2, NT):
            sp.wait_ge(S["fin_ok"], t + 1)
            sp.dma_start(out_dram[t * P:(t + 1) * P, :], gbuf[:, t % 4, 3, :]).then_inc(fin_out[t % 4], 16)
        for k in range(4):
            sp.wait_ge(fin_out[k], 16 * NT // 4)
        sp.wait_ge(S["y_out"], 16 * SLOTS)

    @block.gpsimd
    def _(pool):
        nc.gpsimd.memset(tri, 1.0).then_inc(S["z_cst"], 1)
        nc.gpsimd.memset(ones, 1.0).then_inc(S["z_cst"], 1)
        nc.gpsimd.memset(ident16[:, :], 0.0).then_inc(S["z_cst"], 1)
        pool.wait_ge(S["z_cst"], 3)
        nc.gpsimd.affine_select(out=tri, in_=tri, compare_op=ALU.is_gt, fill=0.0, base=0, pattern=[[1, P]], channel_multiplier=-1).then_inc(S["cst"], 1)
        nc.gpsimd.affine_select(out=ident16[:, :], in_=ident16[:, :], compare_op=ALU.not_equal, fill=1.0, base=0, pattern=[[-1, P]], channel_multiplier=1).then_inc(S["cst"], 1)
        nc.gpsimd.iota(iota_i, pattern=[[1, MOE_SLOTS]], base=0, channel_multiplier=0).then_inc(S["cst"], 1)
        pool.wait_ge(S["pos_ok"], 1)
        for t in range(NT):
            for k in range(2):
                nc.gpsimd.indirect_dma_start(out=xs_dram, out_offset=bass.IndirectOffsetOnAxis(ap=pos_i[:, k, t:t + 1], axis=0),
                                             in_=xhl[:, t, :, :].rearrange("p l d -> p (l d)"), in_offset=None).then_inc(S["sc_done"], 16)
        pool.wait_ge(S["y_out"], 16 * SLOTS)
        for t in range(NT):
            if t >= 4:
                pool.wait_ge(S["fin_ok"], t - 3)
            for k in range(2):
                nc.gpsimd.indirect_dma_start(out=gbuf[:, t % 4, k, :], out_offset=None, in_=ys_dram,
                                             in_offset=bass.IndirectOffsetOnAxis(ap=pos_i[:, k, t:t + 1], axis=0)).then_inc(g_in[t % 4], 16)

    @block.tensor
    def _(pe):
        pe.wait_ge(S["cst"], 3)
        pe.wait_ge(S["vch2"], 3)
        for t in range(NT):
            pe.wait_ge(S["xlo_ok"], t + 1)
            if t >= 2:
                pe.wait_ge(S["tr_ok"], t - 1)
            for l in range(2):
                for c in range(DC):
                    last = nc.tensor.transpose(ps_t[t % 2][:, (l * DC + c) * P:(l * DC + c + 1) * P], xhl[:, t, l, c * P:(c + 1) * P], ident16[:, :])
            last.then_inc(S["tr_ps"], 1)
            pe.wait_ge(S["tr_ok"], t + 1)
            xtt = xt[:, t % 2, :, :].rearrange("p c n -> p (c n)").rearrange("p (l c n) -> p l c n", l=2, c=DC)
            n = 0
            for lx, lw in ((0, 0), (1, 0), (0, 1)):
                for c in range(DC):
                    last = nc.tensor.matmul(ps_g[:, t * E:(t + 1) * E], xtt[:, lx, c, :], wg[:, lw, c, :], start=(t == 0 and n == 0), stop=(n == 5), skip_group_check=True)
                    n += 1
        last.then_inc(S["g_ps"], 1)
        pe.wait_ge(S["both_ok"], 1)
        a = both.rearrange("p t e -> p (t e)")
        nc.tensor.matmul(ps_g[:, 0:NT * E], tri, a, start=True, stop=True)
        nc.tensor.matmul(ps_g[:, NT * E:2 * NT * E], ones, a, start=False, stop=True, skip_group_check=True).then_inc(S["rank_ps"], 1)

        def transposes(s):
            pe.wait_ge(S["xs_in"], s * 16 + 16)
            for l in range(2):
                for c in range(DC):
                    for u in range(SUB):
                        o = (l * DC + c) * SLOT + u * P
                        last = nc.tensor.transpose(ps_t[0][:, o:o + P], xs[:, u, l, c * P:(c + 1) * P], ident16[:, :])
            last.then_inc(S["t_done"], 1)

        def slot(s, e, more):
            pe.wait_ge(S["xt_ok2"], s + 1)
            for f in range(FC):
                n = 0
                for lw, lx in ((0, 0), (0, 1), (1, 0)):
                    for c in range(DC):
                        last = nc.tensor.matmul(ps_h[f // 2][:, (f % 2) * SLOT:(f % 2 + 1) * SLOT], w1_at(e, c, lw, f), xt[:, lx, c, :],
                                                start=(f % 2 == 0 and n == 0), stop=(n == 5), skip_group_check=True)
                        n += 1
                if f % 2:
                    last.then_inc(S["h_ps2"], 1)
            if more:
                transposes(s + 1)
            if not (isinstance(s, int) and s == 0):
                pe.wait_ge(S["y_ok"], s)
            for f in range(FC):
                if f % 2 == 0:
                    pe.wait_ge(S["conv"], s * 4 + f // 2 + 1)
                for u in range(SUB):
                    for lw, lh in ((0, 0), (0, 1), (1, 0)):
                        first = f == 0 and u == 0 and lw == 0 and lh == 0
                        last = nc.tensor.matmul(ps_y[:, u * D:(u + 1) * D], hh[:, lh, f, u * P:(u + 1) * P], w2_at(e, f, lw),
                                                start=first, stop=(f == FC - 1 and lw == 1), skip_group_check=True)
            last.then_inc(S["y_ps"], 1)

        pe.wait_ge(S["w_in"], 16 * 6)
        transposes(0)
        slot(0, E, True)
        with pe.Fori(1, SH_SLOTS) as s:
            slot(s, E, True)
        pe.wait_ge(S["w_late"], 16 * 3)
        with pe.Fori(SH_SLOTS, SLOTS - 1) as s:
            e = pe.value_load(emap[0:1, bass.ds(s - SH_SLOTS, 1)], min_val=0, max_val=E - 1)
            slot(s, e, True)
        e = pe.value_load(emap[0:1, MOE_SLOTS - 1:MOE_SLOTS], min_val=0, max_val=E - 1)
        slot(SLOTS - 1, e, False)

    @block.scalar
    def _(act):
        for t in range(NT):
            if t % 8 == 0:
                act.wait_ge(S["f_var"], t // 8 + 1)
                nc.scalar.activation(rstd[:, t:t + 8], var[:, t:t + 8], ACT.Sqrt).then_inc(S["f_std"], 1)
            act.wait_ge(S["xn_ok2"], t + 1)
            nc.scalar.activation(xhl[:, t, 0, :], xnf[t % 2], ACT.Copy).then_inc(S["xhi_ok"], 1)
            act.wait_ge(S["tr_ps"], t + 1)
            nc.scalar.activation(xt[:, t % 2, :, :].rearrange("p c n -> p (c n)"), ps_t[t % 2][:, 0:4 * P], ACT.Copy).then_inc(S["tr_ok"], 1)
        act.wait_ge(S["gap_ok"], 1)
        nc.scalar.activation(gap, gap, ACT.Exp).then_inc(S["ex_ok"], 1)

        def copy_t(s):
            act.wait_ge(S["t_done"], s + 1)
            nc.scalar.activation(xt[:, :, :, :].rearrange("p l c n -> p (l c n)"), ps_t[0][:, :], ACT.Copy).then_inc(S["xt_ok2"], 1)

        def slot(s, e, more, first=False):
            for f in range(FC):
                if f % 2 == 0:
                    if not (first and f < 4):
                        act.wait_ge(S["conv"], s * 4 + f // 2 - 1)
                    act.wait_ge(S["h_ps2"], s * 4 + f // 2 + 1)
                    settle(act)
                o = e * FC + f
                bias = b1_sb[:, o:o + 1] if isinstance(o, int) else b1_sb[:, bass.ds(o, 1)]
                nc.scalar.activation(hf[:, f % 4, :], ps_h[f // 2][:, (f % 2) * SLOT:(f % 2 + 1) * SLOT], ACT.Relu, bias=bias, scale=XS / (XS * WS)).then_inc(S["relu_ok"], 1)
            if more:
                copy_t(s + 1)

        copy_t(0)
        act.wait_ge(S["rank_ps"], 1)
        slot(0, E, True, True)
        with act.Fori(1, SH_SLOTS) as s:
            slot(s, E, True)
        with act.Fori(SH_SLOTS, SLOTS - 1) as s:
            slot(s, act.value_load(emap[0:1, bass.ds(s - SH_SLOTS, 1)], min_val=0, max_val=E - 1), True)
        slot(SLOTS - 1, act.value_load(emap[0:1, MOE_SLOTS - 1:MOE_SLOTS], min_val=0, max_val=E - 1), False)

    @block.vector
    def _(dve):
        nd = [0]

        def done(ins):
            nd[0] += 1
            ins.then_inc(S["vch2"], 1)
            dve.wait_ge(S["vch2"], nd[0])

        dve.wait_ge(S["cst_in"], 64)
        wgv = wgf.rearrange("p (c e) -> p c e", e=E)
        done(nc.vector.tensor_scalar(wgf, wgf, WS, None, ALU.mult))
        done(nc.vector.tensor_copy(wg[:, 0], wgv))
        done(nc.vector.tensor_tensor(wg[:, 1], wgv, wg[:, 0], ALU.subtract))
        done(nc.vector.tensor_scalar(b1_sb[:, :], b1_sb[:, :], XS, None, ALU.mult))

        def low(t):
            dve.wait_ge(S["xhi_ok"], t + 1)
            nc.vector.tensor_tensor(xhl[:, t, 1, :], xnf[t % 2], xhl[:, t, 0, :], ALU.subtract).then_inc(S["xlo_ok"], 1)

        for k in range(4):
            sl = slice(8 * k, 8 * k + 8)
            for t in range(8 * k, 8 * k + 8):
                nc.vector.bn_stats(stats[:, t, :], x_sb[:, t, :]).then_inc(S["f_stats"], 1)
            dve.wait_ge(S["f_stats"], 8 * k + 8)
            for t in range(8 * k, 8 * k + 8):
                last = nc.vector.bn_aggr(mv[:, t, :], stats[:, t, :])
            done(last)
            nc.vector.tensor_scalar(var[:, sl], mv[:, sl, 1], 1e-5, None, ALU.add).then_inc(S["f_var"], 1)
            dve.wait_ge(S["f_std"], k + 1)
            rsqrt_refined(nc, done, rstd[:, sl], tmp[:, sl], var[:, sl])
            done(nc.vector.tensor_scalar(rstd[:, sl], rstd[:, sl], XS, None, ALU.mult))
            for t in range(8 * k, 8 * k + 8):
                if t >= 2:
                    dve.wait_ge(S["xlo_ok"], t - 1)
                nc.vector.tensor_scalar(xnf[t % 2], x_sb[:, t, :], mv[:, t, 0:1], rstd[:, t:t + 1], ALU.subtract, ALU.mult).then_inc(S["xn_ok2"], 1)
                if t % 8:
                    low(t - 1)
            low(8 * k + 7)
        dve.wait_ge(S["cst"], 3)
        done(nc.vector.tensor_copy(iota_f, iota_i))
        done(nc.vector.tensor_scalar(k256, iota_f[:, 0:16], float(SLOT), None, ALU.mult))
        done(nc.vector.tensor_scalar(desc, iota_f[:, 0:E], -1.0, float(E), ALU.mult, ALU.add))
        dve.wait_ge(S["g_ps"], 1)

        def per_t(v):
            return v.rearrange("p (t o) -> p t o", o=1).broadcast_to([P, NT, E])

        def per_e(v, n=NT):
            return v.rearrange("p (o e) -> p o e", o=1).broadcast_to([P, n, E])

        scr_te = te(scr[:, 0:NT * E])
        done(nc.vector.scalar_tensor_tensor(out=logit, in0=ps_g[:, 0:NT * E].rearrange("p (t e) -> p t e", e=E), scalar=1.0 / (XS * WS), in1=per_e(bg_sb), op0=ALU.mult, op1=ALU.add))

        def first_best(one, best):
            done(nc.vector.tensor_reduce(best, logit, AX, ALU.max))
            done(nc.vector.tensor_tensor(scr_te, logit, per_t(best), ALU.is_equal))
            done(nc.vector.tensor_tensor(scr_te, scr_te, per_e(desc), ALU.mult))
            done(nc.vector.tensor_reduce(mark, scr_te, AX, ALU.max))
            done(nc.vector.tensor_tensor(one, scr_te, per_t(mark), ALU.is_equal))

        first_best(one0, top)
        done(nc.vector.scalar_tensor_tensor(out=logit, in0=one0, scalar=-1e30, in1=logit, op0=ALU.mult, op1=ALU.add))
        first_best(one1, gap)
        done(nc.vector.tensor_tensor(gap, gap, top, ALU.subtract))
        dve.sem_inc(S["gap_ok"], 1)
        nc.vector.tensor_tensor(both, one0, one1, ALU.add).then_inc(S["both_ok"], 1)
        dve.wait_ge(S["ex_ok"], 1)
        done(nc.vector.tensor_scalar(wts[:, 0, :], gap, 1.0, None, ALU.add))
        done(nc.vector.reciprocal(wts[:, 0, :], wts[:, 0, :]))
        done(nc.vector.tensor_tensor(wts[:, 1, :], gap, wts[:, 0, :], ALU.mult))
        dve.wait_ge(S["rank_ps"], 1)
        tot = ps_g[:, NT * E:2 * NT * E].rearrange("p (t e) -> p t e", e=E)
        done(nc.vector.tensor_copy(scan0, tot))
        a, b = scan0, scan1
        d = 1
        while d < NT:
            done(nc.vector.tensor_copy(b[:, 0:d, :], a[:, 0:d, :]))
            done(nc.vector.tensor_tensor(b[:, d:NT, :], a[:, d:NT, :], a[:, 0:NT - d, :], ALU.add))
            a, b = b, a
            d *= 2
        sc16 = scr[:, 0:E * 16].rearrange("p (e k) -> p e k", k=16)
        done(nc.vector.tensor_tensor(sc16, a[:, NT - 1, :].rearrange("p (e o) -> p e o", o=1).broadcast_to([P, E, 16]),
                                     k256.rearrange("p (o k) -> p o k", o=1).broadcast_to([P, E, 16]), ALU.is_gt))
        done(nc.vector.tensor_reduce(cnt, sc16, AX, ALU.add))
        done(nc.vector.tensor_copy(ends, cnt))
        c0, c1 = ends, ends2
        d = 1
        while d < E:
            done(nc.vector.tensor_copy(c1[:, 0:d], c0[:, 0:d]))
            done(nc.vector.tensor_tensor(c1[:, d:E], c0[:, d:E], c0[:, 0:E - d], ALU.add))
            c0, c1 = c1, c0
            d *= 2
        sce = scr[:, 0:MOE_SLOTS * E].rearrange("p (s e) -> p s e", e=E)
        done(nc.vector.tensor_tensor(sce, per_e(c0, MOE_SLOTS), iota_f.rearrange("p (s o) -> p s o", o=1).broadcast_to([P, MOE_SLOTS, E]), ALU.is_le))
        done(nc.vector.tensor_reduce(iota_f, sce, AX, ALU.add))
        done(nc.vector.tensor_scalar(emap[:, :], iota_f, float(E - 1), None, ALU.min))
        done(nc.vector.tensor_tensor(c1, c0, cnt, ALU.subtract))
        done(nc.vector.tensor_scalar(c1, c1, float(SLOT), float(SH_SLOTS * SLOT), ALU.mult, ALU.add))
        done(nc.vector.tensor_tensor(a, a, tot, ALU.subtract))
        done(nc.vector.tensor_tensor(a, a, ps_g[:, 0:NT * E].rearrange("p (t e) -> p t e", e=E), ALU.add))
        done(nc.vector.tensor_tensor(a, a, per_e(c1), ALU.add))
        for k, one in enumerate((one0, one1)):
            done(nc.vector.tensor_tensor(scr_te, one, a, ALU.mult))
            done(nc.vector.tensor_reduce(posf, scr_te, AX, ALU.add))
            done(nc.vector.tensor_copy(pos_i[:, k, :], posf))
        dve.sem_inc(S["pos_ok"], 1)

        def slot(s, e):
            for k in range(4):
                dve.wait_ge(S["relu_ok"], s * FC + 2 * k + 2)
                nc.vector.tensor_copy(hh[:, 0, 2 * k:2 * k + 2, :], hf[:, 2 * k % 4:2 * k % 4 + 2, :]).then_inc(S["hi_ok"], 1)
                dve.wait_ge(S["hi_ok"], s * 4 + k + 1)
                nc.vector.tensor_tensor(hh[:, 1, 2 * k:2 * k + 2, :], hf[:, 2 * k % 4:2 * k % 4 + 2, :], hh[:, 0, 2 * k:2 * k + 2, :], ALU.subtract).then_inc(S["conv"], 1)
            if not (isinstance(s, int) and s == 0):
                dve.wait_ge(S["y_out"], s * 16)
            dve.wait_ge(S["y_ps"], s + 1)
            settle(dve)
            for u in range(SUB):
                b2 = b2_sb[:, e, :] if isinstance(e, int) else b2_sb[:, :, :].rearrange("p e d -> p (e d)")[:, bass.ds(e * D, D)]
                last = nc.vector.scalar_tensor_tensor(out=y_sb[:, u, :], in0=ps_y[:, u * D:(u + 1) * D], scalar=1.0 / (XS * WS), in1=b2, op0=ALU.mult, op1=ALU.add)
            last.then_inc(S["y_ok"], 1)

        slot(0, E)
        with dve.Fori(1, SH_SLOTS) as s:
            slot(s, E)
        with dve.Fori(SH_SLOTS, SLOTS) as s:
            slot(s, dve.value_load(emap[0:1, bass.ds(s - SH_SLOTS, 1)], min_val=0, max_val=E - 1))

        for t in range(NT):
            k = t % 4
            dve.wait_ge(g_in[k], 32 * (t // 4 + 1))
            dve.wait_ge(s_in[k], 16 * (t // 4 + 1))
            if t >= 4:
                dve.wait_ge(fin_out[k], 16 * (t // 4))
            done(nc.vector.scalar_tensor_tensor(out=gbuf[:, k, 3, :], in0=gbuf[:, k, 0, :], scalar=wts[:, 0, t:t + 1], in1=x_sb[:, t, :], op0=ALU.mult, op1=ALU.add))
            done(nc.vector.scalar_tensor_tensor(out=gbuf[:, k, 3, :], in0=gbuf[:, k, 1, :], scalar=wts[:, 1, t:t + 1], in1=gbuf[:, k, 3, :], op0=ALU.mult, op1=ALU.add))
            nc.vector.scalar_tensor_tensor(out=gbuf[:, k, 3, :], in0=gbuf[:, k, 2, :], scalar=1.0 / K, in1=gbuf[:, k, 3, :], op0=ALU.mult, op1=ALU.add).then_inc(S["fin_ok"], 1)


def gat_moe_kernel(nc, x, adj_t, w_t, w_n, b_w, a, w_route, b_route, w_all, b1_all, b2_all, out):
    s_dram = nc.dram_tensor("s_dram", (H, N), F32, kind="Internal").ap()
    v_dram = nc.dram_tensor("v_dram", (H, P, NT * VW), F16, kind="Internal").ap()
    d_dram = nc.dram_tensor("d_dram", (H, P, 2 * NT), F32, kind="Internal").ap()
    w16_dram = nc.dram_tensor("w16_dram", (UNITS, P, 2, F), F16, kind="Internal").ap()
    xs_dram = nc.dram_tensor("xs_dram", (N_ROWS, 2 * D), F16, kind="Internal").ap()
    ys_dram = nc.dram_tensor("ys_dram", (N_ROWS, D), F32, kind="Internal").ap()
    with ExitStack() as outer:
        outer.enter_context(nc.allow_non_contiguous_dma(reason="biases and a few vectors of a hundred elements"))
        x_sb = outer.enter_context(nc.sbuf_tensor("x_sb", [P, NT, D], F32))
        with ExitStack() as ctx:
            gat(nc, ctx, x_sb, x, adj_t, w_t, w_n, b_w, a, w_all, s_dram, v_dram, d_dram, w16_dram, xs_dram)
        with ExitStack() as ctx:
            ffn(nc, ctx, x_sb, w_route, b_route, b1_all, b2_all, w16_dram, xs_dram, ys_dram, out)


def kernel(x, adj, L0_gnn_W_w, L0_gnn_W_b, L0_gnn_a, L0_ffn_Wg, L0_ffn_bg, L0_ffn_W1, L0_ffn_b1, L0_ffn_W2, L0_ffn_b2,
           L0_ffn_Ws1, L0_ffn_bs1, L0_ffn_Ws2, L0_ffn_bs2):
    import numpy as np
    import concourse.bacc as bacc
    from concourse.bass_utils import run_bass_kernel_spmd

    def arr(v):
        return np.asarray(v)

    w1 = np.concatenate([arr(L0_ffn_W1), arr(L0_ffn_Ws1)[None]]).reshape(E + 1, DC, P, F)
    w2 = np.concatenate([arr(L0_ffn_W2), arr(L0_ffn_Ws2)[None]]).reshape(E + 1, 2, 4, P, D).transpose(0, 1, 3, 2, 4).reshape(E + 1, 2, P, F)
    arrays = {
        "x": arr(x),
        "adj_t": arr(adj).T.reshape(NT, P, NB, BI).transpose(2, 0, 1, 3),
        "w_t": arr(L0_gnn_W_w).T, "w_n": arr(L0_gnn_W_w), "b_w": arr(L0_gnn_W_b), "a": arr(L0_gnn_a),
        "w_route": arr(L0_ffn_Wg), "b_route": arr(L0_ffn_bg),
        "w_all": np.concatenate([w1, w2], axis=1).reshape(UNITS, P, F),
        "b1_all": np.concatenate([arr(L0_ffn_b1).reshape(-1), arr(L0_ffn_bs1)]),
        "b2_all": np.concatenate([arr(L0_ffn_b2), arr(L0_ffn_bs2)[None]]),
    }
    arrays = {k: np.ascontiguousarray(v) for k, v in arrays.items()}
    nc = bacc.Bacc("TRN2", target_bir_lowering=False, num_devices=1)
    args = {k: nc.dram_tensor(k, v.shape, mybir.dt.from_np(v.dtype), kind="ExternalInput").ap() for k, v in arrays.items()}
    out = nc.dram_tensor("out", (N, D), F32, kind="ExternalOutput").ap()
    gat_moe_kernel(nc, **args, out=out)
    r = run_bass_kernel_spmd(nc, [arrays], core_ids=[0])
    return r.results[0]["out"]
```

```python
from contextlib import ExitStack
import math

import concourse.bass as bass
from concourse import mybir

F32 = mybir.dt.float32
F16 = mybir.dt.float16
F8 = mybir.dt.float8e4
I32 = mybir.dt.int32
U32 = mybir.dt.uint32
ALU = mybir.AluOpType
ACT = mybir.ActivationFunctionType
AX = mybir.AxisListType.X
RMAX = bass.bass_isa.ReduceOp.max

P = 128
N = 4096
D = 256
H = 8
HD = D // H
DC = D // P
NT = N // P
BI = 1024
NB = N // BI
IT = BI // P
VC = HD + 1
VW = 4 * VC
S0 = 2 * H
CW = S0 + D
NPAIR = NT // 2
MINUS_ONE = 0xB8
GJ = 4
NG = NT // GJ
ACT_T = [2, 2, 2, 3, 2, 2, 2, 3]
DVE_T = [GJ - n for n in ACT_T]
RING = 4
STAGE = 2
VSCALE = 256.0
STEP = 2.0 ** 40
BANK = 512
E = 8
K = 2
F = 1024
FC = F // P
EW = 8 * F
UNITS = 4 * (E + 1)
SLOT = 256
SUB = SLOT // P
SH_A = N // SLOT // 2
MOE_SLOTS = (K * N - E) // SLOT + E
SLOTS = 2 * SH_A + MOE_SLOTS
SH_B = SH_A + MOE_SLOTS
N_ROWS = SLOTS * SLOT
XS = 16.0
WS = 256.0


def rsqrt_refined(nc, done, y, t, v):
    done(nc.vector.reciprocal(y, y))
    done(nc.vector.tensor_tensor(t, y, y, ALU.mult))
    done(nc.vector.tensor_tensor(t, t, v, ALU.mult))
    done(nc.vector.tensor_scalar(t, t, -0.5, 1.5, ALU.mult, ALU.add))
    done(nc.vector.tensor_tensor(y, y, t, ALU.mult))


def gat(nc, ctx, hext, x, x_t, adj_t, w_t, w_n, b_w, a, w_all, s_dram, v_dram, d_dram, w16_dram, xs_dram):
    def sb(name, shape, dt=F32):
        return ctx.enter_context(nc.sbuf_tensor(name, shape, dt))

    def ps(name, shape):
        return ctx.enter_context(nc.psum_tensor(name, shape, F32))

    def sem(name):
        return ctx.enter_context(nc.semaphore(name))

    wext = sb("wext", [P, DC, CW])
    wn_sb = sb("wn_sb", [P, DC, D])
    acol = sb("acol", [P, 2])
    ablk = sb("ablk", [P, DC, S0])
    bcol = sb("bcol", [P, DC])
    bext = sb("bext", [1, CW])
    bias = sb("bias", [P, CW])
    ones = sb("ones", [P, P])
    ident = sb("ident", [P, P])
    stats = sb("stats", [P, NT, 6])
    mv = sb("mv", [P, NT, 2])
    rstd = sb("rstd", [P, NT])
    var = sb("var", [P, NT])
    tmp = sb("tmp", [P, NT])
    st_sb = sb("st_sb", [H, 2, 4 * P])
    hmean = sb("hmean", [P, D])
    dmx = sb("dmx", [P, H])
    dmxa = sb("dmxa", [P, H])
    dcol = sb("dcol", [P, H, 2, NT])
    fw = sb("fw", [P, 2, NT, H])
    ab = sb("ab", [P, 2, NT, H])
    lnc = sb("lnc", [P, 1])
    ws_col = sb("ws_col", [P, 1])
    stage = sb("stage", [P, STAGE, 2, BI], I32)
    x_sb = sb("x_sb", [P, NT, D])
    masks = sb("masks", [P, NT + RING * GJ, BI], F8)
    mask = [x_sb[:, :, :].rearrange("p t d -> p (t d)").bitcast(F8).rearrange("p (t i) -> p t i", i=BI), masks[:, 0:NT, :]]
    mask_u8 = [m.bitcast(mybir.dt.uint8) for m in mask]
    m_ring = masks[:, NT:NT + RING * GJ, :]
    flat = masks[:, :, :].rearrange("p a b -> p (a b)")
    xt_sb = flat[:, 0:NT * BI].bitcast(F32).rearrange("p (c n) -> p c n", c=DC)
    VB = NT * 2 * VC * 4
    v32 = [flat[:, o:o + VB].bitcast(F32).rearrange("p (t s c) -> p t s c", s=2, c=VC) for o in (NT * BI, 0)]
    v_cur = sb("v_cur", [P, 2, NT, VW], F16)
    d_cur = sb("d_cur", [P, 2, 2, NT])
    s_cur = sb("s_cur", [P, 2, BI])
    comb = sb("comb", [P, 2, IT, 2, 2, VC])
    hp = hext[:, :, S0:CW]
    pw = sb("pw", [P, 2, IT, VC])
    den = sb("den", [P, NT, H])
    flag = sb("flag", [P, IT])
    fl = sb("fl", [P, IT, HD])
    HV = NT // 2 * 2 * VC
    wbuf = sb("wbuf", [P, 2 * HV])
    wf = wbuf[:, 0:F]
    w16 = wbuf[:, F:2 * F].bitcast(F16).rearrange("p (l c) -> p l c", l=2)
    zeros = sb("zeros", [P, 2 * D], F16)
    pv32 = wbuf[:, 0:HV].rearrange("p (t s c) -> p t s c", s=2, c=VC)
    pvb = wbuf[:, HV:2 * HV].bitcast(F16)
    pvb5 = pvb.rearrange("p (t s l c) -> p t s l c", s=2, l=2, c=VC)

    acc = [[ps(f"acc{q}{k}", [P, BANK]) for k in range(3)] for q in range(2)]
    aux = [ps(f"aux{k}", [P, BANK]) for k in range(2)]
    h_ps_buf = [acc[0][0], acc[0][1], acc[0][2], acc[1][0]]

    Z_STEPS = 26
    Z_ROWS = MOE_SLOTS * SLOT // Z_STEPS

    names = """w_in a_in ident_ok stats_ok var_ok std_ok h_ps h_ok sT_ps sT_ok wa_ps wa_ok dmx_ok dmxa_ok fw_in
        fw_ok v32_ok vhi_ok vb_ok v_st vb_out pvch d_ok d_out hm_ps hm_ok dch pch ach conv_ok dve_t act_t m_ready pe_done
        comb_ok comb_free hp_ok hm_in settled z_ok z_out wf_in wch w16_out""".split()
    S = {n: sem(n) for n in names}
    x_in = [sem(f"x_in{k}") for k in range(4)]
    xt_in = [sem(f"xt_in{k}") for k in range(4)]
    x2_in = [sem(f"x2_in{k}") for k in range(2)]
    v_in = [sem(f"v_in{q}") for q in range(2)]
    st_out = [sem(f"st_out{k}") for k in range(2)]
    sc_in = [sem(f"sc_in{q}") for q in range(2)]
    adj_in = [sem(f"adj_in{k}") for k in range(STAGE)]
    XH = NT // 2
    x_again = [x_sb[:, k * XH:(k + 1) * XH, :] for k in range(2)]

    adj_v = adj_t.rearrange("b (n k) p i -> b n p k i", k=2)

    def acc_tile(q, it, a0, a1):
        o = (it % 3) * VW
        return acc[q][it // 3][:, o + a0:o + a1]

    def settle(eng):
        eng.sem_inc(S["settled"], 1)

    stage_f = [stage[:, k, :, :].bitcast(F32).rearrange("p a i -> p (a i)").rearrange("p (t d) -> p t d", d=D) for k in range(2)]
    block = ctx.enter_context(nc.Block())

    @block.sync
    def _(sp):
        sp.dma_start(wn_sb[:, :, :], w_n.rearrange("(c p) n -> p c n", p=P)).then_inc(S["w_in"], 16)
        sp.dma_start(wext[:, :, S0:CW], w_t.rearrange("(c p) n -> p c n", p=P)).then_inc(S["w_in"], 16)
        for k in range(4):
            sp.dma_start(xt_sb[:, :, k * 1024:(k + 1) * 1024], x_t[:, :, k * 1024:(k + 1) * 1024].rearrange("c p n -> p c n")).then_inc(xt_in[k], 16)
            sp.dma_start(x_sb[:, k * 8:k * 8 + 8, :], x[k * 1024:(k + 1) * 1024, :].rearrange("(t p) d -> p t d", p=P)).then_inc(x_in[k], 16)

        def load_pair(b, n, k):
            sp.dma_start(stage[:, k, :, :], adj_v[bass.ds(b, 1), n].rearrange("a p k i -> (a p) k i")).then_inc(adj_in[k], 16)

        load_pair(0, 0, 0)
        load_pair(0, 1, 1)
        for n in range(2, NPAIR):
            if n == 12:
                for k in range(2):
                    sp.wait_ge(st_out[k], 16 * (NT // 8))
                for q in range(2):
                    sp.dma_start(s_cur[:, q, :], s_dram[q:q + 1, 0:BI].broadcast_to([P, BI])).then_inc(sc_in[q], 16)
            sp.wait_ge(S["conv_ok"], n - 1)
            load_pair(0, n, n % 2)
        sp.wait_ge(S["d_ok"], 1)
        sp.dma_start(d_dram.rearrange("h p c -> p h c"), dcol[:, :, :, :].rearrange("p h a t -> p h (a t)")).then_inc(S["d_out"], 16)
        sp.wait_ge(S["vb_ok"], 2)
        for q in range(2):
            sp.dma_start(v_dram[q], v_cur[:, q, :, :].rearrange("p t c -> p (t c)")).then_inc(S["v_st"], 16)
        sp.wait_ge(S["d_out"], 16)
        sp.wait_ge(S["v_st"], 32)
        sp.wait_ge(S["z_ok"], 2)

        def step(b, h, masks_too, first_block=False):
            g = b * H + h
            if g < Z_STEPS if isinstance(g, int) else masks_too:
                sp.dma_start(xs_dram[bass.ds(g * Z_ROWS, Z_ROWS), :].rearrange("(r p) c -> p r c", p=P),
                             zeros[:, :].rearrange("p (o c) -> p o c", o=1).broadcast_to([P, Z_ROWS // P, 2 * D])).then_inc(S["z_out"], 16)
            if masks_too:
                for k in range(2):
                    sp.wait_ge(S["conv_ok"], g * 2 + NPAIR - 1 + k)
                    load_pair(b + 1, 2 * h + k, k)
            if b == NB - 1 and h >= H - 2 if isinstance(b, int) else False:
                return
            q, b2, h2 = h % 2, b + (h + 2) // H, (h + 2) % H
            if first_block and h2 >= 2:
                sp.wait_ge(S["vb_out"], 32 * (h2 - 1))
            sp.wait_ge(S["pe_done"], g * NG + NG)
            sp.dma_start(v_cur[:, q, :, :].rearrange("p t c -> p (t c)"), v_dram[h2]).then_inc(v_in[q], 16)
            sp.dma_start(d_cur[:, q, :, :].rearrange("p a t -> p (a t)"), d_dram[h2]).then_inc(v_in[q], 16)
            sp.dma_start(s_cur[:, q, :], s_dram[h2:h2 + 1, bass.ds(b2 * BI, BI)].broadcast_to([P, BI])).then_inc(sc_in[q], 16)

        for h in range(H):
            step(0, h, True, True)
        with sp.Fori(1, NB - 1) as b:
            for h in range(H):
                step(b, h, True)
        for h in range(H):
            step(NB - 1, h, False)
            if h == 2:
                for k in range(2):
                    sp.dma_start(x_again[k], x[k * XH * P:(k + 1) * XH * P, :].rearrange("(t p) d -> p t d", p=P)).then_inc(x2_in[k], 16)
        sp.wait_ge(S["w16_out"], 16 * UNITS)
        sp.wait_ge(S["z_out"], 16 * Z_STEPS)

    @block.gpsimd
    def _(pool):
        nc.gpsimd.memset(ident[:, :], 0.0).then_inc(S["pch"], 1)
        nc.gpsimd.memset(lnc[:, :], math.log(VSCALE)).then_inc(S["pch"], 1)
        nc.gpsimd.memset(ones[:, :], 1.0).then_inc(S["pch"], 1)
        nc.gpsimd.memset(ws_col[:, :], WS).then_inc(S["z_ok"], 1)
        pool.wait_ge(S["pch"], 3)
        nc.gpsimd.affine_select(out=ident[:, :], in_=ident[:, :], compare_op=ALU.not_equal, fill=1.0, base=0,
                                pattern=[[-1, P]], channel_multiplier=1).then_inc(S["ident_ok"], 1)
        nc.gpsimd.memset(zeros[:, :], 0.0).then_inc(S["z_ok"], 1)
        pool.wait_ge(S["z_ok"], 2)
        pool.wait_ge(S["dmx_ok"], 1)
        nc.gpsimd.partition_all_reduce(dmxa[:, :], dmx[:, :], P, RMAX).then_inc(S["dmxa_ok"], 1)

        nv = [0]

        def v_done(ins):
            nv[0] += 1
            ins.then_inc(S["pvch"], 1)
            pool.wait_ge(S["pvch"], nv[0])

        stored = [0]

        def build_v(h):
            for k in range(2):
                sl = slice(k * NT // 2, (k + 1) * NT // 2)
                for s in range(2):
                    f = fw[:, s, sl, h:h + 1]
                    nc.gpsimd.tensor_tensor(pv32[:, :, s, 0:HD], hp[:, sl, h * HD:(h + 1) * HD], f.broadcast_to([P, NT // 2, HD]), ALU.mult).then_inc(S["pvch"], 1)
                    nc.gpsimd.tensor_copy(pv32[:, :, s, HD:VC], f).then_inc(S["pvch"], 1)
                if stored[0]:
                    pool.wait_ge(S["vb_out"], 16 * stored[0])
                for s in range(2):
                    f = fw[:, s, sl, h:h + 1]
                    nc.gpsimd.tensor_tensor(pvb5[:, :, s, 0, 0:HD], hp[:, sl, h * HD:(h + 1) * HD], f.broadcast_to([P, NT // 2, HD]), ALU.mult).then_inc(S["pvch"], 1)
                    nc.gpsimd.tensor_copy(pvb5[:, :, s, 0, HD:VC], f).then_inc(S["pvch"], 1)
                nv[0] += 8
                pool.wait_ge(S["pvch"], nv[0])
                v_done(nc.gpsimd.tensor_tensor(pvb5[:, :, :, 1, :], pv32, pvb5[:, :, :, 0, :], ALU.subtract))
                pool.dma_start(v_dram[h].rearrange("p (k c) -> k p c", k=2)[k], pvb).then_inc(S["vb_out"], 16)
                stored[0] += 1

        LINKS = 9

        def finish_head(b, h, q):
            g = b * H + h
            link = [0]

            def done(ins):
                link[0] += 1
                ins.then_inc(S["pch"], 1)
                pool.wait_ge(S["pch"], 3 + g * LINKS + link[0])

            pool.wait_ge(S["comb_ok"], g + 3)
            al = ab[:, 0, bass.ds(b * IT, IT), h:h + 1].broadcast_to([P, IT, VC])
            be = ab[:, 1, bass.ds(b * IT, IT), h:h + 1].broadcast_to([P, IT, VC])
            for s in range(2):
                done(nc.gpsimd.tensor_tensor(pw[:, s], comb[:, q, :, s, 0, :], comb[:, q, :, s, 1, :], ALU.add))
            done(nc.gpsimd.tensor_tensor(pw[:, 0], pw[:, 0], al, ALU.mult))
            done(nc.gpsimd.tensor_tensor(pw[:, 1], pw[:, 1], be, ALU.mult))
            done(nc.gpsimd.tensor_tensor(pw[:, 0], pw[:, 0], pw[:, 1], ALU.add))
            settle(pool)
            done(nc.gpsimd.tensor_scalar(flag[:, :], pw[:, 0, :, HD], 0.0, None, ALU.is_equal))
            done(nc.gpsimd.tensor_tensor(den[:, bass.ds(b * IT, IT), h], pw[:, 0, :, HD], flag[:, :], ALU.add))
            done(nc.gpsimd.tensor_tensor(fl[:, :, :], flag[:, :].rearrange("p (t o) -> p t o", o=1).broadcast_to([P, IT, HD]),
                                         hmean[:, h * HD:(h + 1) * HD].rearrange("p (o c) -> p o c", o=1).broadcast_to([P, IT, HD]), ALU.mult))
            done(nc.gpsimd.tensor_tensor(hp[:, bass.ds(b * IT, IT), h * HD:(h + 1) * HD], pw[:, 0, :, 0:HD], fl[:, :, :], ALU.add))
            pool.sem_inc(S["comb_free"], 1)

        def split_unit(u):
            if not isinstance(u, int) or u:
                pool.wait_ge(S["wch"], u * 3)
            pool.dma_start(wf, w_all[bass.ds(u, 1)].rearrange("o p c -> (o p) c")).then_inc(S["wf_in"], 16)
            pool.wait_ge(S["wf_in"], u * 16 + 16)
            settle(pool)
            if not isinstance(u, int) or u:
                pool.wait_ge(S["w16_out"], u * 16)
            settle(pool)
            nc.gpsimd.tensor_tensor(w16[:, 0, :], wf, ws_col.broadcast_to([P, F]), ALU.mult).then_inc(S["wch"], 1)
            pool.wait_ge(S["wch"], u * 3 + 1)
            nc.gpsimd.tensor_tensor(wf, wf, ws_col.broadcast_to([P, F]), ALU.mult).then_inc(S["wch"], 1)
            pool.wait_ge(S["wch"], u * 3 + 2)
            nc.gpsimd.tensor_tensor(w16[:, 1, :], wf, w16[:, 0, :], ALU.subtract).then_inc(S["wch"], 1)
            pool.wait_ge(S["wch"], u * 3 + 3)
            pool.dma_start(w16_dram[bass.ds(u, 1)].rearrange("o p l c -> (o p) (l c)"), w16.rearrange("p l c -> p (l c)")).then_inc(S["w16_out"], 16)

        pool.wait_ge(S["fw_ok"], 3)
        pool.sem_inc(S["comb_free"], 1)
        build_v(2)
        build_v(3)
        pool.wait_ge(S["fw_ok"], 4)
        pool.wait_ge(S["hm_ok"], 1)
        for h in range(H):
            if h < H - 4:
                build_v(h + 4)
            finish_head(0, h, h % 2)
            if h == 4:
                pool.wait_ge(S["vb_out"], 16 * stored[0])
            for u in ([], [], [], [], [0, 1], [2, 3], [4, 5], [6, 7, 8])[h]:
                split_unit(u)
        with pool.Fori(1, NB) as b:
            for h in range(H):
                finish_head(b, h, h % 2)
                split_unit(b * (UNITS // NB) + h)
            split_unit(b * (UNITS // NB) + H)

    @block.tensor
    def _(pe):
        pe.wait_ge(S["w_in"], 64)
        pe.wait_ge(S["wa_ok"], 1)
        pe.wait_ge(S["ident_ok"], 1)
        wa = aux[0]
        for c in range(DC):
            for k in range(DC):
                nc.tensor.matmul(wa[:, c * S0:(c + 1) * S0], wn_sb[:, k, c * P:(c + 1) * P], ablk[:, k, :], start=(c == 0 and k == 0), stop=(k == DC - 1), skip_group_check=True)
        for k in range(DC):
            last = nc.tensor.matmul(wa[0:1, 2 * S0:3 * S0], bcol[:, k:k + 1], ablk[:, k, :], start=False, stop=(k == DC - 1), skip_group_check=True)
        last.then_inc(S["wa_ps"], 1)
        pe.wait_ge(S["wa_ok"], 2)
        nc.tensor.matmul(acc[0][0][:, 0:CW], ones[0:1, :], bext[:, :], start=True, stop=True)
        for c in range(DC):
            last = nc.tensor.matmul(acc[0][1][:, 0:CW], ones[:, :], wext[:, c, :], start=(c == 0), stop=(c == DC - 1))
        last.then_inc(S["wa_ps"], 1)
        pe.wait_ge(S["wa_ok"], 3)

        def transpose_scores(t):
            pe.wait_ge(S["h_ok"], t + 1)
            if t % 4 == 0 and t >= 8:
                pe.wait_ge(S["sT_ok"], t // 4 - 1)
            last = nc.tensor.transpose(aux[(t // 4) % 2][:, (t % 4) * P:(t % 4 + 1) * P], hext[:, t, 0:P], ident[:, :])
            if t % 4 == 3:
                last.then_inc(S["sT_ps"], 1)

        for t in range(NT):
            if t % 8 == 0:
                pe.wait_ge(xt_in[t // 8], 16)
            if t >= 4:
                pe.wait_ge(S["h_ok"], t - 3)
            for c in range(DC):
                last = nc.tensor.matmul(h_ps_buf[t % 4][:, 0:CW], xt_sb[:, c, t * P:(t + 1) * P], wext[:, c, :], start=(c == 0), stop=(c == DC - 1))
            last.then_inc(S["h_ps"], 1)
            if t >= 2:
                transpose_scores(t - 2)
        transpose_scores(NT - 2)
        transpose_scores(NT - 1)
        for t in range(NT):
            last = nc.tensor.matmul(acc[1][1][:, 0:D], ones[:, :], hp[:, t, :], start=(t == 0), stop=(t == NT - 1))
        last.then_inc(S["hm_ps"], 1)
        pe.wait_ge(S["hm_ok"], 1)

        def head(b, r, q, par):
            g = b * H + 2 * r + q
            pe.wait_ge(v_in[q], (b * (H // 2) + r) * 32 + 32)
            for n in range(NG):
                if n == 0:
                    pe.wait_ge(S["comb_ok"], g + 1)
                pe.wait_ge(S["m_ready"], g * NG + n + 1)
                settle(pe)
                for jj in range(GJ):
                    j = n * GJ + jj
                    slot = j % (RING * GJ)
                    for it in range(IT):
                        nc.tensor.matmul(acc_tile(q, it, 0, VW), m_ring[:, slot, it * P:(it + 1) * P], v_cur[:, q, j, :],
                                         start=(j == 0 and it % 3 == 0), stop=False, skip_group_check=True)
                        last = nc.tensor.matmul(acc_tile(q, it, 2 * VC, VW), mask[par][:, j, it * P:(it + 1) * P], v_cur[:, q, j, 2 * VC:VW],
                                                start=False, stop=(j == NT - 1), skip_group_check=True)
                last.then_inc(S["pe_done"], 1)

        with pe.Fori(0, NB, 2) as b:
            for par in range(2):
                with pe.Fori(0, H // 2) as r:
                    head(b + par, r, 0, par)
                    head(b + par, r, 1, par)

    @block.scalar
    def _(act):
        act.dma_start(acol[:, :], a).then_inc(S["a_in"], 16)
        act.dma_start(bcol[:, :], b_w.rearrange("(c p) -> p c", p=P)).then_inc(S["w_in"], 16)
        act.dma_start(bext[:, S0:CW], b_w.rearrange("(a n) -> a n", a=1)).then_inc(S["w_in"], 16)

        def root(k):
            act.wait_ge(S["var_ok"], k + 1)
            nc.scalar.activation(rstd[:, k * 8:k * 8 + 8], var[:, k * 8:k * 8 + 8], ACT.Sqrt).then_inc(S["std_ok"], 1)

        root(0)
        for k in range(NT // 4):
            if k % 2 == 0 and k < 6:
                root(k // 2 + 1)
            act.wait_ge(S["sT_ps"], k + 1)
            if k >= 2:
                act.wait_ge(st_out[k % 2], 16 * (k // 2))
            nc.scalar.activation(st_sb[:, k % 2, :], aux[k % 2][0:H, :], ACT.Copy).then_inc(S["sT_ok"], 1)
            act.wait_ge(S["sT_ok"], k + 1)
            act.dma_start(s_dram[:, k * 4 * P:(k + 1) * 4 * P], st_sb[:, k % 2, :]).then_inc(st_out[k % 2], 16)
        act.wait_ge(S["fw_in"], 1)
        nc.scalar.activation(fw[:, 0], fw[:, 0], ACT.Exp, bias=lnc[:, :]).then_inc(S["fw_ok"], 1)
        nc.scalar.activation(fw[:, 1], fw[:, 1], ACT.Exp, bias=lnc[:, :]).then_inc(S["fw_ok"], 1)
        for h in range(2):
            act.wait_ge(S["v32_ok"], h + 1)
            v5 = v_cur[:, h, :, :].rearrange("p t (s l c) -> p t s l c", s=2, l=2)
            nc.scalar.activation(v5[:, :, :, 0, :], v32[h], ACT.Copy).then_inc(S["vhi_ok"], 1)
        act.wait_ge(S["fw_in"], 2)
        nc.scalar.activation(ab[:, :, :, :], ab[:, :, :, :], ACT.Exp).then_inc(S["fw_ok"], 1)
        act.wait_ge(S["hm_ps"], 1)
        nc.scalar.activation(hmean[:, :], acc[1][1][:, 0:D], ACT.Copy, scale=1.0 / N).then_inc(S["hm_ok"], 1)
        act.wait_ge(S["vb_ok"], 2)

        def head(g, r, q):
            act.wait_ge(v_in[q], r * 32 + 32)
            act.wait_ge(sc_in[q], r * 16 + 16)
            for n in range(NG):
                if isinstance(g, int) and g == 0:
                    if n >= RING:
                        act.wait_ge(S["pe_done"], n - RING + 1)
                else:
                    act.wait_ge(S["pe_done"], g * NG + n - RING + 1)
                settle(act)
                for jj in range(ACT_T[n]):
                    j = n * GJ + jj
                    nc.scalar.activation(m_ring[:, j % (RING * GJ), :], s_cur[:, q, :], ACT.Sigmoid,
                                         bias=d_cur[:, q, 1, j:j + 1], scale=STEP, saturate=False).then_inc(S["act_t"], 1)

        head(0, 0, 0)
        head(1, 0, 1)
        with act.Fori(1, NB * H // 2) as r:
            head(2 * r, r, 0)
            head(2 * r + 1, r, 1)
        for k in range(4):
            act.wait_ge(S["hm_in"], k + 1)
            nc.scalar.activation(stage_f[k % 2], stage_f[k % 2], ACT.Exp).then_inc(S["ach"], 1)

    @block.vector
    def _(dve):
        nd = [0]

        def done(ins):
            nd[0] += 1
            ins.then_inc(S["dch"], 1)
            dve.wait_ge(S["dch"], nd[0])

        dve.sem_inc(S["comb_ok"], 2)
        done(nc.vector.memset(ablk[:, :, :], 0.0))
        dve.wait_ge(S["a_in"], 16)
        for q in range(4):
            for c in range(DC):
                for s in range(2):
                    k = s * H + c * 4 + q
                    last = nc.vector.tensor_copy(ablk[32 * q:32 * q + 32, c, k:k + 1], acol[32 * q:32 * q + 32, s:s + 1])
        done(last)
        dve.sem_inc(S["wa_ok"], 1)

        def statistics(k):
            dve.wait_ge(x_in[k], 16)
            for t in range(k * 8, k * 8 + 8):
                nc.vector.bn_stats(stats[:, t, :], x_sb[:, t, :]).then_inc(S["stats_ok"], 1)
            dve.wait_ge(S["stats_ok"], k * 8 + 8)
            for t in range(k * 8, k * 8 + 8):
                last = nc.vector.bn_aggr(mv[:, t, :], stats[:, t, :])
            done(last)
            sl = slice(k * 8, k * 8 + 8)
            nc.vector.tensor_scalar(var[:, sl], mv[:, sl, 1], 1e-5, None, ALU.add).then_inc(S["var_ok"], 1)

        def refine(k):
            sl = slice(k * 8, k * 8 + 8)
            dve.wait_ge(S["std_ok"], k + 1)
            rsqrt_refined(nc, done, rstd[:, sl], tmp[:, sl], var[:, sl])

        dve.wait_ge(S["wa_ps"], 1)
        nc.vector.tensor_copy(wext[:, :, 0:S0], aux[0][:, 0:2 * S0].rearrange("p (c k) -> p c k", c=DC))
        nc.vector.tensor_copy(bext[:, 0:S0], aux[0][0:1, 2 * S0:3 * S0]).then_inc(S["wa_ok"], 1)
        statistics(0)
        dve.wait_ge(S["wa_ps"], 2)
        nc.vector.tensor_copy(bias[:, :], acc[0][0][:, 0:CW])
        for c in range(DC):
            last = nc.vector.scalar_tensor_tensor(out=wext[:, c, :], in0=acc[0][1][:, 0:CW], scalar=-1.0 / D, in1=wext[:, c, :], op0=ALU.mult, op1=ALU.add)
        done(last)
        dve.sem_inc(S["wa_ok"], 1)
        refine(0)

        CONV_T = 12

        def convert(par, n, k, count):
            dve.wait_ge(adj_in[k], count)
            settle(dve)
            nc.vector.tensor_scalar(mask_u8[par][:, bass.ds(2 * n, 2), :], stage[:, k, :, :], 0, MINUS_ONE, ALU.not_equal, ALU.mult).then_inc(S["conv_ok"], 1)

        for t in range(NT):
            dve.wait_ge(S["h_ps"], t + 1)
            nc.vector.scalar_tensor_tensor(out=hext[:, t, :], in0=h_ps_buf[t % 4][:, 0:CW], scalar=rstd[:, t:t + 1], in1=bias[:, :], op0=ALU.mult, op1=ALU.add).then_inc(S["h_ok"], 1)
            if t % 8 == 3 and t < NT - 8:
                statistics(t // 8 + 1)
            if t % 8 == 7 and t < NT - 1:
                refine(t // 8 + 1)
            if t >= CONV_T and t % 2:
                n = (t - CONV_T) // 2
                convert(0, n, n % 2, n // 2 * 16 + 16)
        dve.wait_ge(S["h_ok"], NT)
        dst = hext[:, :, H:2 * H]
        nc.vector.tensor_reduce(dmx[:, :], dst.rearrange("p t h -> p h t"), AX, ALU.max).then_inc(S["dmx_ok"], 1)
        nc.vector.tensor_scalar(dcol[:, :, 0, :], dst.rearrange("p t h -> p h t"), -1.0, None, ALU.mult)
        nc.vector.tensor_scalar(dcol[:, :, 1, :], dst.rearrange("p t h -> p h t"), STEP, None, ALU.mult).then_inc(S["d_ok"], 1)
        dve.wait_ge(S["d_ok"], 1)
        nc.vector.tensor_copy(d_cur[:, :, :, :], dcol[:, 0:2, :, :])
        dve.wait_ge(S["dmxa_ok"], 1)
        dmb = dmxa[:, :].rearrange("p (o h) -> p o h", o=1).broadcast_to([P, NT, H])
        done(nc.vector.tensor_tensor(fw[:, 0], dst, dmb, ALU.subtract))
        done(nc.vector.tensor_scalar(fw[:, 1], fw[:, 0], 0.2, None, ALU.mult))
        dve.sem_inc(S["fw_in"], 1)
        done(nc.vector.tensor_tensor(ab[:, 0], hext[:, :, 0:H], dmb, ALU.add))
        done(nc.vector.tensor_scalar(ab[:, 1], ab[:, 0], -0.8, 0.0, ALU.mult, ALU.min))
        done(nc.vector.tensor_scalar(ab[:, 0], ab[:, 0], 0.8, 0.0, ALU.mult, ALU.min))
        dve.sem_inc(S["fw_in"], 1)
        dve.wait_ge(S["fw_ok"], 2)
        done(nc.vector.tensor_scalar(fw[:, 1], fw[:, 1], -1.0, None, ALU.mult))
        dve.sem_inc(S["fw_ok"], 1)

        def v_low(h):
            v5 = v_cur[:, h, :, :].rearrange("p t (s l c) -> p t s l c", s=2, l=2)
            dve.wait_ge(S["vhi_ok"], h + 1)
            nc.vector.tensor_tensor(v5[:, :, :, 1, :], v32[h], v5[:, :, :, 0, :], ALU.subtract).then_inc(S["vb_ok"], 1)
            dve.wait_ge(S["vb_ok"], h + 1)
            dve.sem_inc(v_in[h], 32)

        for h in range(2):
            for s in range(2):
                f = fw[:, s, :, h:h + 1]
                nc.vector.tensor_tensor(v32[h][:, :, s, 0:HD], hp[:, :, h * HD:(h + 1) * HD], f.broadcast_to([P, NT, HD]), ALU.mult)
                last = nc.vector.tensor_copy(v32[h][:, :, s, HD:VC], f)
            last.then_inc(S["v32_ok"], 1)
            n = 10 + h
            convert(0, n, n % 2, n // 2 * 16 + 16)
            v_low(h)

        ms = m_ring.bitcast(U32)
        mk = [m.bitcast(U32) for m in mask]

        def evacuate(g, q):
            dve.wait_ge(S["pe_done"], g * NG + NG)
            if not (isinstance(g, int) and g == 0):
                dve.wait_ge(S["comb_free"], g)
            for k in range(3):
                t0, t1 = 3 * k, min(3 * k + 3, IT)
                last = nc.vector.tensor_copy(comb[:, q, t0:t1, :, :, :].rearrange("p t s l c -> p (t s l c)"), acc[q][k][:, 0:(t1 - t0) * VW])
            last.then_inc(S["comb_ok"], 1)

        def head(b, r, q, first=False):
            g = b * H + 2 * r + q
            par = b % 2
            dve.wait_ge(v_in[q], (b * (H // 2) + r) * 32 + 32)
            dve.wait_ge(sc_in[q], (b * (H // 2) + r) * 16 + 16)
            for n in range(NG):
                if first:
                    if n >= RING:
                        dve.wait_ge(S["pe_done"], n - RING + 1)
                    for m in ([], [12, 13], [14], [15], [], [], [], [])[n]:
                        convert(0, m, m % 2, m // 2 * 16 + 16)
                    dve.wait_ge(S["conv_ok"], (0, 12, 14, 15, 16, 16, 16, 16)[n] if n else 12)
                else:
                    dve.wait_ge(S["pe_done"], g * NG + n - RING + 1)
                settle(dve)
                for jj in range(ACT_T[n], GJ):
                    j = n * GJ + jj
                    nc.vector.tensor_scalar(m_ring[:, j % (RING * GJ), :], s_cur[:, q, :], d_cur[:, q, 0, j:j + 1], None, ALU.is_gt, saturate=False).then_inc(S["dve_t"], 1)
                dve.wait_ge(S["dve_t"], g * sum(DVE_T) + sum(DVE_T[:n + 1]))
                dve.wait_ge(S["act_t"], g * sum(ACT_T) + sum(ACT_T[:n + 1]))
                j0 = (n * GJ) % (RING * GJ)
                nc.vector.tensor_tensor(ms[:, j0:j0 + GJ, :], ms[:, j0:j0 + GJ, :], mk[par][:, n * GJ:(n + 1) * GJ, :], ALU.bitwise_and).then_inc(S["m_ready"], 1)
                if n == 1 and not first:
                    evacuate(g - 1, 1 - q)
                if n in (4, 6) and b < NB - 1:
                    k = (n - 4) // 2
                    convert(1 - par, (2 * r + q) * 2 + k, k, g * 16 + (NPAIR // 2) * 16 + 16)

        for b in range(NB):
            if b == 0:
                head(0, 0, 0, True)
                head(0, 0, 1)
            with dve.Fori(int(b == 0), H // 2) as r:
                head(b, r, 0)
                head(b, r, 1)
            dve.wait_ge(S["conv_ok"], NPAIR + min(b + 1, NB - 1) * NPAIR)
        evacuate(NB * H - 1, 1)

        dve.wait_ge(S["comb_free"], NB * H + 1)
        done(nc.vector.reciprocal(den[:, :, :], den[:, :, :]))
        for k in range(4):
            sl = slice(8 * k, 8 * k + 8)
            h4 = hp[:, sl, :].rearrange("p t (h c) -> p t h c", h=H)
            done(nc.vector.tensor_tensor(h4, h4, den[:, sl, :].rearrange("p t (h o) -> p t h o", o=1).broadcast_to([P, 8, H, HD]), ALU.mult))
            if k >= 2:
                dve.wait_ge(S["hp_ok"], k - 1)
            nc.vector.tensor_scalar(stage_f[k % 2], hp[:, sl, :], 0.0, None, ALU.min).then_inc(S["hm_in"], 1)
            dve.wait_ge(x2_in[k // 2], 16)
            done(nc.vector.scalar_tensor_tensor(out=hp[:, sl, :], in0=hp[:, sl, :], scalar=0.0, in1=x_sb[:, sl, :], op0=ALU.max, op1=ALU.add))
            dve.wait_ge(S["ach"], k + 1)
            nc.vector.scalar_tensor_tensor(out=hp[:, sl, :], in0=stage_f[k % 2], scalar=-1.0, in1=hp[:, sl, :], op0=ALU.add, op1=ALU.add).then_inc(S["hp_ok"], 1)


def ffn(nc, ctx, x2, w_route, b_route, b1_all, b2_all, w16_dram, xs_dram, ys_dram, out_dram):
    def sb(name, shape, dt=F32):
        return ctx.enter_context(nc.sbuf_tensor(name, shape, dt))

    def ps(name, shape, dt=F32):
        return ctx.enter_context(nc.psum_tensor(name, shape, dt))

    def sem(name):
        return ctx.enter_context(nc.semaphore(name))

    w_sb = sb("w_sb", [P, E + 1, EW], F16)
    w_flat = w_sb[:, :, :].rearrange("p e c -> p (e c)")
    b1_sb = sb("b1_sb", [P, (E + 1) * FC])
    b2_sb = sb("b2_sb", [P, E + 1, D])
    hf = sb("hf", [P, FC // 2, SLOT])
    hh = sb("hh", [P, 2, FC, SLOT], F16)
    xs = sb("xs", [P, SUB, 2, D], F16)
    xt = sb("xt", [P, 2, DC, SLOT], F16)
    y_sb = sb("y_sb", [P, SUB, D])
    pos_i = sb("pos_i", [P, 2, NT], I32)
    wts = sb("wts", [P, 2, NT])
    emap = sb("emap", [P, MOE_SLOTS], I32)

    xhl = w_sb[:, 6:8, :].rearrange("p e c -> p (e c)").rearrange("p (t l d) -> p t l d", l=2, d=D)
    used = [0]

    def temp(n, dt=F32):
        a = used[0]
        used[0] += 2 * n
        assert used[0] <= EW
        return w_sb[:, 5, a:a + 2 * n].bitcast(dt)

    def te(v):
        return v.rearrange("p (t e) -> p t e", e=E)

    logit, one0, one1, both, scan0, scan1 = [te(temp(NT * E)) for _ in range(6)]
    scr = temp(MOE_SLOTS * E)
    top, mark, gap = temp(NT), temp(NT), temp(NT)
    stats, mv = temp(NT * 6), temp(NT * 2)
    stats, mv = stats.rearrange("p (t k) -> p t k", k=6), mv.rearrange("p (t k) -> p t k", k=2)
    rstd, var, tmp = temp(NT), temp(NT), temp(NT)
    iota_i = temp(MOE_SLOTS, I32)
    iota_f, k256, desc, cnt, ends, ends2 = temp(MOE_SLOTS), temp(16), temp(E), temp(E), temp(E), temp(E)
    bg_sb, wgf = temp(E), temp(DC * E)
    posf = temp(NT)
    xnf = hh[:, :, :, :].rearrange("p l f n -> p (l f n)").bitcast(F32).rearrange("p (k t d) -> p k t d", k=2, d=D)
    xtt = [v[:, :, :, :].rearrange("p a b n -> p (a b n)").rearrange("p (u l c n) -> p u l c n", u=2, l=2, c=DC) for v in (xt, xs)]
    wg = temp(DC * E)[:, :].bitcast(F16).rearrange("p (l c e) -> p l c e", l=2, e=E)
    ident16 = sb("ident16", [P, P], F16)
    tri = hf[:, 0, 0:P]
    ones = hf[:, 1, 0:P]

    ps_t = [ps(f"ps_t{k}", [P, 1024], F16) for k in range(2)]
    ps_h = [ps(f"ps_h{k}", [P, BANK]) for k in range(4)]
    ps_y = ps("ps_y", [P, BANK])
    ps_g = ps("ps_g", [P, BANK])

    names = """cst_in w_in w_late z_cst cst vch2 f_stats f_var f_std xn_ok2 xhi_ok xlo_ok tr_ps tr_ok g_ps g_ok gap_ok ex_ok
        both_ok rank_ps pos_ok xs_out sc_done xs_in t_done xt_ok2 h_ps2 relu_ok hi_ok conv y_ps y_ok y_out
        b2_ok fin_ok fin_out settled2""".split()
    S = {n: sem(n) for n in names}
    g_in = [sem(f"g_in{k}") for k in range(2)]

    def settle(eng):
        eng.sem_inc(S["settled2"], 1)

    def w_at(e, o, n):
        return w_flat[:, bass.ds(e * EW + o, n)] if not isinstance(e, int) else w_sb[:, e, o:o + n]

    def w1_at(e, c, l, f):
        return w_at(e, c * 2048 + l * 1024 + f * P, P)

    def w2_at(e, f, l):
        return w_at(e, (2 + f // 4) * 2048 + l * 1024 + (f % 4) * D, D)

    gbuf = w_sb[:, 0, :].bitcast(F32).rearrange("p (i j k d) -> p i j k d", i=2, j=4, d=D)

    def group(i):
        return [SUB * i + u for u in range(SUB)] + [NT // 2 + SUB * i + u for u in range(SUB)]

    block = ctx.enter_context(nc.Block())

    @block.sync
    def _(sp):
        sp.dma_start(wgf, w_route.rearrange("(c p) e -> p c e", p=P)).then_inc(S["cst_in"], 16)
        sp.dma_start(bg_sb, b_route.rearrange("(a e) -> a e", a=1).broadcast_to([P, E])).then_inc(S["cst_in"], 16)
        sp.dma_start(b1_sb[:, :], b1_all.rearrange("(g p) -> p g", p=P)).then_inc(S["cst_in"], 16)
        sp.dma_start(b2_sb[:, :, :], b2_all.rearrange("(a e) d -> a e d", a=1).broadcast_to([P, E + 1, D])).then_inc(S["cst_in"], 16)
        for e in [E] + list(range(5)):
            sp.dma_start(w_sb[:, e, :].rearrange("p (u c) -> p u c", u=4), w16_dram[4 * e:4 * e + 4].rearrange("u p l c -> p u (l c)")).then_inc(S["w_in"], 16)
        for k in range(4):
            sp.wait_ge(S["xlo_ok"], 2 * k + 2)
            row = MOE_SLOTS * SLOT + k * 8 * P
            sp.dma_start(xs_dram[row:row + 8 * P, :].rearrange("(t p) c -> p t c", p=P), xhl[:, 8 * k:8 * k + 8, :, :].rearrange("p t l d -> p t (l d)")).then_inc(S["xs_out"], 16)
        sp.wait_ge(S["xs_out"], 64)

        def load_slot(row):
            src = xs_dram[bass.ds(row * SLOT, SLOT), :].rearrange("(u p) c -> p u c", p=P)
            sp.dma_start(xs[:, :, :, :].rearrange("p u l d -> p u (l d)"), src).then_inc(S["xs_in"], 16)

        def store_slot(s):
            sp.wait_ge(S["y_ok"], s + 1)
            sp.dma_start(ys_dram[bass.ds((s - SH_A) * SLOT, SLOT), :].rearrange("(u p) d -> p u d", p=P), y_sb[:, :, :]).then_inc(S["y_out"], 16)

        sp.wait_ge(S["g_ps"], NT // 2)
        load_slot(MOE_SLOTS)
        with sp.Fori(0, SH_A - 1) as s:
            sp.wait_ge(S["t_done"], s + 1)
            load_slot(MOE_SLOTS + s + 1)
        sp.wait_ge(S["sc_done"], 16 * 2 * NT)
        sp.wait_ge(S["t_done"], SH_A)
        load_slot(0)
        for e in range(5, E):
            sp.dma_start(w_sb[:, e, :].rearrange("p (u c) -> p u c", u=4), w16_dram[4 * e:4 * e + 4].rearrange("u p l c -> p u (l c)")).then_inc(S["w_late"], 16)
        with sp.Fori(SH_A, SH_B - 1) as s:
            sp.wait_ge(S["t_done"], s + 1)
            load_slot(s - SH_A + 1)
            store_slot(s)
        sp.wait_ge(S["t_done"], SH_B)
        load_slot(SH_B)
        store_slot(SH_B - 1)
        with sp.Fori(SH_B, SLOTS - 1) as s:
            sp.wait_ge(S["t_done"], s + 1)
            load_slot(s + 1)
        for i in range(SH_A):
            sp.wait_ge(S["fin_ok"], i + 1)
            for t in (group(i)[0], group(i)[SUB]):
                sp.dma_start(out_dram[t * P:(t + SUB) * P, :].rearrange("(u p) d -> p u d", p=P), x2[:, t:t + SUB, :]).then_inc(S["fin_out"], 16)
        sp.wait_ge(S["fin_out"], 16 * 2 * SH_A)

    @block.gpsimd
    def _(pool):
        nc.gpsimd.memset(tri, 1.0).then_inc(S["z_cst"], 1)
        nc.gpsimd.memset(ones, 1.0).then_inc(S["z_cst"], 1)
        nc.gpsimd.memset(ident16[:, :], 0.0).then_inc(S["z_cst"], 1)
        pool.wait_ge(S["z_cst"], 3)
        nc.gpsimd.affine_select(out=tri, in_=tri, compare_op=ALU.is_gt, fill=0.0, base=0, pattern=[[1, P]], channel_multiplier=-1).then_inc(S["cst"], 1)
        nc.gpsimd.affine_select(out=ident16[:, :], in_=ident16[:, :], compare_op=ALU.not_equal, fill=1.0, base=0, pattern=[[-1, P]], channel_multiplier=1).then_inc(S["cst"], 1)
        nc.gpsimd.iota(iota_i, pattern=[[1, MOE_SLOTS]], base=0, channel_multiplier=0).then_inc(S["cst"], 1)
        pool.wait_ge(S["pos_ok"], 1)
        for t in range(NT):
            for k in range(2):
                nc.gpsimd.indirect_dma_start(out=xs_dram, out_offset=bass.IndirectOffsetOnAxis(ap=pos_i[:, k, t:t + 1], axis=0),
                                             in_=xhl[:, t, :, :].rearrange("p l d -> p (l d)"), in_offset=None).then_inc(S["sc_done"], 16)
        pool.wait_ge(S["y_out"], 16 * MOE_SLOTS)
        for i in range(SH_A):
            if i >= 2:
                pool.wait_ge(S["fin_ok"], i - 1)
            for j, t in enumerate(group(i)):
                for k in range(2):
                    nc.gpsimd.indirect_dma_start(out=gbuf[:, i % 2, j, k, :], out_offset=None, in_=ys_dram,
                                                 in_offset=bass.IndirectOffsetOnAxis(ap=pos_i[:, k, t:t + 1], axis=0)).then_inc(g_in[i % 2], 16)

    @block.tensor
    def _(pe):
        pe.wait_ge(S["cst"], 3)
        pe.wait_ge(S["vch2"], 3)
        def route(k):
            pe.wait_ge(S["tr_ok"], k + 1)
            for t in range(2 * k, 2 * k + 2):
                n = 0
                for lx, lw in ((0, 0), (1, 0), (0, 1)):
                    for c in range(DC):
                        last = nc.tensor.matmul(ps_g[:, t * E:(t + 1) * E], xtt[k % 2][:, t % 2, lx, c, :], wg[:, lw, c, :], start=(t == 0 and n == 0), stop=(n == 5), skip_group_check=True)
                        n += 1
            last.then_inc(S["g_ps"], 1)

        for k in range(NT // 2):
            pe.wait_ge(S["xlo_ok"], k // 2 + 1)
            if k >= 2:
                pe.wait_ge(S["tr_ok"], k - 1)
            for u in range(2):
                for l in range(2):
                    for c in range(DC):
                        o = ((u * 2 + l) * DC + c) * P
                        last = nc.tensor.transpose(ps_t[k % 2][:, o:o + P], xhl[:, 2 * k + u, l, c * P:(c + 1) * P], ident16[:, :])
            last.then_inc(S["tr_ps"], 1)
            if k:
                route(k - 1)
        route(NT // 2 - 1)
        pe.wait_ge(S["both_ok"], 1)
        a = both.rearrange("p t e -> p (t e)")
        nc.tensor.matmul(ps_g[:, 0:NT * E], tri, a, start=True, stop=True)
        nc.tensor.matmul(ps_g[:, NT * E:2 * NT * E], ones, a, start=False, stop=True, skip_group_check=True).then_inc(S["rank_ps"], 1)

        def transposes(s):
            pe.wait_ge(S["xs_in"], s * 16 + 16)
            for l in range(2):
                for c in range(DC):
                    for u in range(SUB):
                        o = (l * DC + c) * SLOT + u * P
                        last = nc.tensor.transpose(ps_t[0][:, o:o + P], xs[:, u, l, c * P:(c + 1) * P], ident16[:, :])
            last.then_inc(S["t_done"], 1)

        def slot(s, e, more):
            pe.wait_ge(S["xt_ok2"], s + 1)
            for f in range(FC):
                n = 0
                for lw, lx in ((0, 0), (0, 1), (1, 0)):
                    for c in range(DC):
                        last = nc.tensor.matmul(ps_h[f // 2][:, (f % 2) * SLOT:(f % 2 + 1) * SLOT], w1_at(e, c, lw, f), xt[:, lx, c, :],
                                                start=(f % 2 == 0 and n == 0), stop=(n == 5), skip_group_check=True)
                        n += 1
                if f % 2:
                    last.then_inc(S["h_ps2"], 1)
            if more:
                transposes(s + 1)
            if not (isinstance(s, int) and s == 0):
                pe.wait_ge(S["y_ok"], s)
            for f in range(FC):
                if f % 2 == 0:
                    pe.wait_ge(S["conv"], s * 4 + f // 2 + 1)
                for u in range(SUB):
                    for lw, lh in ((0, 0), (0, 1), (1, 0)):
                        first = f == 0 and u == 0 and lw == 0 and lh == 0
                        last = nc.tensor.matmul(ps_y[:, u * D:(u + 1) * D], hh[:, lh, f, u * P:(u + 1) * P], w2_at(e, f, lw),
                                                start=first, stop=(f == FC - 1 and lw == 1), skip_group_check=True)
            last.then_inc(S["y_ps"], 1)

        pe.wait_ge(S["pos_ok"], 1)
        pe.wait_ge(S["w_in"], 16 * 6)
        transposes(0)
        slot(0, E, True)
        with pe.Fori(1, SH_A) as s:
            slot(s, E, True)
        pe.wait_ge(S["w_late"], 16 * 3)
        with pe.Fori(SH_A, SH_B) as s:
            e = pe.value_load(emap[0:1, bass.ds(s - SH_A, 1)], min_val=0, max_val=E - 1)
            slot(s, e, True)
        with pe.Fori(SH_B, SLOTS - 1) as s:
            slot(s, E, True)
        slot(SLOTS - 1, E, False)

    @block.scalar
    def _(act):
        def copy_pair(k):
            act.wait_ge(S["tr_ps"], k + 1)
            if k >= 2:
                act.wait_ge(S["g_ps"], k - 1)
            nc.scalar.activation(xtt[k % 2].rearrange("p u l c n -> p (u l c n)"), ps_t[k % 2][:, :], ACT.Copy).then_inc(S["tr_ok"], 1)

        def root(k):
            act.wait_ge(S["f_var"], k + 1)
            nc.scalar.activation(rstd[:, 8 * k:8 * k + 8], var[:, 8 * k:8 * k + 8], ACT.Sqrt).then_inc(S["f_std"], 1)

        root(0)
        for m in range(NT // 4):
            if m % 2 == 0 and m // 2 < 3:
                root(m // 2 + 1)
            act.wait_ge(S["xn_ok2"], m + 1)
            nc.scalar.activation(xhl[:, 4 * m:4 * m + 4, 0, :], xnf[:, m % 2, :, :], ACT.Copy).then_inc(S["xhi_ok"], 1)
            if m:
                copy_pair(2 * m - 2)
                copy_pair(2 * m - 1)
        copy_pair(NT // 2 - 2)
        copy_pair(NT // 2 - 1)
        act.wait_ge(S["gap_ok"], 1)
        nc.scalar.activation(gap, gap, ACT.Exp).then_inc(S["ex_ok"], 1)

        def copy_t(s):
            act.wait_ge(S["t_done"], s + 1)
            nc.scalar.activation(xt[:, :, :, :].rearrange("p l c n -> p (l c n)"), ps_t[0][:, :], ACT.Copy).then_inc(S["xt_ok2"], 1)

        def slot(s, e, more, first=False):
            for f in range(FC):
                if f % 2 == 0:
                    if not (first and f < 4):
                        act.wait_ge(S["conv"], s * 4 + f // 2 - 1)
                    act.wait_ge(S["h_ps2"], s * 4 + f // 2 + 1)
                    settle(act)
                o = e * FC + f
                bias = b1_sb[:, o:o + 1] if isinstance(o, int) else b1_sb[:, bass.ds(o, 1)]
                nc.scalar.activation(hf[:, f % 4, :], ps_h[f // 2][:, (f % 2) * SLOT:(f % 2 + 1) * SLOT], ACT.Relu, bias=bias, scale=XS / (XS * WS)).then_inc(S["relu_ok"], 1)
            if more:
                copy_t(s + 1)

        act.wait_ge(S["g_ps"], NT // 2)
        copy_t(0)
        act.wait_ge(S["rank_ps"], 1)
        slot(0, E, True, True)
        with act.Fori(1, SH_A) as s:
            slot(s, E, True)
        with act.Fori(SH_A, SH_B) as s:
            slot(s, act.value_load(emap[0:1, bass.ds(s - SH_A, 1)], min_val=0, max_val=E - 1), True)
        with act.Fori(SH_B, SLOTS - 1) as s:
            slot(s, E, True)
        slot(SLOTS - 1, E, False)

    @block.vector
    def _(dve):
        nd = [0]

        def done(ins):
            nd[0] += 1
            ins.then_inc(S["vch2"], 1)
            dve.wait_ge(S["vch2"], nd[0])

        dve.wait_ge(S["cst_in"], 64)
        wgv = wgf.rearrange("p (c e) -> p c e", e=E)
        done(nc.vector.tensor_scalar(wgf, wgf, WS, None, ALU.mult))
        done(nc.vector.tensor_copy(wg[:, 0], wgv))
        done(nc.vector.tensor_tensor(wg[:, 1], wgv, wg[:, 0], ALU.subtract))
        done(nc.vector.tensor_scalar(b1_sb[:, :], b1_sb[:, :], XS, None, ALU.mult))
        done(nc.vector.tensor_scalar(b2_sb[:, E, :], b2_sb[:, E, :], 1.0 / K, None, ALU.mult))

        def low(m):
            dve.wait_ge(S["xhi_ok"], m + 1)
            nc.vector.tensor_tensor(xhl[:, 4 * m:4 * m + 4, 1, :], xnf[:, m % 2, :, :], xhl[:, 4 * m:4 * m + 4, 0, :], ALU.subtract).then_inc(S["xlo_ok"], 1)

        def normalise(k):
            sl = slice(8 * k, 8 * k + 8)
            dve.wait_ge(S["f_std"], k + 1)
            rsqrt_refined(nc, done, rstd[:, sl], tmp[:, sl], var[:, sl])
            done(nc.vector.tensor_scalar(rstd[:, sl], rstd[:, sl], XS, None, ALU.mult))
            for m in range(2 * k, 2 * k + 2):
                if m >= 2:
                    dve.wait_ge(S["xlo_ok"], m - 1)
                for t in range(4 * m, 4 * m + 4):
                    last = nc.vector.tensor_scalar(xnf[:, m % 2, t % 4, :], x2[:, t, :], mv[:, t, 0:1], rstd[:, t:t + 1], ALU.subtract, ALU.mult)
                last.then_inc(S["xn_ok2"], 1)
                if m:
                    low(m - 1)

        for k in range(4):
            sl = slice(8 * k, 8 * k + 8)
            for t in range(8 * k, 8 * k + 8):
                nc.vector.bn_stats(stats[:, t, :], x2[:, t, :]).then_inc(S["f_stats"], 1)
            dve.wait_ge(S["f_stats"], 8 * k + 8)
            for t in range(8 * k, 8 * k + 8):
                last = nc.vector.bn_aggr(mv[:, t, :], stats[:, t, :])
            done(last)
            nc.vector.tensor_scalar(var[:, sl], mv[:, sl, 1], 1e-5, None, ALU.add).then_inc(S["f_var"], 1)
            if k:
                normalise(k - 1)
        normalise(3)
        low(NT // 4 - 1)
        dve.wait_ge(S["cst"], 3)
        done(nc.vector.tensor_copy(iota_f, iota_i))
        done(nc.vector.tensor_scalar(k256, iota_f[:, 0:16], float(SLOT), None, ALU.mult))
        done(nc.vector.tensor_scalar(desc, iota_f[:, 0:E], -1.0, float(E), ALU.mult, ALU.add))
        dve.wait_ge(S["g_ps"], NT // 2)

        def per_t(v):
            return v.rearrange("p (t o) -> p t o", o=1).broadcast_to([P, NT, E])

        def per_e(v, n=NT):
            return v.rearrange("p (o e) -> p o e", o=1).broadcast_to([P, n, E])

        scr_te = te(scr[:, 0:NT * E])
        done(nc.vector.scalar_tensor_tensor(out=logit, in0=ps_g[:, 0:NT * E].rearrange("p (t e) -> p t e", e=E), scalar=1.0 / (XS * WS), in1=per_e(bg_sb), op0=ALU.mult, op1=ALU.add))

        def first_best(one, best):
            done(nc.vector.tensor_reduce(best, logit, AX, ALU.max))
            done(nc.vector.tensor_tensor(scr_te, logit, per_t(best), ALU.is_equal))
            done(nc.vector.tensor_tensor(scr_te, scr_te, per_e(desc), ALU.mult))
            done(nc.vector.tensor_reduce(mark, scr_te, AX, ALU.max))
            done(nc.vector.tensor_tensor(one, scr_te, per_t(mark), ALU.is_equal))

        first_best(one0, top)
        done(nc.vector.scalar_tensor_tensor(out=logit, in0=one0, scalar=-1e30, in1=logit, op0=ALU.mult, op1=ALU.add))
        first_best(one1, gap)
        done(nc.vector.tensor_tensor(gap, gap, top, ALU.subtract))
        dve.sem_inc(S["gap_ok"], 1)
        nc.vector.tensor_tensor(both, one0, one1, ALU.add).then_inc(S["both_ok"], 1)
        dve.wait_ge(S["ex_ok"], 1)
        done(nc.vector.tensor_scalar(wts[:, 0, :], gap, 1.0, None, ALU.add))
        done(nc.vector.reciprocal(wts[:, 0, :], wts[:, 0, :]))
        done(nc.vector.tensor_tensor(wts[:, 1, :], gap, wts[:, 0, :], ALU.mult))
        dve.wait_ge(S["rank_ps"], 1)
        tot = ps_g[:, NT * E:2 * NT * E].rearrange("p (t e) -> p t e", e=E)
        done(nc.vector.tensor_copy(scan0, tot))
        a, b = scan0, scan1
        d = 1
        while d < NT:
            done(nc.vector.tensor_copy(b[:, 0:d, :], a[:, 0:d, :]))
            done(nc.vector.tensor_tensor(b[:, d:NT, :], a[:, d:NT, :], a[:, 0:NT - d, :], ALU.add))
            a, b = b, a
            d *= 2
        sc16 = scr[:, 0:E * 16].rearrange("p (e k) -> p e k", k=16)
        done(nc.vector.tensor_tensor(sc16, a[:, NT - 1, :].rearrange("p (e o) -> p e o", o=1).broadcast_to([P, E, 16]),
                                     k256.rearrange("p (o k) -> p o k", o=1).broadcast_to([P, E, 16]), ALU.is_gt))
        done(nc.vector.tensor_reduce(cnt, sc16, AX, ALU.add))
        done(nc.vector.tensor_copy(ends, cnt))
        c0, c1 = ends, ends2
        d = 1
        while d < E:
            done(nc.vector.tensor_copy(c1[:, 0:d], c0[:, 0:d]))
            done(nc.vector.tensor_tensor(c1[:, d:E], c0[:, d:E], c0[:, 0:E - d], ALU.add))
            c0, c1 = c1, c0
            d *= 2
        sce = scr[:, 0:MOE_SLOTS * E].rearrange("p (s e) -> p s e", e=E)
        done(nc.vector.tensor_tensor(sce, per_e(c0, MOE_SLOTS), iota_f.rearrange("p (s o) -> p s o", o=1).broadcast_to([P, MOE_SLOTS, E]), ALU.is_le))
        done(nc.vector.tensor_reduce(iota_f, sce, AX, ALU.add))
        done(nc.vector.tensor_scalar(emap[:, :], iota_f, float(E - 1), None, ALU.min))
        done(nc.vector.tensor_tensor(c1, c0, cnt, ALU.subtract))
        done(nc.vector.tensor_scalar(c1, c1, float(SLOT), None, ALU.mult))
        done(nc.vector.tensor_tensor(a, a, tot, ALU.subtract))
        done(nc.vector.tensor_tensor(a, a, ps_g[:, 0:NT * E].rearrange("p (t e) -> p t e", e=E), ALU.add))
        done(nc.vector.tensor_tensor(a, a, per_e(c1), ALU.add))
        for k, one in enumerate((one0, one1)):
            done(nc.vector.tensor_tensor(scr_te, one, a, ALU.mult))
            done(nc.vector.tensor_reduce(posf, scr_te, AX, ALU.add))
            done(nc.vector.tensor_copy(pos_i[:, k, :], posf))
        dve.sem_inc(S["pos_ok"], 1)

        def split_hidden(s):
            for k in range(4):
                dve.wait_ge(S["relu_ok"], s * FC + 2 * k + 2)
                nc.vector.tensor_copy(hh[:, 0, 2 * k:2 * k + 2, :], hf[:, 2 * k % 4:2 * k % 4 + 2, :]).then_inc(S["hi_ok"], 1)
                dve.wait_ge(S["hi_ok"], s * 4 + k + 1)
                nc.vector.tensor_tensor(hh[:, 1, 2 * k:2 * k + 2, :], hf[:, 2 * k % 4:2 * k % 4 + 2, :], hh[:, 0, 2 * k:2 * k + 2, :], ALU.subtract).then_inc(S["conv"], 1)

        def shared_slot(s, t, n):
            split_hidden(s)
            for u in range(SUB):
                xt2 = x2[:, bass.ds(t + u, 1), :].rearrange("p o d -> p (o d)")
                last = nc.vector.tensor_tensor(xt2, xt2, b2_sb[:, E, :], ALU.add)
            last.then_inc(S["b2_ok"], 1)
            dve.wait_ge(S["b2_ok"], n + 1)
            dve.wait_ge(S["y_ps"], s + 1)
            for u in range(SUB):
                xt2 = x2[:, bass.ds(t + u, 1), :].rearrange("p o d -> p (o d)")
                last = nc.vector.scalar_tensor_tensor(out=xt2, in0=ps_y[:, u * D:(u + 1) * D], scalar=1.0 / (K * XS * WS), in1=xt2, op0=ALU.mult, op1=ALU.add)
            last.then_inc(S["y_ok"], 1)

        def routed_slot(s, e, first):
            split_hidden(s)
            if not first:
                dve.wait_ge(S["y_out"], (s - SH_A) * 16)
            dve.wait_ge(S["y_ps"], s + 1)
            settle(dve)
            for u in range(SUB):
                b2 = b2_sb[:, :, :].rearrange("p e d -> p (e d)")[:, bass.ds(e * D, D)]
                last = nc.vector.scalar_tensor_tensor(out=y_sb[:, u, :], in0=ps_y[:, u * D:(u + 1) * D], scalar=1.0 / (XS * WS), in1=b2, op0=ALU.mult, op1=ALU.add)
            last.then_inc(S["y_ok"], 1)

        def expert_of(m):
            return dve.value_load(emap[0:1, bass.ds(m, 1)], min_val=0, max_val=E - 1)

        with dve.Fori(0, SH_A) as s:
            shared_slot(s, s * SUB, s)
        routed_slot(SH_A, expert_of(0), True)
        with dve.Fori(SH_A + 1, SH_B) as s:
            routed_slot(s, expert_of(s - SH_A), False)

        def add_experts(i):
            dve.wait_ge(g_in[i % 2], 16 * 8 * (i // 2 + 1))
            dve.wait_ge(S["y_ok"], SH_B + i + 1)
            for k in range(2):
                for j, t in enumerate(group(i)):
                    last = nc.vector.scalar_tensor_tensor(out=x2[:, t, :], in0=gbuf[:, i % 2, j, k, :], scalar=wts[:, k, t:t + 1], in1=x2[:, t, :], op0=ALU.mult, op1=ALU.add)
                if k == 0:
                    done(last)
            last.then_inc(S["fin_ok"], 1)

        for i in range(SH_A):
            shared_slot(SH_B + i, NT // 2 + i * SUB, SH_A + i)
            if i:
                add_experts(i - 1)
        add_experts(SH_A - 1)


def gat_moe_kernel(nc, x, x_t, adj_t, w_t, w_n, b_w, a, w_route, b_route, w_all, b1_all, b2_all, out):
    s_dram = nc.dram_tensor("s_dram", (H, N), F32, kind="Internal").ap()
    v_dram = nc.dram_tensor("v_dram", (H, P, NT * VW), F16, kind="Internal").ap()
    d_dram = nc.dram_tensor("d_dram", (H, P, 2 * NT), F32, kind="Internal").ap()
    w16_dram = nc.dram_tensor("w16_dram", (UNITS, P, 2, F), F16, kind="Internal").ap()
    xs_dram = nc.dram_tensor("xs_dram", (N_ROWS, 2 * D), F16, kind="Internal").ap()
    ys_dram = nc.dram_tensor("ys_dram", (MOE_SLOTS * SLOT, D), F32, kind="Internal").ap()
    with ExitStack() as outer:
        outer.enter_context(nc.allow_non_contiguous_dma(reason="biases and a few vectors of a hundred elements"))
        hext = outer.enter_context(nc.sbuf_tensor("hext", [P, NT, CW], F32))
        with ExitStack() as ctx:
            gat(nc, ctx, hext, x, x_t, adj_t, w_t, w_n, b_w, a, w_all, s_dram, v_dram, d_dram, w16_dram, xs_dram)
        with ExitStack() as ctx:
            ffn(nc, ctx, hext[:, :, S0:CW], w_route, b_route, b1_all, b2_all, w16_dram, xs_dram, ys_dram, out)


def kernel(x, adj, L0_gnn_W_w, L0_gnn_W_b, L0_gnn_a, L0_ffn_Wg, L0_ffn_bg, L0_ffn_W1, L0_ffn_b1, L0_ffn_W2, L0_ffn_b2,
           L0_ffn_Ws1, L0_ffn_bs1, L0_ffn_Ws2, L0_ffn_bs2):
    import numpy as np
    import concourse.bacc as bacc
    from concourse.bass_utils import run_bass_kernel_spmd

    def arr(v):
        return np.asarray(v)

    w1 = np.concatenate([arr(L0_ffn_W1), arr(L0_ffn_Ws1)[None]]).reshape(E + 1, DC, P, F)
    w2 = np.concatenate([arr(L0_ffn_W2), arr(L0_ffn_Ws2)[None]]).reshape(E + 1, 2, 4, P, D).transpose(0, 1, 3, 2, 4).reshape(E + 1, 2, P, F)
    arrays = {
        "x": arr(x), "x_t": arr(x).T.reshape(DC, P, N),
        "adj_t": arr(adj).T.reshape(NT, P, NB, BI).transpose(2, 0, 1, 3),
        "w_t": arr(L0_gnn_W_w).T, "w_n": arr(L0_gnn_W_w), "b_w": arr(L0_gnn_W_b), "a": np.tile(arr(L0_gnn_a).reshape(2, HD).T, (P // HD, 1)),
        "w_route": arr(L0_ffn_Wg), "b_route": arr(L0_ffn_bg),
        "w_all": np.concatenate([w1, w2], axis=1).reshape(UNITS, P, F),
        "b1_all": np.concatenate([arr(L0_ffn_b1).reshape(-1), arr(L0_ffn_bs1)]),
        "b2_all": np.concatenate([arr(L0_ffn_b2), arr(L0_ffn_bs2)[None]]),
    }
    arrays = {k: np.ascontiguousarray(v) for k, v in arrays.items()}
    nc = bacc.Bacc("TRN2", target_bir_lowering=False, num_devices=1)
    args = {k: nc.dram_tensor(k, v.shape, mybir.dt.from_np(v.dtype), kind="ExternalInput").ap() for k, v in arrays.items()}
    out = nc.dram_tensor("out", (N, D), F32, kind="ExternalOutput").ap()
    gat_moe_kernel(nc, **args, out=out)
    r = run_bass_kernel_spmd(nc, [arrays], core_ids=[0])
    return r.results[0]["out"]
```

```python
from contextlib import ExitStack
import math

import concourse.bass as bass
from concourse import mybir

F32 = mybir.dt.float32
F16 = mybir.dt.float16
F8 = mybir.dt.float8e4
I32 = mybir.dt.int32
U32 = mybir.dt.uint32
ALU = mybir.AluOpType
ACT = mybir.ActivationFunctionType
AX = mybir.AxisListType.X
RMAX = bass.bass_isa.ReduceOp.max

P = 128
N = 4096
D = 256
H = 8
HD = D // H
DC = D // P
NT = N // P
BI = 1024
NB = N // BI
IT = BI // P
VC = HD + 1
VW = 4 * VC
S0 = 2 * H
CW = S0 + D
NPAIR = NT // 2
MINUS_ONE = 0xB8
GJ = 4
NG = NT // GJ
ACT_T = [2, 2, 3, 2, 2, 3, 2, 3]
DVE_T = [GJ - n for n in ACT_T]
RING = 4
STAGE = 2
VSCALE = 256.0
STEP = 2.0 ** 40
BANK = 512
E = 8
K = 2
F = 1024
FC = F // P
EW = 8 * F
UNITS = 4 * (E + 1)
SLOT = 256
SUB = SLOT // P
SH_SLOTS = N // SLOT
SH_A = SH_SLOTS * 5 // 8
MOE_SLOTS = (K * N - E) // SLOT + E
SLOTS = SH_SLOTS + MOE_SLOTS
SH_B = SH_A + MOE_SLOTS
N_ROWS = SLOTS * SLOT
XS = 16.0
WS = 256.0


def rsqrt_refined(nc, done, y, t, v):
    done(nc.vector.reciprocal(y, y))
    done(nc.vector.tensor_tensor(t, y, y, ALU.mult))
    done(nc.vector.tensor_tensor(t, t, v, ALU.mult))
    done(nc.vector.tensor_scalar(t, t, -0.5, 1.5, ALU.mult, ALU.add))
    done(nc.vector.tensor_tensor(y, y, t, ALU.mult))


def gat(nc, ctx, hext, mv2, x, x_t, adj_t, w_t, w_n, b_w, a, w_all, s_dram, v_dram, d_dram, w16_dram, xs_dram):
    def sb(name, shape, dt=F32):
        return ctx.enter_context(nc.sbuf_tensor(name, shape, dt))

    def ps(name, shape):
        return ctx.enter_context(nc.psum_tensor(name, shape, F32))

    def sem(name):
        return ctx.enter_context(nc.semaphore(name))

    wext = sb("wext", [P, DC, CW])
    wn_sb = sb("wn_sb", [P, DC, D])
    acol = sb("acol", [P, 2])
    ablk = sb("ablk", [P, DC, S0])
    bcol = sb("bcol", [P, DC])
    bext = sb("bext", [1, CW])
    bias = sb("bias", [P, CW])
    ones = sb("ones", [P, P])
    ident = sb("ident", [P, P])
    stats = sb("stats", [P, NT, 6])
    mv = sb("mv", [P, NT, 2])
    rstd = sb("rstd", [P, NT])
    var = sb("var", [P, NT])
    tmp = sb("tmp", [P, NT])
    st_sb = sb("st_sb", [H, 2, 4 * P])
    hmean = sb("hmean", [P, D])
    dmx = sb("dmx", [P, H])
    dmxa = sb("dmxa", [P, H])
    dcol = sb("dcol", [P, H, 2, NT])
    fw = sb("fw", [P, 2, NT, H])
    ab = sb("ab", [P, 2, NT, H])
    lnc = sb("lnc", [P, 1])
    ws_col = sb("ws_col", [P, 1])
    stage = sb("stage", [P, STAGE, 2, BI], I32)
    x_sb = sb("x_sb", [P, NT, D])
    masks = sb("masks", [P, NT + RING * GJ, BI], F8)
    mask = [x_sb[:, :, :].rearrange("p t d -> p (t d)").bitcast(F8).rearrange("p (t i) -> p t i", i=BI), masks[:, 0:NT, :]]
    mask_u8 = [m.bitcast(mybir.dt.uint8) for m in mask]
    m_ring = masks[:, NT:NT + RING * GJ, :]
    flat = masks[:, :, :].rearrange("p a b -> p (a b)")
    xt_sb = flat[:, 0:NT * BI].bitcast(F32).rearrange("p (c n) -> p c n", c=DC)
    VB = NT * 2 * VC * 4
    v32 = [flat[:, o:o + VB].bitcast(F32).rearrange("p (t s c) -> p t s c", s=2, c=VC) for o in (0, 0)]
    v_cur = sb("v_cur", [P, 2, NT, VW], F16)
    d_cur = sb("d_cur", [P, 2, 2, NT])
    s_cur = sb("s_cur", [P, 2, BI])
    comb = sb("comb", [P, 2, IT, 2, 2, VC])
    hp = hext[:, :, S0:CW]
    pw = sb("pw", [P, 2, IT, VC])
    den = sb("den", [P, NT, H])
    flag = sb("flag", [P, IT])
    fl = sb("fl", [P, IT, HD])
    HV = NT // 2 * 2 * VC
    wbuf = sb("wbuf", [P, 4 * F])
    wf = [wbuf[:, 2 * k * F:(2 * k + 1) * F] for k in range(2)]
    w16 = [wbuf[:, (2 * k + 1) * F:(2 * k + 2) * F].bitcast(F16).rearrange("p (l c) -> p l c", l=2) for k in range(2)]
    zeros = sb("zeros", [P, 2 * D], F16)
    pv32 = wbuf[:, 0:HV].rearrange("p (t s c) -> p t s c", s=2, c=VC)
    pvb = [wbuf[:, (1 + k) * HV:(2 + k) * HV].bitcast(F16) for k in range(2)]
    pvb5 = [v.rearrange("p (t s l c) -> p t s l c", s=2, l=2, c=VC) for v in pvb]

    acc = [[ps(f"acc{q}{k}", [P, BANK]) for k in range(3)] for q in range(2)]
    aux = [ps(f"aux{k}", [P, BANK]) for k in range(2)]
    h_ps_buf = [acc[q][k] for q in range(2) for k in range(3)]

    Z_STEPS = 26
    Z_ROWS = MOE_SLOTS * SLOT // Z_STEPS

    den_flat = den[:, :, :].rearrange("p t h -> p (t h)")
    xr = wn_sb[:, :, :]
    rr = wext[:, :, :].rearrange("p c n -> p (c n)")[:, 0:2 * D].rearrange("p (t d) -> p t d", d=D)
    ee = sb("ee", [P, 2, D])
    st2 = sb("st2", [P, 2, 6])
    mvt = sb("mvt", [P, 2, 2])
    NPOST = (NB - 1) * IT // 2

    names = """w_in a_in ident_ok stats_ok var_ok std_ok h_ps h_ok sT_ps sT_ok wa_ps wa_ok dmx_ok dmxa_ok fw_in
        fw_ok ab_ok dcur_ok v32_ok vhi_ok vb_ok v_st pvch d_ok d_out hs_ok hm_ps hm_ok dch pch ach conv_ok dve_t act_t m_ready pe_done
        comb_ok comb_free hp_ok hm_in settled z_ok z_out wch rden_ok y_ok rr_ok pxch x2_ok st2_ok mv_ok""".split()
    S = {n: sem(n) for n in names}
    x_in = [sem(f"x_in{k}") for k in range(4)]
    xt_in = [sem(f"xt_in{k}") for k in range(4)]
    x2_in = sem("x2_in")
    xr_in = sem("xr_in")
    vb_out = [sem(f"vb_out{k}") for k in range(2)]
    wf_in = [sem(f"wf_in{k}") for k in range(2)]
    w16_out = [sem(f"w16_out{k}") for k in range(2)]
    v_in = [sem(f"v_in{q}") for q in range(2)]
    st_out = [sem(f"st_out{k}") for k in range(2)]
    sc_in = [sem(f"sc_in{q}") for q in range(2)]
    adj_in = [sem(f"adj_in{k}") for k in range(STAGE)]

    adj_v = adj_t.rearrange("b (n k) p i -> b n p k i", k=2)

    def acc_tile(q, it, a0, a1):
        o = (it % 3) * VW
        return acc[q][it // 3][:, o + a0:o + a1]

    def settle(eng):
        eng.sem_inc(S["settled"], 1)

    stage_f = [stage[:, k, :, :].bitcast(F32).rearrange("p a i -> p (a i)")[:, 0:4 * D].rearrange("p (t d) -> p t d", d=D) for k in range(2)]
    block = ctx.enter_context(nc.Block())

    @block.sync
    def _(sp):
        sp.dma_start(wn_sb[:, :, :], w_n.rearrange("(c p) n -> p c n", p=P)).then_inc(S["w_in"], 16)
        sp.dma_start(wext[:, :, S0:CW], w_t.rearrange("(c p) n -> p c n", p=P)).then_inc(S["w_in"], 16)
        for k in range(4):
            sp.dma_start(xt_sb[:, :, k * 1024:(k + 1) * 1024], x_t[:, :, k * 1024:(k + 1) * 1024].rearrange("c p n -> p c n")).then_inc(xt_in[k], 16)
            sp.dma_start(x_sb[:, k * 8:k * 8 + 8, :], x[k * 1024:(k + 1) * 1024, :].rearrange("(t p) d -> p t d", p=P)).then_inc(x_in[k], 16)

        def load_pair(b, n, k):
            sp.dma_start(stage[:, k, :, :], adj_v[bass.ds(b, 1), n].rearrange("a p k i -> (a p) k i")).then_inc(adj_in[k], 16)

        load_pair(0, 0, 0)
        load_pair(0, 1, 1)
        for n in range(2, NPAIR):
            if n == 12:
                for k in range(2):
                    sp.wait_ge(st_out[k], 16 * (NT // 8))
                for q in range(2):
                    sp.dma_start(s_cur[:, q, :], s_dram[q:q + 1, 0:BI].broadcast_to([P, BI])).then_inc(sc_in[q], 16)
            sp.wait_ge(S["conv_ok"], n - 1)
            load_pair(0, n, n % 2)
        sp.wait_ge(S["d_ok"], 1)
        sp.dma_start(d_dram.rearrange("h p c -> p h c"), dcol[:, :, :, :].rearrange("p h a t -> p h (a t)")).then_inc(S["d_out"], 16)

        def step(b, h, masks_too, first_block=False):
            g = b * H + h
            if not (isinstance(b, int) and b == 0) and h % 2 == 0:
                pair = (b - 1) * (IT // 2) + h // 2
                sp.wait_ge(S["x2_ok"], pair + 1)
                sp.dma_start(xr, x[bass.ds(pair * 2 * P, 2 * P), :].rearrange("(t p) d -> p t d", p=P)).then_inc(xr_in, 16)
            if masks_too:
                for k in range(2):
                    sp.wait_ge(S["conv_ok"], g * 2 + NPAIR - 1 + k)
                    load_pair(b + 1, 2 * h + k, k)
            if first_block and h == 0:
                sp.wait_ge(S["vb_ok"], 2)
                for k in range(2):
                    sp.dma_start(v_dram[k], v_cur[:, k, :, :].rearrange("p t c -> p (t c)")).then_inc(S["v_st"], 16)
                sp.wait_ge(S["d_out"], 16)
                sp.wait_ge(S["v_st"], 32)
                sp.wait_ge(S["z_ok"], 2)
            if masks_too or g < Z_STEPS:
                sp.dma_start(xs_dram[bass.ds(g * Z_ROWS, Z_ROWS), :].rearrange("(r p) c -> p r c", p=P),
                             zeros[:, :].rearrange("p (o c) -> p o c", o=1).broadcast_to([P, Z_ROWS // P, 2 * D])).then_inc(S["z_out"], 16)
            if not masks_too and h >= H - 2:
                return
            q, b2, h2 = h % 2, b + (h + 2) // H, (h + 2) % H
            if first_block and h2 >= 2:
                for k in range(2):
                    sp.wait_ge(vb_out[k], 16 * (h2 - 1))
            sp.wait_ge(S["pe_done"], g * NG + NG)
            sp.dma_start(v_cur[:, q, :, :].rearrange("p t c -> p (t c)"), v_dram[h2]).then_inc(v_in[q], 16)
            sp.dma_start(d_cur[:, q, :, :].rearrange("p a t -> p (a t)"), d_dram[h2]).then_inc(v_in[q], 16)
            sp.dma_start(s_cur[:, q, :], s_dram[h2:h2 + 1, bass.ds(b2 * BI, BI)].broadcast_to([P, BI])).then_inc(sc_in[q], 16)

        for h in range(H):
            step(0, h, True, True)
        with sp.Fori(1, NB - 1) as b:
            for h in range(H):
                step(b, h, True)
        for h in range(H):
            step(NB - 1, h, False)
            if h == 2:
                sp.dma_start(x_sb[:, NT - IT:NT, :], x[(NT - IT) * P:N, :].rearrange("(t p) d -> p t d", p=P)).then_inc(x2_in, 16)
        for k in range(2):
            sp.wait_ge(w16_out[k], 16 * UNITS // 2)
        sp.wait_ge(S["z_out"], 16 * Z_STEPS)

    @block.gpsimd
    def _(pool):
        nc.gpsimd.memset(ident[:, :], 0.0).then_inc(S["pch"], 1)
        nc.gpsimd.memset(lnc[:, :], math.log(VSCALE)).then_inc(S["pch"], 1)
        nc.gpsimd.memset(ones[:, :], 1.0).then_inc(S["pch"], 1)
        nc.gpsimd.memset(ws_col[:, :], WS).then_inc(S["z_ok"], 1)
        pool.wait_ge(S["pch"], 3)
        nc.gpsimd.affine_select(out=ident[:, :], in_=ident[:, :], compare_op=ALU.not_equal, fill=1.0, base=0,
                                pattern=[[-1, P]], channel_multiplier=1).then_inc(S["ident_ok"], 1)
        nc.gpsimd.memset(zeros[:, :], 0.0).then_inc(S["z_ok"], 1)
        pool.wait_ge(S["z_ok"], 2)
        for t in range(1, NT):
            pool.wait_ge(S["h_ok"], t + 1)
            if t > 1:
                pool.wait_ge(S["hs_ok"], t - 1)
            nc.gpsimd.tensor_tensor(hmean[:, :], hp[:, 0, :] if t == 1 else hmean[:, :], hp[:, t, :], ALU.add).then_inc(S["hs_ok"], 1)
        pool.wait_ge(S["dmx_ok"], 1)
        nc.gpsimd.partition_all_reduce(dmxa[:, :], dmx[:, :], P, RMAX).then_inc(S["dmxa_ok"], 1)

        nv = [0]

        def v_done(ins):
            nv[0] += 1
            ins.then_inc(S["pvch"], 1)
            pool.wait_ge(S["pvch"], nv[0])

        stored = [0]

        def build_v(h):
            for k in range(2):
                sl = slice(k * NT // 2, (k + 1) * NT // 2)
                for s in range(2):
                    f = fw[:, s, sl, h:h + 1]
                    nc.gpsimd.tensor_tensor(pv32[:, :, s, 0:HD], hp[:, sl, h * HD:(h + 1) * HD], f.broadcast_to([P, NT // 2, HD]), ALU.mult).then_inc(S["pvch"], 1)
                    nc.gpsimd.tensor_copy(pv32[:, :, s, HD:VC], f).then_inc(S["pvch"], 1)
                if stored[0]:
                    pool.wait_ge(vb_out[k], 16 * stored[0])
                for s in range(2):
                    f = fw[:, s, sl, h:h + 1]
                    nc.gpsimd.tensor_tensor(pvb5[k][:, :, s, 0, 0:HD], hp[:, sl, h * HD:(h + 1) * HD], f.broadcast_to([P, NT // 2, HD]), ALU.mult).then_inc(S["pvch"], 1)
                    nc.gpsimd.tensor_copy(pvb5[k][:, :, s, 0, HD:VC], f).then_inc(S["pvch"], 1)
                nv[0] += 8
                pool.wait_ge(S["pvch"], nv[0])
                v_done(nc.gpsimd.tensor_tensor(pvb5[k][:, :, :, 1, :], pv32, pvb5[k][:, :, :, 0, :], ALU.subtract))
                pool.dma_start(v_dram[h].rearrange("p (k c) -> k p c", k=2)[k], pvb[k]).then_inc(vb_out[k], 16)
            stored[0] += 1

        LINKS = 9

        def finish_head(b, h, q):
            g = b * H + h
            link = [0]

            def done(ins):
                link[0] += 1
                ins.then_inc(S["pch"], 1)
                pool.wait_ge(S["pch"], 3 + g * LINKS + link[0])

            pool.wait_ge(S["comb_ok"], g + 3)
            al = ab[:, 0, bass.ds(b * IT, IT), h:h + 1].broadcast_to([P, IT, VC])
            be = ab[:, 1, bass.ds(b * IT, IT), h:h + 1].broadcast_to([P, IT, VC])
            for s in range(2):
                done(nc.gpsimd.tensor_tensor(pw[:, s], comb[:, q, :, s, 0, :], comb[:, q, :, s, 1, :], ALU.add))
            done(nc.gpsimd.tensor_tensor(pw[:, 0], pw[:, 0], al, ALU.mult))
            done(nc.gpsimd.tensor_tensor(pw[:, 1], pw[:, 1], be, ALU.mult))
            done(nc.gpsimd.tensor_tensor(pw[:, 0], pw[:, 0], pw[:, 1], ALU.add))
            settle(pool)
            done(nc.gpsimd.tensor_scalar(flag[:, :], pw[:, 0, :, HD], 0.0, None, ALU.is_equal))
            done(nc.gpsimd.tensor_tensor(den[:, bass.ds(b * IT, IT), h], pw[:, 0, :, HD], flag[:, :], ALU.add))
            done(nc.gpsimd.tensor_tensor(fl[:, :, :], flag[:, :].rearrange("p (t o) -> p t o", o=1).broadcast_to([P, IT, HD]),
                                         hmean[:, h * HD:(h + 1) * HD].rearrange("p (o c) -> p o c", o=1).broadcast_to([P, IT, HD]), ALU.mult))
            done(nc.gpsimd.tensor_tensor(hp[:, bass.ds(b * IT, IT), h * HD:(h + 1) * HD], pw[:, 0, :, 0:HD], fl[:, :, :], ALU.add))
            pool.sem_inc(S["comb_free"], 1)

        def load_unit(u, k):
            pool.dma_start(wf[k], w_all[bass.ds(u, 1)].rearrange("o p c -> (o p) c")).then_inc(wf_in[k], 16)

        def split_unit(u, half, k, more):
            if more:
                load_unit(u + 1, 1 - k)
            pool.wait_ge(wf_in[k], half * 16 + 16)
            if not isinstance(u, int) or u >= 2:
                pool.wait_ge(w16_out[k], half * 16)
            settle(pool)
            nc.gpsimd.tensor_tensor(w16[k][:, 0, :], wf[k], ws_col.broadcast_to([P, F]), ALU.mult).then_inc(S["wch"], 1)
            nc.gpsimd.tensor_tensor(wf[k], wf[k], ws_col.broadcast_to([P, F]), ALU.mult).then_inc(S["wch"], 1)
            pool.wait_ge(S["wch"], u * 3 + 2)
            nc.gpsimd.tensor_tensor(w16[k][:, 1, :], wf[k], w16[k][:, 0, :], ALU.subtract).then_inc(S["wch"], 1)
            pool.wait_ge(S["wch"], u * 3 + 3)
            pool.dma_start(w16_dram[bass.ds(u, 1)].rearrange("o p l c -> (o p) (l c)"), w16[k].rearrange("p l c -> p (l c)")).then_inc(w16_out[k], 16)

        def post_divide(pair):
            pool.wait_ge(S["rden_ok"], pair + 1)
            settle(pool)
            y4 = hp[:, bass.ds(2 * pair, 2), :].rearrange("p t (h c) -> p t h c", h=H)
            rd = den[:, bass.ds(2 * pair, 2), :].rearrange("p t (h o) -> p t h o", o=1).broadcast_to([P, 2, H, HD])
            nc.gpsimd.tensor_tensor(y4, y4, rd, ALU.mult).then_inc(S["y_ok"], 1)

        def post_add(pair):
            link = [0]

            def done(ins):
                link[0] += 1
                ins.then_inc(S["pxch"], 1)
                pool.wait_ge(S["pxch"], pair * 3 + link[0])
                settle(pool)

            y = hp[:, bass.ds(2 * pair, 2), :]
            pool.wait_ge(S["rr_ok"], pair * 2 + 2)
            pool.wait_ge(xr_in, pair * 16 + 16)
            settle(pool)
            done(nc.gpsimd.tensor_tensor(y, y, rr, ALU.add))
            done(nc.gpsimd.tensor_tensor(y, y, xr, ALU.add))
            done(nc.gpsimd.tensor_tensor(ee[:, :, :], ee[:, :, :], ones[:, 0:1].rearrange("p (t o) -> p t o", o=1).broadcast_to([P, 2, D]), ALU.subtract))
            nc.gpsimd.tensor_tensor(y, y, ee[:, :, :], ALU.add).then_inc(S["x2_ok"], 1)

        pool.wait_ge(S["fw_ok"], 3)
        pool.sem_inc(S["comb_free"], 1)
        pool.sem_inc(S["x2_ok"], 1)
        build_v(2)
        build_v(3)
        pool.wait_ge(S["ab_ok"], 1)
        pool.wait_ge(S["hm_ok"], 1)
        for h in range(H):
            if h < H - 4:
                build_v(h + 4)
            finish_head(0, h, h % 2)
            if h == H // 2:
                for k in range(2):
                    pool.wait_ge(vb_out[k], 16 * stored[0])
                load_unit(0, 0)
            for u in ([], [], [], [], [0], [1, 2], [3], [4, 5])[h]:
                split_unit(u, u // 2, u % 2, u < 5)
        with pool.Fori(1, NB) as b:
            load_unit(b * 10 - 4, 0)
            for h in range(H):
                pair = (b - 1) * (IT // 2) + h // 2
                if h % 2 == 0:
                    post_divide(pair)
                finish_head(b, h, h % 2)
                for i in ([0], [1, 2], [3], [4], [5], [6, 7], [8], [9])[h]:
                    split_unit(b * 10 - 4 + i, b * 5 - 2 + i // 2, i % 2, i < 9)
                if h % 2 == 0:
                    post_add(pair)

    @block.tensor
    def _(pe):
        pe.wait_ge(S["w_in"], 64)
        pe.wait_ge(S["wa_ok"], 1)
        pe.wait_ge(S["ident_ok"], 1)
        wa = aux[0]
        for c in range(DC):
            for k in range(DC):
                nc.tensor.matmul(wa[:, c * S0:(c + 1) * S0], wn_sb[:, k, c * P:(c + 1) * P], ablk[:, k, :], start=(c == 0 and k == 0), stop=(k == DC - 1), skip_group_check=True)
        for k in range(DC):
            last = nc.tensor.matmul(wa[0:1, 2 * S0:3 * S0], bcol[:, k:k + 1], ablk[:, k, :], start=False, stop=(k == DC - 1), skip_group_check=True)
        last.then_inc(S["wa_ps"], 1)
        pe.wait_ge(S["wa_ok"], 2)
        nc.tensor.matmul(acc[0][0][:, 0:CW], ones[0:1, :], bext[:, :], start=True, stop=True)
        for c in range(DC):
            last = nc.tensor.matmul(acc[0][1][:, 0:CW], ones[:, :], wext[:, c, :], start=(c == 0), stop=(c == DC - 1))
        last.then_inc(S["wa_ps"], 1)
        pe.wait_ge(S["wa_ok"], 3)

        def transpose_scores(t):
            pe.wait_ge(S["h_ok"], t + 1)
            if t % 4 == 0 and t >= 8:
                pe.wait_ge(S["sT_ok"], t // 4 - 1)
            last = nc.tensor.transpose(aux[(t // 4) % 2][:, (t % 4) * P:(t % 4 + 1) * P], hext[:, t, 0:P], ident[:, :])
            if t % 4 == 3:
                last.then_inc(S["sT_ps"], 1)

        for t in range(NT):
            if t % 8 == 0:
                pe.wait_ge(xt_in[t // 8], 16)
            if t >= len(h_ps_buf):
                pe.wait_ge(S["h_ok"], t - len(h_ps_buf) + 1)
            for c in range(DC):
                last = nc.tensor.matmul(h_ps_buf[t % len(h_ps_buf)][:, 0:CW], xt_sb[:, c, t * P:(t + 1) * P], wext[:, c, :], start=(c == 0), stop=(c == DC - 1))
            last.then_inc(S["h_ps"], 1)
            if t >= 2:
                transpose_scores(t - 2)
        transpose_scores(NT - 2)
        transpose_scores(NT - 1)
        pe.wait_ge(S["hs_ok"], NT - 1)
        nc.tensor.matmul(acc[1][1][:, 0:D], ones[:, :], hmean[:, :], start=True, stop=True).then_inc(S["hm_ps"], 1)

        def head(b, r, q, par):
            g = b * H + 2 * r + q
            pe.wait_ge(v_in[q], (b * (H // 2) + r) * 32 + 32)
            if q:
                pe.wait_ge(S["hm_ok"], 1)
            for n in range(NG):
                if n == 0:
                    pe.wait_ge(S["comb_ok"], g + 1)
                pe.wait_ge(S["m_ready"], g * NG + n + 1)
                settle(pe)
                for jj in range(GJ):
                    j = n * GJ + jj
                    slot = j % (RING * GJ)
                    for it in range(IT):
                        nc.tensor.matmul(acc_tile(q, it, 0, VW), m_ring[:, slot, it * P:(it + 1) * P], v_cur[:, q, j, :],
                                         start=(j == 0 and it % 3 == 0), stop=False, skip_group_check=True)
                        last = nc.tensor.matmul(acc_tile(q, it, 2 * VC, VW), mask[par][:, j, it * P:(it + 1) * P], v_cur[:, q, j, 2 * VC:VW],
                                                start=False, stop=(j == NT - 1), skip_group_check=True)
                last.then_inc(S["pe_done"], 1)

        with pe.Fori(0, NB, 2) as b:
            for par in range(2):
                with pe.Fori(0, H // 2) as r:
                    head(b + par, r, 0, par)
                    head(b + par, r, 1, par)

    @block.scalar
    def _(act):
        act.dma_start(acol[:, :], a).then_inc(S["a_in"], 16)
        act.dma_start(bcol[:, :], b_w.rearrange("(c p) -> p c", p=P)).then_inc(S["w_in"], 16)
        act.dma_start(bext[:, S0:CW], b_w.rearrange("(a n) -> a n", a=1)).then_inc(S["w_in"], 16)

        def root(k):
            act.wait_ge(S["var_ok"], k + 1)
            nc.scalar.activation(rstd[:, k * 8:k * 8 + 8], var[:, k * 8:k * 8 + 8], ACT.Sqrt).then_inc(S["std_ok"], 1)

        root(0)
        for k in range(NT // 4):
            if k % 2 == 0 and k < 6:
                root(k // 2 + 1)
            act.wait_ge(S["sT_ps"], k + 1)
            if k >= 2:
                act.wait_ge(st_out[k % 2], 16 * (k // 2))
            nc.scalar.activation(st_sb[:, k % 2, :], aux[k % 2][0:H, :], ACT.Copy).then_inc(S["sT_ok"], 1)
            act.wait_ge(S["sT_ok"], k + 1)
            act.dma_start(s_dram[:, k * 4 * P:(k + 1) * 4 * P], st_sb[:, k % 2, :]).then_inc(st_out[k % 2], 16)
        act.wait_ge(S["fw_in"], 1)
        nc.scalar.activation(fw[:, 0], fw[:, 0], ACT.Exp, bias=lnc[:, :]).then_inc(S["fw_ok"], 1)
        nc.scalar.activation(fw[:, 1], fw[:, 1], ACT.Exp, bias=lnc[:, :]).then_inc(S["fw_ok"], 1)

        def v_high(h):
            act.wait_ge(S["v32_ok"], h + 1)
            v5 = v_cur[:, h, :, :].rearrange("p t (s l c) -> p t s l c", s=2, l=2)
            nc.scalar.activation(v5[:, :, :, 0, :], v32[h], ACT.Copy).then_inc(S["vhi_ok"], 1)

        def rest_of_setup():
            v_high(1)
            act.wait_ge(S["hm_ps"], 1)
            nc.scalar.activation(hmean[:, :], acc[1][1][:, 0:D], ACT.Copy, scale=1.0 / N).then_inc(S["hm_ok"], 1)
            act.wait_ge(S["fw_in"], 2)
            nc.scalar.activation(ab[:, :, :, :], ab[:, :, :, :], ACT.Exp).then_inc(S["ab_ok"], 1)

        v_high(0)
        act.wait_ge(S["dcur_ok"], 1)
        POST_N = 4

        def head(g, r, q, post=False):
            if not (isinstance(g, int) and g == 0):
                act.wait_ge(v_in[q], r * 32 + 32)
            act.wait_ge(sc_in[q], r * 16 + 16)
            for n in range(NG):
                if isinstance(g, int) and g == 0:
                    if n >= RING:
                        act.wait_ge(S["pe_done"], n - RING + 1)
                else:
                    act.wait_ge(S["pe_done"], g * NG + n - RING + 1)
                settle(act)
                if isinstance(g, int) and g == 0 and n == 3:
                    rest_of_setup()
                if post and q and n == POST_N:
                    act.wait_ge(S["y_ok"], r - H // 2 + 1)
                    act.wait_ge(S["x2_ok"], r - H // 2 + 1)
                    settle(act)
                    nc.scalar.activation(rr, hp[:, bass.ds(2 * r - H, 2), :], ACT.Relu, scale=-1.0).then_inc(S["rr_ok"], 1)
                    act.wait_ge(S["rr_ok"], 2 * r - H + 1)
                    settle(act)
                    nc.scalar.activation(ee[:, :, :], rr, ACT.Exp, scale=-1.0).then_inc(S["rr_ok"], 1)
                for jj in range(ACT_T[n]):
                    j = n * GJ + jj
                    nc.scalar.activation(m_ring[:, j % (RING * GJ), :], s_cur[:, q, :], ACT.Sigmoid,
                                         bias=d_cur[:, q, 1, j:j + 1], scale=STEP, saturate=False).then_inc(S["act_t"], 1)

        head(0, 0, 0)
        head(1, 0, 1)
        with act.Fori(1, H // 2) as r:
            head(2 * r, r, 0)
            head(2 * r + 1, r, 1)
        with act.Fori(H // 2, NB * H // 2) as r:
            head(2 * r, r, 0, True)
            head(2 * r + 1, r, 1, True)
        for k in range(2):
            act.wait_ge(S["hm_in"], k + 1)
            nc.scalar.activation(stage_f[k % 2], stage_f[k % 2], ACT.Exp).then_inc(S["ach"], 1)

    @block.vector
    def _(dve):
        nd = [0]

        def done(ins):
            nd[0] += 1
            ins.then_inc(S["dch"], 1)
            dve.wait_ge(S["dch"], nd[0])

        dve.sem_inc(S["comb_ok"], 2)
        done(nc.vector.memset(ablk[:, :, :], 0.0))
        dve.wait_ge(S["a_in"], 16)
        for q in range(4):
            for c in range(DC):
                for s in range(2):
                    k = s * H + c * 4 + q
                    last = nc.vector.tensor_copy(ablk[32 * q:32 * q + 32, c, k:k + 1], acol[32 * q:32 * q + 32, s:s + 1])
        done(last)
        dve.sem_inc(S["wa_ok"], 1)

        def statistics(k):
            dve.wait_ge(x_in[k], 16)
            for t in range(k * 8, k * 8 + 8):
                nc.vector.bn_stats(stats[:, t, :], x_sb[:, t, :]).then_inc(S["stats_ok"], 1)
            dve.wait_ge(S["stats_ok"], k * 8 + 8)
            for t in range(k * 8, k * 8 + 8):
                last = nc.vector.bn_aggr(mv[:, t, :], stats[:, t, :])
            done(last)
            sl = slice(k * 8, k * 8 + 8)
            nc.vector.tensor_scalar(var[:, sl], mv[:, sl, 1], 1e-5, None, ALU.add).then_inc(S["var_ok"], 1)

        def refine(k):
            sl = slice(k * 8, k * 8 + 8)
            dve.wait_ge(S["std_ok"], k + 1)
            rsqrt_refined(nc, done, rstd[:, sl], tmp[:, sl], var[:, sl])

        dve.wait_ge(S["wa_ps"], 1)
        nc.vector.tensor_copy(wext[:, :, 0:S0], aux[0][:, 0:2 * S0].rearrange("p (c k) -> p c k", c=DC))
        nc.vector.tensor_copy(bext[:, 0:S0], aux[0][0:1, 2 * S0:3 * S0]).then_inc(S["wa_ok"], 1)
        statistics(0)
        dve.wait_ge(S["wa_ps"], 2)
        nc.vector.tensor_copy(bias[:, :], acc[0][0][:, 0:CW])
        for c in range(DC):
            last = nc.vector.scalar_tensor_tensor(out=wext[:, c, :], in0=acc[0][1][:, 0:CW], scalar=-1.0 / D, in1=wext[:, c, :], op0=ALU.mult, op1=ALU.add)
        done(last)
        dve.sem_inc(S["wa_ok"], 1)
        refine(0)

        CONV_T, CONV_N, CONV_V = 8, 10, 2

        def convert(par, n, k, count):
            dve.wait_ge(adj_in[k], count)
            settle(dve)
            nc.vector.tensor_scalar(mask_u8[par][:, bass.ds(2 * n, 2), :], stage[:, k, :, :], 0, MINUS_ONE, ALU.not_equal, ALU.mult).then_inc(S["conv_ok"], 1)

        for t in range(NT):
            dve.wait_ge(S["h_ps"], t + 1)
            nc.vector.scalar_tensor_tensor(out=hext[:, t, :], in0=h_ps_buf[t % len(h_ps_buf)][:, 0:CW], scalar=rstd[:, t:t + 1], in1=bias[:, :], op0=ALU.mult, op1=ALU.add).then_inc(S["h_ok"], 1)
            if t % 8 == 3 and t < NT - 8:
                statistics(t // 8 + 1)
            if t % 8 == 7 and t < NT - 1:
                refine(t // 8 + 1)
            if t >= CONV_T and t % 2 and t < CONV_T + 2 * CONV_N:
                n = (t - CONV_T) // 2
                convert(0, n, n % 2, n // 2 * 16 + 16)
        dve.wait_ge(S["h_ok"], NT)
        dst = hext[:, :, H:2 * H]
        nc.vector.tensor_reduce(dmx[:, :], dst.rearrange("p t h -> p h t"), AX, ALU.max).then_inc(S["dmx_ok"], 1)
        nc.vector.tensor_scalar(dcol[:, :, 0, :], dst.rearrange("p t h -> p h t"), -1.0, None, ALU.mult)
        nc.vector.tensor_scalar(dcol[:, :, 1, :], dst.rearrange("p t h -> p h t"), STEP, None, ALU.mult).then_inc(S["d_ok"], 1)
        dve.wait_ge(S["d_ok"], 1)
        nc.vector.tensor_copy(d_cur[:, :, :, :], dcol[:, 0:2, :, :]).then_inc(S["dcur_ok"], 1)
        dve.wait_ge(S["dmxa_ok"], 1)
        dmb = dmxa[:, :].rearrange("p (o h) -> p o h", o=1).broadcast_to([P, NT, H])
        done(nc.vector.tensor_tensor(fw[:, 0], dst, dmb, ALU.subtract))
        done(nc.vector.tensor_scalar(fw[:, 1], fw[:, 0], 0.2, None, ALU.mult))
        dve.sem_inc(S["fw_in"], 1)
        dve.wait_ge(S["fw_ok"], 2)
        done(nc.vector.tensor_scalar(fw[:, 1], fw[:, 1], -1.0, None, ALU.mult))
        dve.sem_inc(S["fw_ok"], 1)

        def v_low(h):
            v5 = v_cur[:, h, :, :].rearrange("p t (s l c) -> p t s l c", s=2, l=2)
            dve.wait_ge(S["vhi_ok"], h + 1)
            nc.vector.tensor_tensor(v5[:, :, :, 1, :], v32[h], v5[:, :, :, 0, :], ALU.subtract).then_inc(S["vb_ok"], 1)
            dve.wait_ge(S["vb_ok"], h + 1)
            dve.sem_inc(v_in[h], 32)

        def v_columns(h):
            for s in range(2):
                f = fw[:, s, :, h:h + 1]
                nc.vector.tensor_tensor(v32[h][:, :, s, 0:HD], hp[:, :, h * HD:(h + 1) * HD], f.broadcast_to([P, NT, HD]), ALU.mult)
                last = nc.vector.tensor_copy(v32[h][:, :, s, HD:VC], f)
            last.then_inc(S["v32_ok"], 1)

        v_columns(0)
        done(nc.vector.tensor_tensor(ab[:, 0], hext[:, :, 0:H], dmb, ALU.add))
        done(nc.vector.tensor_scalar(ab[:, 1], ab[:, 0], -0.8, 0.0, ALU.mult, ALU.min))
        done(nc.vector.tensor_scalar(ab[:, 0], ab[:, 0], 0.8, 0.0, ALU.mult, ALU.min))
        dve.sem_inc(S["fw_in"], 1)
        for n in range(CONV_N, CONV_N + CONV_V):
            convert(0, n, n % 2, n // 2 * 16 + 16)
        dve.wait_ge(S["dcur_ok"], 1)

        ms = m_ring.bitcast(U32)
        mk = [m.bitcast(U32) for m in mask]

        def evacuate(g, q):
            dve.wait_ge(S["pe_done"], g * NG + NG)
            if not (isinstance(g, int) and g == 0):
                dve.wait_ge(S["comb_free"], g)
            for k in range(3):
                t0, t1 = 3 * k, min(3 * k + 3, IT)
                last = nc.vector.tensor_copy(comb[:, q, t0:t1, :, :, :].rearrange("p t s l c -> p (t s l c)"), acc[q][k][:, 0:(t1 - t0) * VW])
            last.then_inc(S["comb_ok"], 1)

        def statistics_of(pair):
            dve.wait_ge(S["x2_ok"], pair + 2)
            settle(dve)
            for u in range(2):
                nc.vector.bn_stats(st2[:, u, :], hp[:, bass.ds(2 * pair + u, 1), :].rearrange("p o d -> p (o d)")).then_inc(S["st2_ok"], 1)
            dve.wait_ge(S["st2_ok"], 2 * pair + 2)
            settle(dve)
            for u in range(2):
                last = nc.vector.bn_aggr(mvt[:, u, :], st2[:, u, :])
            last.then_inc(S["mv_ok"], 1)
            dve.wait_ge(S["mv_ok"], 2 * pair + 1)
            settle(dve)
            nc.vector.tensor_copy(mv2[:, bass.ds(2 * pair, 2), :], mvt[:, :, :]).then_inc(S["mv_ok"], 1)

        def head(b, r, q, first=False):
            g = b * H + 2 * r + q
            par = b % 2
            if not first:
                dve.wait_ge(v_in[q], (b * (H // 2) + r) * 32 + 32)
            dve.wait_ge(sc_in[q], (b * (H // 2) + r) * 16 + 16)
            for n in range(NG):
                if first:
                    if n >= RING:
                        dve.wait_ge(S["pe_done"], n - RING + 1)
                    made = min(NPAIR, CONV_N + CONV_V + 2 * n)
                    if n:
                        for m in range(min(NPAIR, CONV_N + CONV_V + 2 * n - 2), made):
                            convert(0, m, m % 2, m // 2 * 16 + 16)
                    dve.wait_ge(S["conv_ok"], made)
                else:
                    dve.wait_ge(S["pe_done"], g * NG + n - RING + 1)
                if first and n == 1:
                    v_columns(1)
                if first and n == 3:
                    v_low(1)
                settle(dve)
                for jj in range(ACT_T[n], GJ):
                    j = n * GJ + jj
                    nc.vector.tensor_scalar(m_ring[:, j % (RING * GJ), :], s_cur[:, q, :], d_cur[:, q, 0, j:j + 1], None, ALU.is_gt, saturate=False).then_inc(S["dve_t"], 1)
                j0, k = (n * GJ) % (RING * GJ), ACT_T[n]
                dve.wait_ge(S["act_t"], g * sum(ACT_T) + sum(ACT_T[:n + 1]))
                nc.vector.tensor_tensor(ms[:, j0:j0 + k, :], ms[:, j0:j0 + k, :], mk[par][:, n * GJ:n * GJ + k, :], ALU.bitwise_and)
                dve.wait_ge(S["dve_t"], g * sum(DVE_T) + sum(DVE_T[:n + 1]))
                nc.vector.tensor_tensor(ms[:, j0 + k:j0 + GJ, :], ms[:, j0 + k:j0 + GJ, :], mk[par][:, n * GJ + k:(n + 1) * GJ, :], ALU.bitwise_and).then_inc(S["m_ready"], 1)
                if n == 0 and first:
                    v_low(0)
                if n == 1 and not first:
                    evacuate(g - 1, 1 - q)
                if b and q == 0 and n == 6:
                    dve.wait_ge(S["comb_free"], b * H + 1)
                    rd = den_flat[:, bass.ds(((b - 1) * IT + 2 * r) * H, 2 * H)]
                    nc.vector.reciprocal(rd, rd).then_inc(S["rden_ok"], 1)
                if b and q == 0 and n == 3 and not (b == 1 and isinstance(r, int)):
                    statistics_of((b - 1) * (IT // 2) + r - 1)
                if n in (4, 6) and b < NB - 1:
                    k = (n - 4) // 2
                    convert(1 - par, (2 * r + q) * 2 + k, k, g * 16 + (NPAIR // 2) * 16 + 16)

        for b in range(NB):
            if b == 0:
                head(0, 0, 0, True)
                head(0, 0, 1)
            if b == 1:
                head(b, 0, 0)
                head(b, 0, 1)
            with dve.Fori(int(b <= 1), H // 2) as r:
                head(b, r, 0)
                head(b, r, 1)
            dve.wait_ge(S["conv_ok"], NPAIR + min(b + 1, NB - 1) * NPAIR)
        evacuate(NB * H - 1, 1)

        statistics_of(NPOST - 1)
        dve.wait_ge(S["comb_free"], NB * H + 1)
        sl = slice(NT - IT, NT)
        done(nc.vector.reciprocal(den[:, sl, :], den[:, sl, :]))
        for k in range(2):
            sl = slice(NT - IT + 4 * k, NT - IT + 4 * k + 4)
            h4 = hp[:, sl, :].rearrange("p t (h c) -> p t h c", h=H)
            done(nc.vector.tensor_tensor(h4, h4, den[:, sl, :].rearrange("p t (h o) -> p t h o", o=1).broadcast_to([P, 4, H, HD]), ALU.mult))
            nc.vector.tensor_scalar(stage_f[k], hp[:, sl, :], 0.0, None, ALU.min).then_inc(S["hm_in"], 1)
        dve.wait_ge(x2_in, 16)
        for k in range(2):
            sl = slice(NT - IT + 4 * k, NT - IT + 4 * k + 4)
            done(nc.vector.scalar_tensor_tensor(out=hp[:, sl, :], in0=hp[:, sl, :], scalar=0.0, in1=x_sb[:, sl, :], op0=ALU.max, op1=ALU.add))
            dve.wait_ge(S["ach"], k + 1)
            nc.vector.scalar_tensor_tensor(out=hp[:, sl, :], in0=stage_f[k], scalar=-1.0, in1=hp[:, sl, :], op0=ALU.add, op1=ALU.add).then_inc(S["hp_ok"], 1)
        for t in range(NT - IT, NT):
            dve.wait_ge(S["hp_ok"], (t - NT + IT) // 4 + 1)
            nc.vector.bn_stats(stats[:, t, :], hp[:, t, :]).then_inc(S["stats_ok"], 1)
        dve.wait_ge(S["stats_ok"], NT + IT)
        for t in range(NT - IT, NT):
            last = nc.vector.bn_aggr(mv2[:, t, :], stats[:, t, :])
        done(last)


def ffn(nc, ctx, x2, mv, w_route, b_route, b1_all, b2_all, w16_dram, xs_dram, ys_dram, out_dram):
    def sb(name, shape, dt=F32):
        return ctx.enter_context(nc.sbuf_tensor(name, shape, dt))

    def ps(name, shape, dt=F32):
        return ctx.enter_context(nc.psum_tensor(name, shape, dt))

    def sem(name):
        return ctx.enter_context(nc.semaphore(name))

    w_sb = sb("w_sb", [P, E + 1, EW], F16)
    w_flat = w_sb[:, :, :].rearrange("p e c -> p (e c)")
    b1_sb = sb("b1_sb", [P, (E + 1) * FC])
    b2_sb = sb("b2_sb", [P, E + 1, D])
    hf = sb("hf", [P, FC // 2, SLOT])
    hh = sb("hh", [P, 2, FC, SLOT], F16)
    xs = sb("xs", [P, SUB, 2, D], F16)
    xt = sb("xt", [P, 2, DC, SLOT], F16)
    y_sb = sb("y_sb", [P, SUB, D])
    pos_i = sb("pos_i", [P, 2, NT], I32)
    wts = sb("wts", [P, 2, NT])
    emap = sb("emap", [P, MOE_SLOTS], I32)

    xhl = w_sb[:, 6:8, :].rearrange("p e c -> p (e c)").rearrange("p (t l d) -> p t l d", l=2, d=D)
    used = [0]

    def temp(n, dt=F32):
        a = used[0]
        used[0] += 2 * n
        assert used[0] <= EW
        return w_sb[:, 5, a:a + 2 * n].bitcast(dt)

    def te(v):
        return v.rearrange("p (t e) -> p t e", e=E)

    logit, one0, one1, both, scan0, scan1 = [te(temp(NT * E)) for _ in range(6)]
    scr = temp(MOE_SLOTS * E)
    top, mark, gap = temp(NT), temp(NT), temp(NT)
    rstd, var, tmp = temp(NT), temp(NT), temp(NT)
    iota_i = temp(MOE_SLOTS, I32)
    iota_f, k256, desc, cnt, ends, ends2 = temp(MOE_SLOTS), temp(16), temp(E), temp(E), temp(E), temp(E)
    bg_sb, wgf = temp(E), temp(DC * E)
    posf = temp(NT)
    xnf = hh[:, :, :, :].rearrange("p l f n -> p (l f n)").bitcast(F32).rearrange("p (k t d) -> p k t d", k=2, d=D)
    xtt = [temp(4 * DC * P // 2).bitcast(F16).rearrange("p (u l c n) -> p u l c n", u=2, l=2, c=DC) for _ in range(2)]
    wg = temp(DC * E)[:, :].bitcast(F16).rearrange("p (l c e) -> p l c e", l=2, e=E)
    ident16 = sb("ident16", [P, P], F16)
    tri, ones = temp(P), temp(P)

    ps_t = [ps(f"ps_t{k}", [P, 1024], F16) for k in range(2)]
    ps_h = [ps(f"ps_h{k}", [P, BANK]) for k in range(4)]
    ps_y = ps("ps_y", [P, BANK])
    ps_g = ps("ps_g", [P, BANK])

    names = """cst_in b1_ok w_sh w_in w_late z_cst cst vch2 wg_in wg_ok f_var f_std xn_ok2 xhi_ok xlo_ok tr_ps tr_ok g_ps g_ok gap_ok ex_ok
        both_ok rank_ps pos_ok xs_out sc_done xs_in t_done xt_ok2 h_ps2 relu_ok hi_ok conv y_ps y_ok y_out
        b2_ok fin_ok fin_out settled2""".split()
    S = {n: sem(n) for n in names}
    g_in = [sem(f"g_in{k}") for k in range(4)]

    def settle(eng):
        eng.sem_inc(S["settled2"], 1)

    def w_at(e, o, n):
        return w_flat[:, bass.ds(e * EW + o, n)] if not isinstance(e, int) else w_sb[:, e, o:o + n]

    def w1_at(e, c, l, f):
        return w_at(e, c * 2048 + l * 1024 + f * P, P)

    def w2_at(e, f, l):
        return w_at(e, (2 + f // 4) * 2048 + l * 1024 + (f % 4) * D, D)

    GBUF = 4
    gbuf = w_sb[:, 0:2, :].rearrange("p e c -> p (e c)").bitcast(F32).rearrange("p (i j k d) -> p i j k d", i=GBUF, j=4, d=D)

    GT = 4
    GROUPS = NT // GT

    block = ctx.enter_context(nc.Block())

    @block.sync
    def _(sp):
        sp.dma_start(wgf, w_route.rearrange("(c p) e -> p c e", p=P)).then_inc(S["wg_in"], 16)
        sp.dma_start(bg_sb, b_route.rearrange("(a e) -> a e", a=1).broadcast_to([P, E])).then_inc(S["cst_in"], 16)
        sp.dma_start(b1_sb[:, :], b1_all.rearrange("(g p) -> p g", p=P)).then_inc(S["cst_in"], 16)
        sp.dma_start(b2_sb[:, :, :], b2_all.rearrange("(a e) d -> a e d", a=1).broadcast_to([P, E + 1, D])).then_inc(S["cst_in"], 16)
        for e in (E, 0, 1):
            sp.dma_start(w_sb[:, e, :].rearrange("p (u c) -> p u c", u=4), w16_dram[4 * e:4 * e + 4].rearrange("u p l c -> p u (l c)")).then_inc(S["w_sh" if e == E else "w_in"], 16)
        for k in range(4):
            sp.wait_ge(S["xlo_ok"], 2 * k + 2)
            row = MOE_SLOTS * SLOT + k * 8 * P
            sp.dma_start(xs_dram[row:row + 8 * P, :].rearrange("(t p) c -> p t c", p=P), xhl[:, 8 * k:8 * k + 8, :, :].rearrange("p t l d -> p t (l d)")).then_inc(S["xs_out"], 16)
        def load_slot(row):
            src = xs_dram[bass.ds(row * SLOT, SLOT), :].rearrange("(u p) c -> p u c", p=P)
            sp.dma_start(xs[:, :, :, :].rearrange("p u l d -> p u (l d)"), src).then_inc(S["xs_in"], 16)

        def store_slot(s):
            sp.wait_ge(S["y_ok"], s + 1)
            sp.dma_start(ys_dram[bass.ds((s - SH_A) * SLOT, SLOT), :].rearrange("(u p) d -> p u d", p=P), y_sb[:, :, :]).then_inc(S["y_out"], 16)

        sp.wait_ge(S["xs_out"], 64)
        load_slot(MOE_SLOTS + 2)
        for e in range(2, 5):
            sp.dma_start(w_sb[:, e, :].rearrange("p (u c) -> p u c", u=4), w16_dram[4 * e:4 * e + 4].rearrange("u p l c -> p u (l c)")).then_inc(S["w_in"], 16)
        with sp.Fori(2, SH_A - 1) as s:
            sp.wait_ge(S["t_done"], s + 1)
            load_slot(MOE_SLOTS + s + 1)
        sp.wait_ge(S["sc_done"], 16 * 2 * NT)
        sp.wait_ge(S["y_ok"], 3)
        for e in range(5, E):
            sp.dma_start(w_sb[:, e, :].rearrange("p (u c) -> p u c", u=4), w16_dram[4 * e:4 * e + 4].rearrange("u p l c -> p u (l c)")).then_inc(S["w_late"], 16)
        sp.wait_ge(S["t_done"], SH_A)
        load_slot(0)
        with sp.Fori(SH_A, SH_B - 1) as s:
            sp.wait_ge(S["t_done"], s + 1)
            load_slot(s - SH_A + 1)
            store_slot(s)
        sp.wait_ge(S["t_done"], SH_B)
        load_slot(SH_B)
        store_slot(SH_B - 1)
        with sp.Fori(SH_B, SLOTS - 1) as s:
            sp.wait_ge(S["t_done"], s + 1)
            load_slot(s + 1)
        for i in range(GROUPS):
            sp.wait_ge(S["fin_ok"], i + 1)
            sp.dma_start(out_dram[i * GT * P:(i + 1) * GT * P, :].rearrange("(u p) d -> p u d", p=P), x2[:, i * GT:(i + 1) * GT, :]).then_inc(S["fin_out"], 16)
        sp.wait_ge(S["fin_out"], 16 * GROUPS)

    @block.gpsimd
    def _(pool):
        nc.gpsimd.memset(tri, 1.0).then_inc(S["z_cst"], 1)
        nc.gpsimd.memset(ones, 1.0).then_inc(S["z_cst"], 1)
        nc.gpsimd.memset(ident16[:, :], 0.0).then_inc(S["z_cst"], 1)
        pool.wait_ge(S["z_cst"], 3)
        nc.gpsimd.affine_select(out=tri, in_=tri, compare_op=ALU.is_gt, fill=0.0, base=0, pattern=[[1, P]], channel_multiplier=-1).then_inc(S["cst"], 1)
        nc.gpsimd.affine_select(out=ident16[:, :], in_=ident16[:, :], compare_op=ALU.not_equal, fill=1.0, base=0, pattern=[[-1, P]], channel_multiplier=1).then_inc(S["cst"], 1)
        nc.gpsimd.iota(iota_i, pattern=[[1, MOE_SLOTS]], base=0, channel_multiplier=0).then_inc(S["cst"], 1)
        for m in range(NT // 4):
            pool.wait_ge(S["xhi_ok"], m + 1)
            nc.gpsimd.tensor_tensor(xhl[:, 4 * m:4 * m + 4, 1, :], xnf[:, m % 2, :, :], xhl[:, 4 * m:4 * m + 4, 0, :], ALU.subtract).then_inc(S["xlo_ok"], 1)
        pool.wait_ge(S["pos_ok"], 1)
        for t in range(NT):
            for k in range(2):
                nc.gpsimd.indirect_dma_start(out=xs_dram, out_offset=bass.IndirectOffsetOnAxis(ap=pos_i[:, k, t:t + 1], axis=0),
                                             in_=xhl[:, t, :, :].rearrange("p l d -> p (l d)"), in_offset=None).then_inc(S["sc_done"], 16)
        pool.wait_ge(S["y_out"], 16 * MOE_SLOTS)
        for i in range(GROUPS):
            if i >= GBUF:
                pool.wait_ge(S["fin_ok"], i - GBUF + 1)
            for j, t in enumerate(range(i * GT, (i + 1) * GT)):
                for k in range(2):
                    nc.gpsimd.indirect_dma_start(out=gbuf[:, i % GBUF, j, k, :], out_offset=None, in_=ys_dram,
                                                 in_offset=bass.IndirectOffsetOnAxis(ap=pos_i[:, k, t:t + 1], axis=0)).then_inc(g_in[i % GBUF], 16)

    @block.tensor
    def _(pe):
        pe.wait_ge(S["cst"], 3)
        def route(k):
            if k == 0:
                pe.wait_ge(S["wg_ok"], 1)
            pe.wait_ge(S["tr_ok"], k + 1)
            for t in range(2 * k, 2 * k + 2):
                n = 0
                for lx, lw in ((0, 0), (1, 0), (0, 1)):
                    for c in range(DC):
                        last = nc.tensor.matmul(ps_g[:, t * E:(t + 1) * E], xtt[k % 2][:, t % 2, lx, c, :], wg[:, lw, c, :], start=(t == 0 and n == 0), stop=(n == 5), skip_group_check=True)
                        n += 1
            last.then_inc(S["g_ps"], 1)

        for k in range(NT // 2):
            pe.wait_ge(S["xlo_ok"], k // 2 + 1)
            if k >= 2:
                pe.wait_ge(S["tr_ok"], k - 1)
            for u in range(2):
                for l in range(2):
                    for c in range(DC):
                        o = ((u * 2 + l) * DC + c) * P
                        last = nc.tensor.transpose(ps_t[k % 2][:, o:o + P], xhl[:, 2 * k + u, l, c * P:(c + 1) * P], ident16[:, :])
            last.then_inc(S["tr_ps"], 1)
            if k:
                route(k - 1)
        route(NT // 2 - 1)
        def ranks():
            pe.wait_ge(S["both_ok"], 1)
            a = both.rearrange("p t e -> p (t e)")
            nc.tensor.matmul(ps_g[:, 0:NT * E], tri, a, start=True, stop=True)
            nc.tensor.matmul(ps_g[:, NT * E:2 * NT * E], ones, a, start=False, stop=True, skip_group_check=True).then_inc(S["rank_ps"], 1)

        def transposes(s):
            rows = xhl[:, s * SUB:(s + 1) * SUB, :, :] if isinstance(s, int) and s < 2 else xs
            if rows is xs:
                pe.wait_ge(S["xs_in"], (s - 1) * 16)
            for l in range(2):
                for c in range(DC):
                    for u in range(SUB):
                        o = (l * DC + c) * SLOT + u * P
                        last = nc.tensor.transpose(ps_t[0][:, o:o + P], rows[:, u, l, c * P:(c + 1) * P], ident16[:, :])
            last.then_inc(S["t_done"], 1)

        def slot(s, e, more):
            pe.wait_ge(S["xt_ok2"], s + 1)
            for f in range(FC):
                n = 0
                for lw, lx in ((0, 0), (0, 1), (1, 0)):
                    for c in range(DC):
                        last = nc.tensor.matmul(ps_h[f // 2][:, (f % 2) * SLOT:(f % 2 + 1) * SLOT], w1_at(e, c, lw, f), xt[:, lx, c, :],
                                                start=(f % 2 == 0 and n == 0), stop=(n == 5), skip_group_check=True)
                        n += 1
                if f % 2:
                    last.then_inc(S["h_ps2"], 1)
            if more:
                transposes(s + 1)
            if isinstance(s, int) and s == 0:
                ranks()
            else:
                pe.wait_ge(S["y_ok"], s)
            for f in range(FC):
                if f % 2 == 0:
                    pe.wait_ge(S["conv"], s * 4 + f // 2 + 1)
                for u in range(SUB):
                    for lw, lh in ((0, 0), (0, 1), (1, 0)):
                        first = f == 0 and u == 0 and lw == 0 and lh == 0
                        last = nc.tensor.matmul(ps_y[:, u * D:(u + 1) * D], hh[:, lh, f, u * P:(u + 1) * P], w2_at(e, f, lw),
                                                start=first, stop=(f == FC - 1 and lw == 1), skip_group_check=True)
            last.then_inc(S["y_ps"], 1)

        pe.wait_ge(S["tr_ok"], NT // 2)
        pe.wait_ge(S["w_sh"], 16)
        transposes(0)
        slot(0, E, True)
        with pe.Fori(1, SH_A) as s:
            slot(s, E, True)
        pe.wait_ge(S["w_in"], 16 * 5)
        pe.wait_ge(S["w_late"], 16 * 3)
        with pe.Fori(SH_A, SH_B) as s:
            e = pe.value_load(emap[0:1, bass.ds(s - SH_A, 1)], min_val=0, max_val=E - 1)
            slot(s, e, True)
        with pe.Fori(SH_B, SLOTS - 1) as s:
            slot(s, E, True)
        slot(SLOTS - 1, E, False)

    @block.scalar
    def _(act):
        def copy_pair(k):
            act.wait_ge(S["tr_ps"], k + 1)
            if k >= 2:
                act.wait_ge(S["g_ps"], k - 1)
            nc.scalar.activation(xtt[k % 2].rearrange("p u l c n -> p (u l c n)"), ps_t[k % 2][:, :], ACT.Copy).then_inc(S["tr_ok"], 1)

        act.wait_ge(S["f_var"], 1)
        nc.scalar.activation(rstd, var, ACT.Sqrt).then_inc(S["f_std"], 1)
        for k in range(NT // 2):
            copy_pair(k)
        def copy_t(s):
            act.wait_ge(S["t_done"], s + 1)
            nc.scalar.activation(xt[:, :, :, :].rearrange("p l c n -> p (l c n)"), ps_t[0][:, :], ACT.Copy).then_inc(S["xt_ok2"], 1)

        def slot(s, e, more, first=False):
            for f in range(FC):
                if f % 2 == 0:
                    if not (first and f < 4):
                        act.wait_ge(S["conv"], s * 4 + f // 2 - 1)
                    act.wait_ge(S["h_ps2"], s * 4 + f // 2 + 1)
                    settle(act)
                o = e * FC + f
                bias = b1_sb[:, o:o + 1] if isinstance(o, int) else b1_sb[:, bass.ds(o, 1)]
                nc.scalar.activation(hf[:, f % 4, :], ps_h[f // 2][:, (f % 2) * SLOT:(f % 2 + 1) * SLOT], ACT.Relu, bias=bias, scale=XS / (XS * WS)).then_inc(S["relu_ok"], 1)
            if more:
                copy_t(s + 1)

        copy_t(0)
        act.wait_ge(S["b1_ok"], 1)
        slot(0, E, True, True)
        act.wait_ge(S["gap_ok"], 1)
        nc.scalar.activation(gap, gap, ACT.Exp).then_inc(S["ex_ok"], 1)
        with act.Fori(1, SH_A) as s:
            slot(s, E, True)
        with act.Fori(SH_A, SH_B) as s:
            slot(s, act.value_load(emap[0:1, bass.ds(s - SH_A, 1)], min_val=0, max_val=E - 1), True)
        with act.Fori(SH_B, SLOTS - 1) as s:
            slot(s, E, True)
        slot(SLOTS - 1, E, False)

    @block.vector
    def _(dve):
        nd = [0]

        def done(ins):
            nd[0] += 1
            ins.then_inc(S["vch2"], 1)
            dve.wait_ge(S["vch2"], nd[0])

        nc.vector.tensor_scalar(var, mv[:, :, 1], 1e-5, None, ALU.add).then_inc(S["f_var"], 1)
        dve.wait_ge(S["f_std"], 1)
        rsqrt_refined(nc, done, rstd, tmp, var)
        done(nc.vector.tensor_scalar(rstd, rstd, XS, None, ALU.mult))
        for m in range(NT // 4):
            if m == 1:
                dve.wait_ge(S["wg_in"], 16)
                wgv = wgf.rearrange("p (c e) -> p c e", e=E)
                done(nc.vector.tensor_scalar(wgf, wgf, WS, None, ALU.mult))
                done(nc.vector.tensor_copy(wg[:, 0], wgv))
                done(nc.vector.tensor_tensor(wg[:, 1], wgv, wg[:, 0], ALU.subtract))
                dve.sem_inc(S["wg_ok"], 1)
            if m >= 2:
                dve.wait_ge(S["xlo_ok"], m - 1)
            for t in range(4 * m, 4 * m + 4):
                last = nc.vector.tensor_scalar(xnf[:, m % 2, t % 4, :], x2[:, t, :], mv[:, t, 0:1], rstd[:, t:t + 1], ALU.subtract, ALU.mult)
            last.then_inc(S["xn_ok2"], 1)
            dve.wait_ge(S["xn_ok2"], m + 1)
            nc.vector.tensor_copy(xhl[:, 4 * m:4 * m + 4, 0, :], xnf[:, m % 2, :, :]).then_inc(S["xhi_ok"], 1)
        dve.wait_ge(S["cst_in"], 48)
        done(nc.vector.tensor_scalar(b1_sb[:, :], b1_sb[:, :], XS, None, ALU.mult))
        dve.sem_inc(S["b1_ok"], 1)
        done(nc.vector.tensor_scalar(b2_sb[:, E, :], b2_sb[:, E, :], 1.0 / K, None, ALU.mult))
        dve.wait_ge(S["cst"], 3)
        done(nc.vector.tensor_copy(iota_f, iota_i))
        done(nc.vector.tensor_scalar(k256, iota_f[:, 0:16], float(SLOT), None, ALU.mult))
        done(nc.vector.tensor_scalar(desc, iota_f[:, 0:E], -1.0, float(E), ALU.mult, ALU.add))
        dve.wait_ge(S["g_ps"], NT // 2)

        def split_hidden(s):
            for k in range(4):
                dve.wait_ge(S["relu_ok"], s * FC + 2 * k + 2)
                nc.vector.tensor_copy(hh[:, 0, 2 * k:2 * k + 2, :], hf[:, 2 * k % 4:2 * k % 4 + 2, :]).then_inc(S["hi_ok"], 1)
                dve.wait_ge(S["hi_ok"], s * 4 + k + 1)
                nc.vector.tensor_tensor(hh[:, 1, 2 * k:2 * k + 2, :], hf[:, 2 * k % 4:2 * k % 4 + 2, :], hh[:, 0, 2 * k:2 * k + 2, :], ALU.subtract).then_inc(S["conv"], 1)

        def per_t(v):
            return v.rearrange("p (t o) -> p t o", o=1).broadcast_to([P, NT, E])

        def per_e(v, n=NT):
            return v.rearrange("p (o e) -> p o e", o=1).broadcast_to([P, n, E])

        scr_te = te(scr[:, 0:NT * E])
        done(nc.vector.scalar_tensor_tensor(out=logit, in0=ps_g[:, 0:NT * E].rearrange("p (t e) -> p t e", e=E), scalar=1.0 / (XS * WS), in1=per_e(bg_sb), op0=ALU.mult, op1=ALU.add))

        def first_best(one, best):
            done(nc.vector.tensor_reduce(best, logit, AX, ALU.max))
            done(nc.vector.tensor_tensor(scr_te, logit, per_t(best), ALU.is_equal))
            done(nc.vector.tensor_tensor(scr_te, scr_te, per_e(desc), ALU.mult))
            done(nc.vector.tensor_reduce(mark, scr_te, AX, ALU.max))
            done(nc.vector.tensor_tensor(one, scr_te, per_t(mark), ALU.is_equal))

        first_best(one0, top)
        done(nc.vector.scalar_tensor_tensor(out=logit, in0=one0, scalar=-1e30, in1=logit, op0=ALU.mult, op1=ALU.add))
        first_best(one1, gap)
        done(nc.vector.tensor_tensor(gap, gap, top, ALU.subtract))
        dve.sem_inc(S["gap_ok"], 1)
        nc.vector.tensor_tensor(both, one0, one1, ALU.add).then_inc(S["both_ok"], 1)
        split_hidden(0)
        dve.wait_ge(S["rank_ps"], 1)
        tot = ps_g[:, NT * E:2 * NT * E].rearrange("p (t e) -> p t e", e=E)
        done(nc.vector.tensor_copy(scan0, tot))
        a, b = scan0, scan1
        d = 1
        while d < NT:
            done(nc.vector.tensor_copy(b[:, 0:d, :], a[:, 0:d, :]))
            done(nc.vector.tensor_tensor(b[:, d:NT, :], a[:, d:NT, :], a[:, 0:NT - d, :], ALU.add))
            a, b = b, a
            d *= 2
        sc16 = scr[:, 0:E * 16].rearrange("p (e k) -> p e k", k=16)
        done(nc.vector.tensor_tensor(sc16, a[:, NT - 1, :].rearrange("p (e o) -> p e o", o=1).broadcast_to([P, E, 16]),
                                     k256.rearrange("p (o k) -> p o k", o=1).broadcast_to([P, E, 16]), ALU.is_gt))
        done(nc.vector.tensor_reduce(cnt, sc16, AX, ALU.add))
        done(nc.vector.tensor_copy(ends, cnt))
        c0, c1 = ends, ends2
        d = 1
        while d < E:
            done(nc.vector.tensor_copy(c1[:, 0:d], c0[:, 0:d]))
            done(nc.vector.tensor_tensor(c1[:, d:E], c0[:, d:E], c0[:, 0:E - d], ALU.add))
            c0, c1 = c1, c0
            d *= 2
        sce = scr[:, 0:MOE_SLOTS * E].rearrange("p (s e) -> p s e", e=E)
        done(nc.vector.tensor_tensor(sce, per_e(c0, MOE_SLOTS), iota_f.rearrange("p (s o) -> p s o", o=1).broadcast_to([P, MOE_SLOTS, E]), ALU.is_le))
        done(nc.vector.tensor_reduce(iota_f, sce, AX, ALU.add))
        done(nc.vector.tensor_scalar(emap[:, :], iota_f, float(E - 1), None, ALU.min))
        done(nc.vector.tensor_tensor(c1, c0, cnt, ALU.subtract))
        done(nc.vector.tensor_scalar(c1, c1, float(SLOT), None, ALU.mult))
        done(nc.vector.tensor_tensor(a, a, tot, ALU.subtract))
        done(nc.vector.tensor_tensor(a, a, ps_g[:, 0:NT * E].rearrange("p (t e) -> p t e", e=E), ALU.add))
        done(nc.vector.tensor_tensor(a, a, per_e(c1), ALU.add))
        for k, one in enumerate((one0, one1)):
            done(nc.vector.tensor_tensor(scr_te, one, a, ALU.mult))
            done(nc.vector.tensor_reduce(posf, scr_te, AX, ALU.add))
            done(nc.vector.tensor_copy(pos_i[:, k, :], posf))
        dve.sem_inc(S["pos_ok"], 1)
        def shared_slot(s, t, n, split=True):
            if split:
                split_hidden(s)
            for u in range(SUB):
                xt2 = x2[:, bass.ds(t + u, 1), :].rearrange("p o d -> p (o d)")
                last = nc.vector.tensor_tensor(xt2, xt2, b2_sb[:, E, :], ALU.add)
            last.then_inc(S["b2_ok"], 1)
            dve.wait_ge(S["b2_ok"], n + 1)
            dve.wait_ge(S["y_ps"], s + 1)
            for u in range(SUB):
                xt2 = x2[:, bass.ds(t + u, 1), :].rearrange("p o d -> p (o d)")
                last = nc.vector.scalar_tensor_tensor(out=xt2, in0=ps_y[:, u * D:(u + 1) * D], scalar=1.0 / (K * XS * WS), in1=xt2, op0=ALU.mult, op1=ALU.add)
            last.then_inc(S["y_ok"], 1)

        def routed_slot(s, e, first):
            split_hidden(s)
            if not first:
                dve.wait_ge(S["y_out"], (s - SH_A) * 16)
            dve.wait_ge(S["y_ps"], s + 1)
            settle(dve)
            for u in range(SUB):
                b2 = b2_sb[:, :, :].rearrange("p e d -> p (e d)")[:, bass.ds(e * D, D)]
                last = nc.vector.scalar_tensor_tensor(out=y_sb[:, u, :], in0=ps_y[:, u * D:(u + 1) * D], scalar=1.0 / (XS * WS), in1=b2, op0=ALU.mult, op1=ALU.add)
            last.then_inc(S["y_ok"], 1)

        def expert_of(m):
            return dve.value_load(emap[0:1, bass.ds(m, 1)], min_val=0, max_val=E - 1)

        shared_slot(0, 0, 0, False)
        shared_slot(1, SUB, 1)
        dve.wait_ge(S["ex_ok"], 1)
        done(nc.vector.tensor_scalar(wts[:, 0, :], gap, 1.0, None, ALU.add))
        done(nc.vector.reciprocal(wts[:, 0, :], wts[:, 0, :]))
        done(nc.vector.tensor_tensor(wts[:, 1, :], gap, wts[:, 0, :], ALU.mult))
        with dve.Fori(2, SH_A) as s:
            shared_slot(s, s * SUB, s)
        routed_slot(SH_A, expert_of(0), True)
        with dve.Fori(SH_A + 1, SH_B) as s:
            routed_slot(s, expert_of(s - SH_A), False)

        def add_experts(i):
            dve.wait_ge(g_in[i % GBUF], 16 * 2 * GT * (i // GBUF + 1))
            done_slot = (i + 1) * GT // SUB - 1
            dve.wait_ge(S["y_ok"], done_slot + 1 + (MOE_SLOTS if done_slot >= SH_A else 0))
            for k in range(2):
                for j, t in enumerate(range(i * GT, (i + 1) * GT)):
                    last = nc.vector.scalar_tensor_tensor(out=x2[:, t, :], in0=gbuf[:, i % GBUF, j, k, :], scalar=wts[:, k, t:t + 1], in1=x2[:, t, :], op0=ALU.mult, op1=ALU.add)
                if k == 0:
                    done(last)
            last.then_inc(S["fin_ok"], 1)

        TAIL = [[0], [1], [2], [3], [4, 5], [6, 7]]
        for i in range(SH_SLOTS - SH_A):
            shared_slot(SH_B + i, (SH_A + i) * SUB, SH_A + i)
            for g in TAIL[i]:
                add_experts(g)


def gat_moe_kernel(nc, x, x_t, adj_t, w_t, w_n, b_w, a, w_route, b_route, w_all, b1_all, b2_all, out):
    s_dram = nc.dram_tensor("s_dram", (H, N), F32, kind="Internal").ap()
    v_dram = nc.dram_tensor("v_dram", (H, P, NT * VW), F16, kind="Internal").ap()
    d_dram = nc.dram_tensor("d_dram", (H, P, 2 * NT), F32, kind="Internal").ap()
    w16_dram = nc.dram_tensor("w16_dram", (UNITS, P, 2, F), F16, kind="Internal").ap()
    xs_dram = nc.dram_tensor("xs_dram", (N_ROWS, 2 * D), F16, kind="Internal").ap()
    ys_dram = nc.dram_tensor("ys_dram", (MOE_SLOTS * SLOT, D), F32, kind="Internal").ap()
    with ExitStack() as outer:
        outer.enter_context(nc.allow_non_contiguous_dma(reason="biases and a few vectors of a hundred elements"))
        hext = outer.enter_context(nc.sbuf_tensor("hext", [P, NT, CW], F32))
        mv2 = outer.enter_context(nc.sbuf_tensor("mv2", [P, NT, 2], F32))
        with ExitStack() as ctx:
            gat(nc, ctx, hext, mv2, x, x_t, adj_t, w_t, w_n, b_w, a, w_all, s_dram, v_dram, d_dram, w16_dram, xs_dram)
        with ExitStack() as ctx:
            ffn(nc, ctx, hext[:, :, S0:CW], mv2, w_route, b_route, b1_all, b2_all, w16_dram, xs_dram, ys_dram, out)


def kernel(x, adj, L0_gnn_W_w, L0_gnn_W_b, L0_gnn_a, L0_ffn_Wg, L0_ffn_bg, L0_ffn_W1, L0_ffn_b1, L0_ffn_W2, L0_ffn_b2,
           L0_ffn_Ws1, L0_ffn_bs1, L0_ffn_Ws2, L0_ffn_bs2):
    import numpy as np
    import concourse.bacc as bacc
    from concourse.bass_utils import run_bass_kernel_spmd

    def arr(v):
        return np.asarray(v)

    w1 = np.concatenate([arr(L0_ffn_W1), arr(L0_ffn_Ws1)[None]]).reshape(E + 1, DC, P, F)
    w2 = np.concatenate([arr(L0_ffn_W2), arr(L0_ffn_Ws2)[None]]).reshape(E + 1, 2, 4, P, D).transpose(0, 1, 3, 2, 4).reshape(E + 1, 2, P, F)
    arrays = {
        "x": arr(x), "x_t": arr(x).T.reshape(DC, P, N),
        "adj_t": arr(adj).T.reshape(NT, P, NB, BI).transpose(2, 0, 1, 3),
        "w_t": arr(L0_gnn_W_w).T, "w_n": arr(L0_gnn_W_w), "b_w": arr(L0_gnn_W_b), "a": np.tile(arr(L0_gnn_a).reshape(2, HD).T, (P // HD, 1)),
        "w_route": arr(L0_ffn_Wg), "b_route": arr(L0_ffn_bg),
        "w_all": np.concatenate([w1, w2], axis=1).reshape(UNITS, P, F),
        "b1_all": np.concatenate([arr(L0_ffn_b1).reshape(-1), arr(L0_ffn_bs1)]),
        "b2_all": np.concatenate([arr(L0_ffn_b2), arr(L0_ffn_bs2)[None]]),
    }
    arrays = {k: np.ascontiguousarray(v) for k, v in arrays.items()}
    nc = bacc.Bacc("TRN2", target_bir_lowering=False, num_devices=1)
    args = {k: nc.dram_tensor(k, v.shape, mybir.dt.from_np(v.dtype), kind="ExternalInput").ap() for k, v in arrays.items()}
    out = nc.dram_tensor("out", (N, D), F32, kind="ExternalOutput").ap()
    gat_moe_kernel(nc, **args, out=out)
    r = run_bass_kernel_spmd(nc, [arrays], core_ids=[0])
    return r.results[0]["out"]
```
